# Optimizing a Trainium2 kernel written in Bass

```python
import numpy as np
import jax
import jax.numpy as jnp

def _softmax(x, axis=-1):
    return jax.nn.softmax(x, axis=axis)

def _gelu(x):
    return jax.nn.gelu(x, approximate=True)

def _silu(x):
    return jax.nn.silu(x)

def _sigmoid(x):
    return jax.nn.sigmoid(x)

def _layernorm(x, axis=-1, eps=1e-05):
    m = jnp.mean(x, axis=axis, keepdims=True)
    v = jnp.var(x, axis=axis, keepdims=True)
    return (x - m) / jnp.sqrt(v + eps)

def _scatter_add(tgt, idx, src, axis=0):
    return tgt.at[idx].add(src)

def _segment_sum(src, seg, n):
    return jax.ops.segment_sum(src, seg, n)
kernel_name = 'mk_seq_postln_d2_jaxref_r8_f1b02a'

def setup_inputs(seed: int=0):
    np.random.seed(seed)
    _w = jnp.asarray

    def _L0_attn_setup():
        import jax, jax.numpy as jnp
        import numpy as np
        NUM_HEADS = 16
        EMBED_DIM = 128

        def _linear_attention(x, Wq, bq, Wk, bk, Wv, bv, Wo, bo):
            B, S, D = x.shape
            H = NUM_HEADS
            hd = D // H
            v = (x @ Wv + bv).reshape(B, S, H, hd)
            q = (x @ Wq + bq).reshape(B, S, H, hd)
            k = (x @ Wk + bk).reshape(B, S, H, hd)
            q = jax.nn.elu(q) + 1.0
            k = jax.nn.elu(k) + 1.0
            qT = q.transpose(1, 0, 2, 3)
            kT = k.transpose(1, 0, 2, 3)
            vT = v.transpose(1, 0, 2, 3)
            s0 = jnp.zeros((B, H, hd, hd), dtype=x.dtype)
            z0 = jnp.zeros((B, H, hd), dtype=x.dtype)

            def step(carry, qkv):
                s, z = carry
                q_i, k_i, v_i = qkv
                s = s + jnp.einsum('bhd,bhm->bhdm', k_i, v_i)
                z = z + k_i
                qs = jnp.einsum('bhd,bhdm->bhm', q_i, s)
                qz = jnp.einsum('bhd,bhd->bh', q_i, z)[..., None]
                return ((s, z), qs / (qz + 1e-06))
            (_, _), values = jax.lax.scan(step, (s0, z0), (qT, kT, vT))
            values = values.transpose(1, 0, 2, 3).reshape(B, S, D)
            return values @ Wo + bo
        key = jax.random.key(seed)
        ks = jax.random.split(key, 6)
        B, S, D = (4, 256, EMBED_DIM)
        sc = 1.0 / np.sqrt(D)
        return {'x': jax.random.normal(ks[0], (B, S, D), dtype=jnp.float32), 'mask': jnp.ones((B, S), dtype=jnp.int32), 'Wq': jax.random.normal(ks[1], (D, D), dtype=jnp.float32) * sc, 'bq': jnp.zeros((D,), dtype=jnp.float32), 'Wk': jax.random.normal(ks[2], (D, D), dtype=jnp.float32) * sc, 'bk': jnp.zeros((D,), dtype=jnp.float32), 'Wv': jax.random.normal(ks[3], (D, D), dtype=jnp.float32) * sc, 'bv': jnp.zeros((D,), dtype=jnp.float32), 'Wo': jax.random.normal(ks[4], (D, D), dtype=jnp.float32) * sc, 'bo': jnp.zeros((D,), dtype=jnp.float32)}
    _L0_attn_in = _L0_attn_setup()

    def _L0_ffn_setup():
        import jax, jax.numpy as jnp
        import numpy as np
        B, T, DIM = (4, 128, 128)
        H, E, DH, K = (8, 5, 64, 3)

        def _topk_mask(s, k):
            idx = jax.lax.top_k(s, k)[1]
            return jnp.sum(jax.nn.one_hot(idx, s.shape[-1], dtype=s.dtype), axis=-2)
        key = jax.random.key(seed)
        ks = jax.random.split(key, 6)
        w = lambda k, shape: jax.random.normal(k, shape, jnp.float32) * 0.02
        return {'x': jax.random.normal(ks[0], (B, T, DIM), jnp.float32), 'Wq': w(ks[1], (DIM, H * E * DH)), 'Wkv': w(ks[2], (DIM, 2 * H * E * DH)), 'Ws': w(ks[3], (DIM, H * E)), 'Wd': w(ks[4], (DIM, H * E)), 'Wo': w(ks[5], (DH, E * DIM))}
    _L0_ffn_in = _L0_ffn_setup()

    def _L1_attn_setup():
        import jax, jax.numpy as jnp
        import numpy as np
        import math
        D_MODEL = 128
        N_HEADS = 16
        HEAD_DIM = D_MODEL // N_HEADS

        def rotary_embedding(dim, seq_len):
            inv_freq = 1.0 / 10000.0 ** (jnp.arange(0, dim, 2, dtype=jnp.float32) / dim)
            t = jnp.arange(seq_len, dtype=jnp.float32)
            freqs = t[:, None] * inv_freq[None, :]
            return jnp.concatenate((freqs, freqs), axis=-1)

        def apply_rope(x, rope):
            x1 = x[..., ::2]
            x2 = x[..., 1::2]
            ang = rope[..., ::2]
            c, s = (jnp.cos(ang), jnp.sin(ang))
            o1 = x1 * c - x2 * s
            o2 = x1 * s + x2 * c
            return jnp.stack((o1, o2), axis=-1).reshape(x.shape)
        key = jax.random.key(seed)
        ks = jax.random.split(key, 9)
        d = D_MODEL
        sc = 1.0 / math.sqrt(d)
        return {'x': jax.random.normal(ks[0], (2, 256, d), dtype=jnp.float32), 'Wq': jax.random.normal(ks[1], (d, d), dtype=jnp.float32) * sc, 'bq': jax.random.normal(ks[2], (d,), dtype=jnp.float32) * 0.02, 'Wk': jax.random.normal(ks[3], (d, d), dtype=jnp.float32) * sc, 'bk': jax.random.normal(ks[4], (d,), dtype=jnp.float32) * 0.02, 'Wv': jax.random.normal(ks[5], (d, d), dtype=jnp.float32) * sc, 'bv': jax.random.normal(ks[6], (d,), dtype=jnp.float32) * 0.02, 'Wo': jax.random.normal(ks[7], (d, d), dtype=jnp.float32) * sc, 'bo': jax.random.normal(ks[8], (d,), dtype=jnp.float32) * 0.02}
    _L1_attn_in = _L1_attn_setup()

    def _L1_ffn_setup():
        import jax, jax.numpy as jnp
        import numpy as np
        CAPACITY = 0.5
        key = jax.random.key(seed)
        ks = jax.random.split(key, 7)
        b, s, d, h = (4, 1024, 128, 512)
        sc_r = 1.0 / np.sqrt(d)
        sc_1 = 1.0 / np.sqrt(d)
        sc_2 = 1.0 / np.sqrt(h)
        return {'x': jax.random.normal(ks[0], (b, s, d), dtype=jnp.float32), 'w_r': jax.random.uniform(ks[1], (d, 1), jnp.float32, -sc_r, sc_r), 'b_r': jax.random.uniform(ks[2], (1,), jnp.float32, -sc_r, sc_r), 'W1': jax.random.uniform(ks[3], (d, h), jnp.float32, -sc_1, sc_1), 'b1': jax.random.uniform(ks[4], (h,), jnp.float32, -sc_1, sc_1), 'W2': jax.random.uniform(ks[5], (h, d), jnp.float32, -sc_2, sc_2), 'b2': jax.random.uniform(ks[6], (d,), jnp.float32, -sc_2, sc_2)}
    _L1_ffn_in = _L1_ffn_setup()
    _d = {'L0_attn_x': _L0_attn_in['x'], 'L0_attn_mask': _L0_attn_in['mask'], 'L0_attn_Wq': _L0_attn_in['Wq'], 'L0_attn_bq': _L0_attn_in['bq'], 'L0_attn_Wk': _L0_attn_in['Wk'], 'L0_attn_bk': _L0_attn_in['bk'], 'L0_attn_Wv': _L0_attn_in['Wv'], 'L0_attn_bv': _L0_attn_in['bv'], 'L0_attn_Wo': _L0_attn_in['Wo'], 'L0_attn_bo': _L0_attn_in['bo'], 'L0_ffn_Wq': _L0_ffn_in['Wq'], 'L0_ffn_Wkv': _L0_ffn_in['Wkv'], 'L0_ffn_Ws': _L0_ffn_in['Ws'], 'L0_ffn_Wd': _L0_ffn_in['Wd'], 'L0_ffn_Wo': _L0_ffn_in['Wo'], 'L1_attn_Wq': _L1_attn_in['Wq'], 'L1_attn_bq': _L1_attn_in['bq'], 'L1_attn_Wk': _L1_attn_in['Wk'], 'L1_attn_bk': _L1_attn_in['bk'], 'L1_attn_Wv': _L1_attn_in['Wv'], 'L1_attn_bv': _L1_attn_in['bv'], 'L1_attn_Wo': _L1_attn_in['Wo'], 'L1_attn_bo': _L1_attn_in['bo'], 'L1_ffn_w_r': _L1_ffn_in['w_r'], 'L1_ffn_b_r': _L1_ffn_in['b_r'], 'L1_ffn_W1': _L1_ffn_in['W1'], 'L1_ffn_b1': _L1_ffn_in['b1'], 'L1_ffn_W2': _L1_ffn_in['W2'], 'L1_ffn_b2': _L1_ffn_in['b2']}
    _x0 = _d['L0_attn_x']
    _d['L0_attn_x'] = jax.random.normal(jax.random.fold_in(jax.random.key(seed), 1), (4, 1024, 128), dtype=_x0.dtype)
    del _x0
    return _d

def reference(L0_attn_x, L0_attn_mask, L0_attn_Wq, L0_attn_bq, L0_attn_Wk, L0_attn_bk, L0_attn_Wv, L0_attn_bv, L0_attn_Wo, L0_attn_bo, L0_ffn_Wq, L0_ffn_Wkv, L0_ffn_Ws, L0_ffn_Wd, L0_ffn_Wo, L1_attn_Wq, L1_attn_bq, L1_attn_Wk, L1_attn_bk, L1_attn_Wv, L1_attn_bv, L1_attn_Wo, L1_attn_bo, L1_ffn_w_r, L1_ffn_b_r, L1_ffn_W1, L1_ffn_b1, L1_ffn_W2, L1_ffn_b2):

    def _L0_attn_ref(x, mask, Wq, bq, Wk, bk, Wv, bv, Wo, bo):
        import jax, jax.numpy as jnp
        import numpy as np
        NUM_HEADS = 16
        EMBED_DIM = 128

        def _linear_attention(x, Wq, bq, Wk, bk, Wv, bv, Wo, bo):
            B, S, D = x.shape
            H = NUM_HEADS
            hd = D // H
            v = (x @ Wv + bv).reshape(B, S, H, hd)
            q = (x @ Wq + bq).reshape(B, S, H, hd)
            k = (x @ Wk + bk).reshape(B, S, H, hd)
            q = jax.nn.elu(q) + 1.0
            k = jax.nn.elu(k) + 1.0
            qT = q.transpose(1, 0, 2, 3)
            kT = k.transpose(1, 0, 2, 3)
            vT = v.transpose(1, 0, 2, 3)
            s0 = jnp.zeros((B, H, hd, hd), dtype=x.dtype)
            z0 = jnp.zeros((B, H, hd), dtype=x.dtype)

            def step(carry, qkv):
                s, z = carry
                q_i, k_i, v_i = qkv
                s = s + jnp.einsum('bhd,bhm->bhdm', k_i, v_i)
                z = z + k_i
                qs = jnp.einsum('bhd,bhdm->bhm', q_i, s)
                qz = jnp.einsum('bhd,bhd->bh', q_i, z)[..., None]
                return ((s, z), qs / (qz + 1e-06))
            (_, _), values = jax.lax.scan(step, (s0, z0), (qT, kT, vT))
            values = values.transpose(1, 0, 2, 3).reshape(B, S, D)
            return values @ Wo + bo
        return _linear_attention(x, Wq, bq, Wk, bk, Wv, bv, Wo, bo)

    def _L0_ffn_ref(x, Wq, Wkv, Ws, Wd, Wo):
        import jax, jax.numpy as jnp
        import numpy as np
        B, T, DIM = (4, 128, 128)
        H, E, DH, K = (8, 5, 64, 3)

        def _topk_mask(s, k):
            idx = jax.lax.top_k(s, k)[1]
            return jnp.sum(jax.nn.one_hot(idx, s.shape[-1], dtype=s.dtype), axis=-2)
        b, t, _ = x.shape
        scale = DH ** (-0.5)
        ss = jax.nn.sigmoid(x @ Ws).reshape(b, t, H, E)
        sd = jax.nn.sigmoid(x @ Wd).reshape(b, t, H, E)
        ms = _topk_mask(ss, K)
        md = _topk_mask(sd, K)
        ss_g = ss * ms
        sd_g = sd * md
        q5 = (x @ Wq).reshape(b, t, H, E, DH)
        kv = (x @ Wkv).reshape(b, t, 2, H, E, DH)
        k5, v5 = (kv[:, :, 0], kv[:, :, 1])
        q = jnp.einsum('bthed,bthe->bhtd', q5, sd_g)
        k = jnp.einsum('bthed,bthe->bhtd', k5, ss_g)
        v = jnp.einsum('bthed,bthe->bhtd', v5, ss_g)
        attn = jax.nn.softmax(jnp.einsum('bhid,bhjd->bhij', q * scale, k), axis=-1)
        out = jnp.einsum('bhij,bhjd->bihd', attn, v)
        o5 = jnp.einsum('bthd,dm->bthm', out, Wo).reshape(b, t, H, E, DIM)
        return jnp.einsum('bthem,bthe->btm', o5, md)

    def _L1_attn_ref(x, Wq, bq, Wk, bk, Wv, bv, Wo, bo):
        import jax, jax.numpy as jnp
        import numpy as np
        import math
        D_MODEL = 128
        N_HEADS = 16
        HEAD_DIM = D_MODEL // N_HEADS

        def rotary_embedding(dim, seq_len):
            inv_freq = 1.0 / 10000.0 ** (jnp.arange(0, dim, 2, dtype=jnp.float32) / dim)
            t = jnp.arange(seq_len, dtype=jnp.float32)
            freqs = t[:, None] * inv_freq[None, :]
            return jnp.concatenate((freqs, freqs), axis=-1)

        def apply_rope(x, rope):
            x1 = x[..., ::2]
            x2 = x[..., 1::2]
            ang = rope[..., ::2]
            c, s = (jnp.cos(ang), jnp.sin(ang))
            o1 = x1 * c - x2 * s
            o2 = x1 * s + x2 * c
            return jnp.stack((o1, o2), axis=-1).reshape(x.shape)
        B, S, d = x.shape
        H, Dh = (N_HEADS, HEAD_DIM)
        q = (x @ Wq + bq).reshape(B, S, H, Dh).transpose(0, 2, 1, 3)
        k = (x @ Wk + bk).reshape(B, S, H, Dh).transpose(0, 2, 1, 3)
        v = (x @ Wv + bv).reshape(B, S, H, Dh).transpose(0, 2, 1, 3)
        rope = rotary_embedding(Dh, S)
        q = apply_rope(q, rope)
        k = apply_rope(k, rope)
        scores = jnp.einsum('bhqd,bhkd->bhqk', q, k) / math.sqrt(Dh)
        attn = jax.nn.softmax(scores, axis=-1)
        out = jnp.einsum('bhqk,bhkd->bhqd', attn, v)
        out = out.transpose(0, 2, 1, 3).reshape(B, S, d)
        return out @ Wo + bo

    def _L1_ffn_ref(x, w_r, b_r, W1, b1, W2, b2):
        import jax, jax.numpy as jnp
        import numpy as np
        CAPACITY = 0.5
        b, s, d = x.shape
        k = int(CAPACITY * s)
        weights = (jnp.einsum('bsd,do->bso', x, w_r) + b_r).squeeze(-1)
        top_vals, _ = jax.lax.top_k(weights, k)
        threshold = top_vals[:, -1]
        selected = weights > threshold[:, None]
        hidden = jax.nn.gelu(jnp.einsum('bsd,dh->bsh', x, W1) + b1, approximate=False)
        blk = jnp.einsum('bsh,hd->bsd', hidden, W2) + b2
        m = selected[..., None]
        return jnp.where(m, blk, x)
    x = L0_attn_x
    x = _layernorm(x + _L0_attn_ref(x, L0_attn_mask, L0_attn_Wq, L0_attn_bq, L0_attn_Wk, L0_attn_bk, L0_attn_Wv, L0_attn_bv, L0_attn_Wo, L0_attn_bo), axis=-1)
    x = _layernorm(x + _L0_ffn_ref(x, L0_ffn_Wq, L0_ffn_Wkv, L0_ffn_Ws, L0_ffn_Wd, L0_ffn_Wo), axis=-1)
    x = _layernorm(x + _L1_attn_ref(x, L1_attn_Wq, L1_attn_bq, L1_attn_Wk, L1_attn_bk, L1_attn_Wv, L1_attn_bv, L1_attn_Wo, L1_attn_bo), axis=-1)
    x = _layernorm(x + _L1_ffn_ref(x, L1_ffn_w_r, L1_ffn_b_r, L1_ffn_W1, L1_ffn_b1, L1_ffn_W2, L1_ffn_b2), axis=-1)
    return x

_drawn_inputs = setup_inputs


def setup_inputs(seed=0):
    import zlib

    import numpy as np

    out = dict(_drawn_inputs(seed))
    spreads = {'L0_attn_bq': (0.0, 2.0),
     'L0_attn_bk': (0.0, 2.0),
     'L0_attn_bv': (0.0, 0.1),
     'L0_attn_bo': (0.0, 0.1)}
    factors = {'L0_attn_Wq': 2.916,
     'L0_ffn_Wq': 39.509,
     'L0_ffn_Ws': 11.964,
     'L0_ffn_Wd': 9.933,
     'L1_attn_bq': 29.261,
     'L1_attn_bk': 24.505,
     'L1_attn_bo': 2.744,
     'L1_ffn_b1': 4.469,
     'L1_ffn_b2': 3.119}
    for name, (base, spread) in spreads.items():
        noise = np.random.default_rng([zlib.crc32(name.encode()), seed]).standard_normal(out[name].shape)
        drawn = base * np.exp(spread * noise) if base else spread * noise
        out[name] = jnp.asarray(drawn.astype(out[name].dtype))
    for name, factor in factors.items():
        out[name] = (out[name] * factor).astype(out[name].dtype)
    return out
```

```python
import concourse.bass as bass
from concourse import mybir
from contextlib import ExitStack, nullcontext

F32 = mybir.dt.float32
F32R = mybir.dt.float32r
I32 = mybir.dt.int32
ALU = mybir.AluOpType
ACT = mybir.ActivationFunctionType
AX = mybir.AxisListType

P = 128
B, T, D = 4, 1024, 128
NT = T // P
HALF = 512
LN_EPS = 1e-5
H = 16
HD = D // H


ONE = 1


class Steps:

    def __init__(self, eng, sem, base=0):
        self.eng, self.sem, self.base, self.n = eng, sem, base, 0

    def done(self, ins):
        ins.then_inc(self.sem, 1)
        self.n += 1
        return ins

    def settle(self):
        self.eng.wait_ge(self.sem, self.base + self.n)

    def settle_apart(self):
        self.settle()
        self.eng.sem_inc(self.sem, 1)
        self.n += 1

    def link(self, ins):
        self.done(ins)
        self.settle()


def layer_norm(nc, st, y, out, stats, mv, rs, tmp):
    st.settle()
    for t in range(NT):
        st.done(nc.vector.bn_stats(stats[:, t, :], y[:, t, :]))
    st.settle_apart()
    for t in range(NT):
        st.done(nc.vector.bn_aggr(mv[:, t, :], stats[:, t, :]))
    st.settle()
    var = tmp[:, 0, :]
    half_step = tmp[:, 1, :]
    st.link(nc.vector.tensor_scalar(var, mv[:, :, 1], LN_EPS, None, ALU.add))
    st.link(nc.vector.tensor_scalar(rs[:, :].bitcast(I32), var.bitcast(I32), -0.5, float(0x5F3759DF),
                                    ALU.mult, ALU.add))
    for _ in range(3):
        st.link(nc.vector.tensor_tensor(half_step, rs[:, :], rs[:, :], ALU.mult))
        st.link(nc.vector.scalar_tensor_tensor(half_step, half_step, -0.5, var, ALU.mult, ALU.mult))
        st.link(nc.vector.scalar_tensor_tensor(rs[:, :], half_step, 1.5, rs[:, :], ALU.add, ALU.mult))
    for t in range(NT):
        st.done(nc.vector.tensor_scalar(out[:, t, :], y[:, t, :], mv[:, t, 0:1], rs[:, t:t + 1],
                                        ALU.subtract, ALU.mult))


LN_STEPS = 3 * NT + 3 + 9


def semaphores(nc, ctx, tag):
    sems = []

    def sem(name):
        sems.append(ctx.enter_context(nc.semaphore(tag + name)))
        return sems[-1]

    return sems, sem


def clear_semaphores(nc, sems):
    with nc.Block() as block:
        @block.gpsimd
        def _(pool):
            for sem in sems:
                pool.sem_clear(sem)


SAFE_LOW, SAFE_HIGH = 1e-18, 1e18


def only_if(eng, flag):
    return nullcontext() if flag is None else eng.If(eng.value_load(flag[0:1, 0:1], min_val=0, max_val=1))


def count_safe(nc, dve, judged, recips, ok, good):
    nc.vector.tensor_scalar(ok[:, :], recips[:, :], SAFE_LOW, None, ALU.is_ge).then_inc(judged, 1)
    dve.wait_ge(judged, 1)
    nc.vector.scalar_tensor_tensor(ok[:, :], recips[:, :], SAFE_HIGH, ok[:, :], ALU.is_le, ALU.mult).then_inc(judged, 1)
    dve.wait_ge(judged, 2)
    nc.vector.reduce_sum(good[:, 0:1], ok[:, :], AX.X).then_inc(judged, 1)


def turn_counts(nc, pe, judged, good, ident, row):
    pe.wait_ge(judged, 3)
    nc.tensor.matmul(row, good[:, 0:1], ident[:, :], start=True, stop=True).then_inc(judged, 1)


def raise_flag(nc, dve, judged, row, total, count, flag):
    dve.wait_ge(judged, 4)
    nc.vector.reduce_sum(total[0:1, 0:1], row, AX.X).then_inc(judged, 1)
    dve.wait_ge(judged, 5)
    nc.vector.tensor_scalar(flag[0:1, 0:1], total[0:1, 0:1], float(count), None, ALU.is_lt).then_inc(judged, 1)
    dve.wait_ge(judged, 6)


def linear_attention(nc, x_dram, out, ps, ident, I):
    ctx = ExitStack()
    with ctx:
        sb = lambda name, shape, dt=F32: ctx.enter_context(nc.sbuf_tensor(name, shape, dt))
        sems, sem = semaphores(nc, ctx, "a_")
        wq, wk, wv, wo = (sb(f"a_{n}", [P, D]) for n in ("wq", "wk", "wv", "wo"))
        wv_rep = sb("a_wv_rep", [P, HD, H, HD])
        bq, bk = sb("a_bq", [P, 1]), sb("a_bk", [P, 1])
        rows = sb("a_rows", [1, 2, D])
        bv_rep = sb("a_bv_rep", [1, HD, H, HD])
        bv_col = sb("a_bv_col", [P, HD])
        bo_all = sb("a_bo_all", [P, D])
        sel = sb("a_sel", [P, HD + 1, P])
        ones = sb("a_ones", [P, T])
        xs, xT = sb("a_xs", [P, NT, D]), sb("a_xT", [P, T])
        low, relu, expo = (sb(f"a_{n}", [P, 2, T]) for n in ("low", "relu", "expo"))
        q, k = sb("a_q", [P, T]), sb("a_k", [P, T])
        kv, scan, qscan = sb("a_kv", [P, T]), sb("a_scan", [P, 2, T]), sb("a_qscan", [P, 2, T])
        rden, vals = sb("a_rden", [P, T]), sb("a_vals", [P, T])
        xb, y = sb("a_xb", [P, NT, D]), sb("a_y", [P, NT, D])
        stats, mv, rs, tmp = sb("a_stats", [P, NT, 6]), sb("a_mv", [P, NT, 2]), sb("a_rs", [P, NT]), sb("a_tmp", [P, 2, NT])

        x_in, w_in, ones_rdy, reps, bias_ps, bias_sb = map(sem, ("x_in", "w_in", "ones", "reps", "bias_ps", "bias_sb"))
        xT_ps, xT_sb, qk_ps, low_rdy, exp_rdy, q_rdy = map(sem, ("xT_ps", "xT_sb", "qk_ps", "low", "exp", "q"))
        v_ps, kv_rdy, scan_rdy, qs_rdy, acc_ps = map(sem, ("v_ps", "kv", "scan", "qs", "acc_ps"))
        den_read, vals_rdy, o_ps, xb_rdy, y_rdy, steps = map(sem, ("den_read", "vals", "o_ps", "xb", "y", "steps"))
        NJ = HD + 1
        bank2 = lambda i: ps[:, i:i + 2, :].rearrange("p a n -> p (a n)")
        tr_ps, q_ps, k_ps = bank2(0), bank2(2), bank2(4)
        vb_ps = [bank2(6), bank2(0)]
        num_ps, den_ps, o2_ps = q_ps, k_ps, bank2(0)
        V_STEPS = 2 + 2 + LN_STEPS
        W_IN = 16 * 10

        ctx.callback(clear_semaphores, nc, sems)
        block = ctx.enter_context(nc.Block())

        @block.sync
        def _(sp):
            sp.dma_start(ident[:, :], I["ident"]).then_inc(w_in, 16)
            for dst, src in ((wq, "L0_attn_Wq"), (wk, "L0_attn_Wk"), (wv, "L0_attn_Wv"), (wo, "L0_attn_Wo")):
                sp.dma_start(dst[:, :], I[src]).then_inc(w_in, 16)
            for dst, src in ((bq, "L0_attn_bq"), (bk, "L0_attn_bk")):
                sp.dma_start(dst[:, :], I[src].rearrange("(p o) -> p o", o=1)).then_inc(w_in, 16)
            for j, src in enumerate(("L0_attn_bv", "L0_attn_bo")):
                sp.dma_start(rows[:, j, :], I[src].rearrange("(o n) -> o n", o=1)).then_inc(w_in, 16)
            sp.dma_start(sel[:, :, :], I["sel"]).then_inc(w_in, 16)
            with sp.Fori(0, B) as b:
                sp.wait_ge(y_rdy, ONE + b)
                sp.dma_start(xs[:, :, :], x_dram[b].rearrange("(t p) c -> p t c", p=P)).then_inc(x_in, 16)

        @block.gpsimd
        def _(pool):
            nc.gpsimd.memset(ones[:, :], 1.0).then_inc(ones_rdy, 1)
            pool.wait_ge(w_in, W_IN)
            for m in range(HD):
                nc.gpsimd.tensor_copy(wv_rep[:, m, :, :],
                                      wv[:, :].rearrange("p (h m) -> p m h", h=H)[:, m, :].unsqueeze(2).broadcast_to([P, H, HD])).then_inc(reps, 1)
                nc.gpsimd.tensor_copy(bv_rep[:, m, :, :],
                                      rows[:, 0, :].rearrange("p (h m) -> p m h", h=H)[:, m, :].unsqueeze(2).broadcast_to([1, H, HD])).then_inc(reps, 1)
            pool.wait_ge(bias_sb, 2)
            with pool.Fori(0, B) as b:
                pool.wait_ge(x_in, 16 * b + 16)
                pool.wait_ge(y_rdy, ONE + b)
                nc.gpsimd.tensor_tensor(xb[:, :, :], xs[:, :, :],
                                        bo_all[:, :].unsqueeze(1).broadcast_to([P, NT, D]), ALU.add).then_inc(xb_rdy, 1)
                for j in range(NJ):
                    pool.wait_ge(scan_rdy, b * NJ + j + 1)
                    if j >= 2:
                        pool.wait_ge(acc_ps, b * NJ + j - 1)
                    nc.gpsimd.tensor_tensor(qscan[:, j % 2, :], scan[:, j % 2, :], q[:, :], ALU.mult).then_inc(qs_rdy, 1)

        @block.scalar
        def _(act):
            nc.scalar.preload_act_table(ACT.Exp)
            with act.Fori(0, B) as b:
                act.wait_ge(xT_ps, b + 1)
                nc.scalar.copy(xT[:, :], tr_ps).then_inc(xT_sb, 1)
                for j in range(2):
                    act.wait_ge(low_rdy, 2 * b + j + 1)
                    nc.scalar.activation(expo[:, j, :], low[:, j, :], ACT.Exp).then_inc(exp_rdy, 1)

        @block.tensor
        def _(pe):
            pe.wait_ge(w_in, W_IN)
            pe.wait_ge(ones_rdy, 1)
            pe.wait_ge(reps, 2 * HD)
            for m in range(HD):
                last = nc.tensor.matmul(ps[:, 0, m:m + 1], bv_rep[:, m, :, :].rearrange("p h d -> p (h d)"), ones[0:1, 0:1], start=True, stop=True)
            last.then_inc(bias_ps, 1)
            nc.tensor.matmul(ps[:, 1, 0:D], ones[0:1, 0:P], rows[:, 1, :], start=True, stop=True).then_inc(bias_ps, 1)
            pe.wait_ge(bias_sb, 2)
            with pe.Fori(0, B) as b:
                pe.wait_ge(x_in, 16 * b + 16)
                pe.wait_ge(y_rdy, ONE + b)
                for t in range(NT):
                    last = nc.tensor.transpose(tr_ps[:, t * P:(t + 1) * P], xs[:, t, :], ident[:, :])
                last.then_inc(xT_ps, 1)
                pe.wait_ge(xT_sb, b + 1)
                for w, dst in ((wq, q_ps), (wk, k_ps)):
                    for s in range(0, T, HALF):
                        last = nc.tensor.matmul(dst[:, s:s + HALF], w[:, :], xT[:, s:s + HALF], start=True, stop=True)
                    last.then_inc(qk_ps, 1)

                def value_column(m):
                    if m >= 2:
                        pe.wait_ge(kv_rdy, b * HD + m - 1)
                    for s in range(0, T, HALF):
                        last = nc.tensor.matmul(vb_ps[m % 2][:, s:s + HALF], wv_rep[:, m, :, :].rearrange("p h d -> p (h d)"), xT[:, s:s + HALF], start=True, stop=True)
                    last.then_inc(v_ps, 1)

                value_column(0)
                value_column(1)
                pe.wait_ge(q_rdy, 2 * b + 2)
                for j in range(NJ):
                    pe.wait_ge(qs_rdy, b * NJ + j + 1)
                    dst, pick = (den_ps, HD) if j == 0 else (num_ps, j - 1)
                    for s in range(0, T, HALF):
                        last = nc.tensor.matmul(dst[:, s:s + HALF], sel[:, pick, :], qscan[:, j % 2, s:s + HALF], start=(j <= 1), stop=(j in (0, HD)))
                    last.then_inc(acc_ps, 1)
                    if j + 2 < HD:
                        value_column(j + 2)
                pe.wait_ge(vals_rdy, b + 1)
                for t in range(NT):
                    last = nc.tensor.matmul(o2_ps[:, t * P:(t + 1) * P], vals[:, t * P:(t + 1) * P], wo[:, :], start=True, stop=True)
                last.then_inc(o_ps, 1)

        @block.vector
        def _(dve):
            dve.sem_inc(y_rdy, ONE)
            dve.wait_ge(bias_ps, 1)
            nc.vector.tensor_copy(bv_col[:, :], ps[:, 0, 0:HD]).then_inc(bias_sb, 1)
            dve.wait_ge(bias_ps, 2)
            nc.vector.tensor_copy(bo_all[:, :], ps[:, 1, 0:D]).then_inc(bias_sb, 1)
            dve.wait_ge(bias_sb, 2)
            with dve.Fori(0, B) as b:
                st = Steps(dve, steps, b * V_STEPS)
                for j, (src, bias) in enumerate(((q_ps, bq), (k_ps, bk))):
                    dve.wait_ge(qk_ps, 2 * b + j + 1)
                    nc.vector.tensor_scalar(low[:, j, :], src, bias[:, 0:1], 0.0, ALU.add, ALU.min).then_inc(low_rdy, 1)
                    st.done(nc.vector.tensor_scalar(relu[:, j, :], src, bias[:, 0:1], 0.0, ALU.add, ALU.max))
                st.settle()
                for j, dst in enumerate((q, k)):
                    dve.wait_ge(exp_rdy, 2 * b + j + 1)
                    nc.vector.tensor_tensor(dst[:, :], relu[:, j, :], expo[:, j, :], ALU.add).then_inc(q_rdy, 1)
                dve.wait_ge(q_rdy, 2 * b + 2)
                for j in range(NJ):
                    if j >= 1:
                        dve.wait_ge(v_ps, b * HD + j)
                        nc.vector.scalar_tensor_tensor(kv[:, :], vb_ps[(j - 1) % 2], bv_col[:, j - 1:j], k[:, :], ALU.add, ALU.mult).then_inc(kv_rdy, 1)
                        dve.wait_ge(kv_rdy, b * HD + j)
                    if j >= 2:
                        dve.wait_ge(qs_rdy, b * NJ + j - 1)
                    nc.vector.tensor_tensor_scan(scan[:, j % 2, :], ones[:, :], (k if j == 0 else kv)[:, :], 0.0, ALU.mult, ALU.add).then_inc(scan_rdy, 1)
                    if j >= 1:
                        dve.wait_ge(scan_rdy, b * NJ + j + 1)
                    if j == 3:
                        dve.wait_ge(acc_ps, b * NJ + 1)
                        st.link(nc.vector.tensor_scalar(rden[:, :], den_ps, 1e-6, None, ALU.add))
                        st.link(nc.vector.reciprocal(rden[:, :], rden[:, :]))
                dve.wait_ge(acc_ps, b * NJ + NJ)
                nc.vector.tensor_tensor(vals[:, :], num_ps, rden[:, :], ALU.mult).then_inc(vals_rdy, 1)
                dve.wait_ge(o_ps, b + 1)
                dve.wait_ge(xb_rdy, b + 1)
                nc.vector.tensor_tensor(y[:, :, :].rearrange("p t c -> p (t c)"), o2_ps, xb[:, :, :].rearrange("p t c -> p (t c)"), ALU.add).then_inc(y_rdy, 1)
                dve.wait_ge(y_rdy, ONE + b + 1)
                layer_norm(nc, st, y, out[:, bass.ds(b * NT, NT), :], stats, mv, rs, tmp)
                st.settle()
                assert st.n == V_STEPS, st.n



def switch_attention(nc, x, out, ps, ident, I, redo, flag, tag):
    NH, E, DH, TOP = 8, 5, 64, 3
    ED = E * DH
    U = 3 * NT
    NG = 2 * NH
    HALVES = ((0, HALF), (HALF, T))
    with_max = redo is not None
    ctx = ExitStack()
    with ctx:
        sb = lambda name, shape, dt=F32: ctx.enter_context(nc.sbuf_tensor(tag + name, shape, dt))
        sems, sem = semaphores(nc, ctx, tag)
        w = sb("w", [P, 2, 2, 3, ED], F32R)
        wg = sb("wg", [P, NG * E])
        wo = sb("wo", [P, 3, D])
        ones = sb("ones", [P, P])
        xs, xT = sb("xs", [P, NT, D]), sb("xT", [P, T])
        xh, xl = sb("xh", [P, T], F32R), sb("xl", [P, T], F32R)
        gate = sb("gate", [P, NT, NG * E])
        beats = sb("beats", [P, NT * NG, E, E])
        mask = sb("mask", [P, NT * NG, E])
        picked = sb("picked", [P, B, NT, NH * E])
        gated = sb("gated", [P, 2, 3, ED])
        tok = sb("tok", [P, 2, NT, 3, DH])
        kk = sb("kk", [P, 2, T], F32R)
        qh, ql = sb("qh", [P, 2, T], F32R), sb("ql", [P, 2, T], F32R)
        vals = sb("vals", [P, 2, NT, DH])
        probs = sb("probs", [P, 4, T])
        psum = sb("psum", [P, 2, T])
        acc, sums = sb("acc", [P, HALF]), sb("sums", [P, 2 * P])
        o = sb("o", [P, NT, DH])
        share, z = sb("share", [P, NT, E, DH]), sb("z", [P, NT, E, DH])
        zT = sb("zT", [P, 3, P])
        y = sb("y", [P, NT, D])
        stats, mv, rs, tmp = sb("stats", [P, NT, 6]), sb("mv", [P, NT, 2]), sb("rs", [P, NT]), sb("tmp", [P, 2, NT])
        w_dram = nc.dram_tensor(tag + "w_split", [NH, P, 2 * 3 * ED], F32).ap()
        recips, ok, good, total = sb("recips", [P, B * NH * NT]), sb("ok", [P, B * NH * NT]), sb("good", [P, 1]), sb("total", [1, 1])
        judged = sem("judged")
        if with_max:
            mx, neg_max = sb("mx", [P, NT]), sb("neg_max", [1, T])
            max_ps, max_rdy, neg_ps, neg_rdy = map(sem, ("max_ps", "max", "neg_ps", "neg"))

        w_in, clear = sem("w_in"), sem("clear")
        raw_in = [sem("raw_in0"), sem("raw_in1")]
        w_high, w_low = sem("w_high"), sem("w_low")
        w_out = [sem("w_out0"), sem("w_out1")]
        w_rdy = [sem("w_rdy0"), sem("w_rdy1")]
        x_in, xT_ps, xT_sb, x_split, gate_ps, gate_exp, gate_rdy = map(sem, ("x_in", "xT_ps", "xT_sb", "x_split", "gate_ps", "gate_exp", "gate_rdy"))
        proj_ps, mult, tok_rdy = map(sem, ("proj_ps", "mult", "tok_rdy"))
        turn_ps, high_rdy, low_rdy, vals_rdy = map(sem, ("turn_ps", "high", "low", "vals_rdy"))
        score_ps, exp_rdy, pv_done, psum_rdy = map(sem, ("score_ps", "exp", "pv", "psum_rdy"))
        acc_sb, sum_ps, sum_sb, sumT_ps, recip_rdy, accT_ps, o_rdy = map(sem, ("acc_sb", "sum_ps", "sum_sb", "sumT_ps", "recip_rdy", "accT_ps", "o_rdy"))
        share_rdy, z_rdy, zT_ps, zT_sb, out_ps, y_rdy, steps = map(sem, ("share_rdy", "z_rdy", "zT_ps", "zT_sb", "out_ps", "y_rdy", "steps"))
        norm_steps = sem("norm_steps")

        proj_b = [ps[:, 0, :], ps[:, 1, :]]
        turn_b, acc_b = ps[:, 2, :], ps[:, 3, :]
        score_b = [ps[:, i:i + 2, :].rearrange("p a n -> p (a n)") for i in (4, 6)]
        MULT0, TOK0, VALS0, EXP0, PV0, PSUM0, SUM0 = 2, 2, 2, 2, 4, NT - 1, 2
        ACC0 = ACCT0 = SUMT0 = O0 = SHARE0 = Z0 = ZT0 = 1
        NORM_STEPS = LN_STEPS + 1
        GATE_STEPS = 2 + 2 * (E - 1) + 2 + 3
        raw_w = [probs[:, 2 * i, 0:3 * ED].rearrange("p (j n) -> p j n", j=3) for i in range(2)]

        def pairs(eng, b, body):
            body(b, 0)
            with eng.Fori(1, NH // 2 - 1) as hp:
                body(b, hp)
            body(b, NH // 2 - 1)

        def batches(eng, body):
            body(0, True, False)
            with eng.Fori(1, B - 1) as b:
                body(b, False, False)
            body(B - 1, False, True)

        def picked_of(b, h):
            return picked[:, bass.ds(b, 1), :, bass.ds(h * E, E)].rearrange("p b t e -> p (b t) e")

        def run_periods(eng, period):
            def batch(b, first, last):
                def pair(b, hp):
                    for par in range(2):
                        at0 = isinstance(hp, int) and hp == 0
                        at3 = isinstance(hp, int) and hp == NH // 2 - 1
                        period(b * NH + hp * 2 + par, b, par,
                               share=(b - 1, NH - 1) if at0 and par == 0 else (b, hp * 2 + par - 1),
                               ahead=par if at3 else hp * 2 + par + 2,
                               start=first and at0 and par == 0,
                               has_next=not (last and at3 and par == 1),
                               projecting=not (last and at3),
                               prep=at3 and par == 0 and not last,
                               project_out=at0 and par == 1 and not first,
                               first_head=at0 and par == 1)
                pairs(eng, b, pair)
            batches(eng, batch)

        ctx.callback(clear_semaphores, nc, sems)
        block = ctx.enter_context(nc.Block())

        @block.sync
        def _(sp):
            with only_if(sp, redo):
                sp.dma_start(xs[:, :, :], x[:, 0:NT, :]).then_inc(x_in, 16)
                sp.dma_start(wg[:, 0:NH * E], I["L0_ffn_Ws"]).then_inc(w_in, 16)
                sp.dma_start(wg[:, NH * E:], I["L0_ffn_Wd"]).then_inc(w_in, 16)
                for e in range(E):
                    at = DH * (e % 2)
                    sp.dma_start(wo[at:at + DH, e // 2, :], I["L0_ffn_Wo"][:, e * D:(e + 1) * D]).then_inc(w_in, 16)
                wq_h = I["L0_ffn_Wq"].rearrange("c (h n) -> h c n", h=NH)
                wkv_h = I["L0_ffn_Wkv"].rearrange("c (j h n) -> h c j n", j=2, h=NH)

                def raw(h):
                    if h >= 2:
                        sp.wait_ge(w_low, h - 1)
                    sp.dma_start(raw_w[h % 2][:, 0, :], wq_h[h]).then_inc(raw_in[h % 2], 16)
                    sp.dma_start(raw_w[h % 2][:, 1:3, :], wkv_h[h]).then_inc(raw_in[h % 2], 16)

                raw(0)
                raw(1)
                for h in range(NH):
                    sp.wait_ge(w_low, h + 1)
                    sp.dma_start(w_dram[h], w[:, h % 2, :, :, :].rearrange("p a j n -> p (a j n)").bitcast(F32)).then_inc(w_out[h % 2], 16)
                    if h + 2 < NH:
                        raw(h + 2)
                for par in range(2):
                    sp.wait_ge(w_out[par], 8 * NH)

                def weights(h, par):
                    sp.dma_start(w[:, par, :, :, :].rearrange("p a j n -> p (a j n)").bitcast(F32), w_dram[h]).then_inc(w_rdy[par], 16)

                weights(0, 0)
                weights(1, 1)

                def batch(b, first, last):
                    def pair(b, hp):
                        for par in range(2):
                            n = b * NH + hp * 2 + par
                            ahead = isinstance(hp, int) and hp == NH // 2 - 1
                            if ahead and last:
                                continue
                            if ahead and par == 0:
                                sp.wait_ge(xT_ps, 2 * (b + 1))
                                sp.dma_start(xs[:, :, :], x[:, bass.ds((b + 1) * NT, NT), :]).then_inc(x_in, 16)
                            sp.wait_ge(proj_ps, U * (n + 1))
                            h2 = par if ahead else hp * 2 + par + 2
                            weights(h2, par) if isinstance(h2, int) else \
                                sp.dma_start(w[:, par, :, :, :].rearrange("p a j n -> p (a j n)").bitcast(F32),
                                             w_dram[bass.ds(h2, 1), :, :].rearrange("h p n -> p (h n)")).then_inc(w_rdy[par], 16)
                    pairs(sp, b, pair)

                batches(sp, batch)

        @block.gpsimd
        def _(pool):
            with only_if(pool, redo):
                pool.sem_inc(psum_rdy, PSUM0)
                pool.sem_inc(share_rdy, SHARE0)
                nc.gpsimd.memset(ones[:, :], 1.0).then_inc(clear, 1)
                nc.gpsimd.memset(beats[:, :, :, :], 0.0).then_inc(clear, 1)

                def add_probs(n, par, i):
                    pool.wait_ge(exp_rdy, EXP0 + NT * n + i + 1)
                    if i == 1:
                        pool.wait_ge(sum_ps, SUM0 + n - 1)
                        prev = probs[:, 0, :]
                    else:
                        pool.wait_ge(psum_rdy, PSUM0 + (NT - 1) * n + i - 1)
                        prev = psum[:, par, :]
                    nc.gpsimd.tensor_tensor(psum[:, par, :], prev, probs[:, i % 4, :], ALU.add).then_inc(psum_rdy, 1)

                def gated_share(n, b, h):
                    pool.wait_ge(o_rdy, O0 + n + 1)
                    pool.wait_ge(z_rdy, Z0 + 2 * n)
                    nc.gpsimd.tensor_tensor(share[:, :, :, :], o[:, :, :].unsqueeze(2).broadcast_to([P, NT, E, DH]),
                                            picked_of(b, h).unsqueeze(3).broadcast_to([P, NT, E, DH]), ALU.mult).then_inc(share_rdy, 1)

                def period(n, b, par, share, ahead, start, has_next, projecting, prep, project_out, first_head):
                    for i in range(1, NT):
                        add_probs(n, par, i)
                        if i == 3 and not start:
                            gated_share(n - 1, *share)

                run_periods(pool, period)
                gated_share(B * NH - 1, B - 1, NH - 1)

        @block.scalar
        def _(act):
            with only_if(act, redo):
                nc.scalar.preload_act_table(ACT.Exp)
                act.sem_inc(exp_rdy, EXP0)
                act.sem_inc(vals_rdy, VALS0)
                act.sem_inc(acc_sb, ACC0)

                def prepare(b):
                    for r, (lo, hi) in enumerate(HALVES):
                        act.wait_ge(xT_ps, 2 * b + r + 1)
                        nc.scalar.copy(xT[:, lo:hi], turn_b).then_inc(xT_sb, 1)
                    for r in range(2):
                        act.wait_ge(gate_ps, 2 * b + r + 1)
                        act.wait_ge(tok_rdy, TOK0 + NT * NH * b)
                        nc.scalar.activation(gate[:, 4 * r:4 * r + 4, :], turn_b[:, 0:4 * NG * E].rearrange("p (t c) -> p t c", t=4), ACT.Exp, scale=-1.0).then_inc(gate_exp, 1)

                def high_part(n, par, r):
                    act.wait_ge(turn_ps, 4 * n + r + 1)
                    lo, hi = HALVES[r % 2]
                    nc.scalar.copy((kk if r < 2 else qh)[:, par, lo:hi], turn_b).then_inc(high_rdy, 1)

                def copy_values(n, par):
                    act.wait_ge(tok_rdy, TOK0 + NT * (n + 1))
                    nc.scalar.copy(vals[:, par, :, :], tok[:, par, :, 2, :]).then_inc(vals_rdy, 1)

                def copy_acc(n):
                    act.wait_ge(pv_done, PV0 + NT * (n + 1))
                    act.wait_ge(accT_ps, ACCT0 + n)
                    nc.scalar.copy(acc[:, :], acc_b).then_inc(acc_sb, 1)

                def copy_sums(n):
                    act.wait_ge(sum_ps, SUM0 + n + 1)
                    act.wait_ge(sumT_ps, SUMT0 + n)
                    nc.scalar.copy(sums[:, :], turn_b[:, 0:2 * P]).then_inc(sum_sb, 1)

                def copy_zT(b, t):
                    act.wait_ge(zT_ps, ZT0 + NT * b + t + 1)
                    nc.scalar.copy(zT[:, 0:2, :], proj_b[0][:, 0:2 * P].rearrange("p (k c) -> p k c", k=2)).then_inc(zT_sb, 1)
                    nc.scalar.copy(zT[0:DH, 2, :], proj_b[0][0:DH, 2 * P:3 * P]).then_inc(zT_sb, 1)

                def period(n, b, par, share, ahead, start, has_next, projecting, prep, project_out, first_head):
                    for i in range(NT):
                        if project_out and not with_max:
                            copy_zT(b - 1, i)
                        if i == 0 and prep:
                            prepare(b + 1)
                        if i == 1 and not start:
                            copy_sums(n - 1)
                        if 3 <= i < 7 and has_next:
                            high_part(n + 1, 1 - par, i - 3)
                        act.wait_ge(score_ps, NT * n + i + 1)
                        act.wait_ge(pv_done, PV0 + NT * n + i - 3)
                        act.wait_ge(psum_rdy, PSUM0 + (NT - 1) * n + (max(i - 4, 1) if i >= 4 else i - 3))
                        nc.scalar.activation(probs[:, i % 4, :], score_b[i % 2], ACT.Exp).then_inc(exp_rdy, 1)
                        if project_out and with_max:
                            copy_zT(b - 1, i)
                        if i == 0 and not start:
                            copy_acc(n - 1)
                        if i == 2 and has_next:
                            copy_values(n + 1, 1 - par)

                prepare(0)
                for r in range(4):
                    high_part(0, 0, r)
                copy_values(0, 0)
                run_periods(act, period)
                copy_acc(B * NH - 1)
                copy_sums(B * NH - 1)
                for t in range(NT):
                    copy_zT(B - 1, t)

        @block.tensor
        def _(pe):
            with only_if(pe, redo):
                pe.sem_inc(pv_done, PV0)
                pe.sem_inc(sum_ps, SUM0)
                pe.sem_inc(sumT_ps, SUMT0)
                pe.sem_inc(accT_ps, ACCT0)
                pe.sem_inc(zT_ps, ZT0)

                def prepare(b):
                    pe.wait_ge(x_in, 16 * (b + 1))
                    for r in range(2):
                        if r == 0:
                            turn_free(b)
                        else:
                            pe.wait_ge(xT_sb, 2 * b + 1)
                        for j in range(4):
                            last = nc.tensor.transpose(turn_b[:, j * P:(j + 1) * P], xs[:, 4 * r + j, :], ident[:, :])
                        last.then_inc(xT_ps, 1)
                    for r in range(2):
                        if r == 0:
                            pe.wait_ge(xT_sb, 2 * b + 2)
                        else:
                            pe.wait_ge(gate_exp, 2 * b + 1)
                        for j in range(4):
                            t = 4 * r + j
                            last = nc.tensor.matmul(turn_b[:, j * NG * E:(j + 1) * NG * E], xT[:, t * P:(t + 1) * P], wg[:, :], start=True, stop=True)
                        last.then_inc(gate_ps, 1)
                    pe.wait_ge(gate_exp, 2 * b + 2)
                    pe.wait_ge(x_split, 4 * b + 4)

                def turn_free(b):
                    if not (isinstance(b, int) and b == 0):
                        pe.wait_ge(low_rdy, 4 * (NH * b - 1))

                def project(n, par, t, js=(0, 1, 2)):
                    if t == 0 and 0 in js:
                        pe.wait_ge(w_rdy[par], half_count(n, par))
                    for j in js:
                        u = 3 * t + j
                        pe.wait_ge(mult, MULT0 + U * n + u - 1)
                        for i, (a, part) in enumerate(((xh, 0), (xl, 0), (xh, 1))):
                            last = nc.tensor.matmul(proj_b[u % 2][:, 0:ED], a[:, t * P:(t + 1) * P], w[:, par, part, j, :], start=(i == 0), stop=(i == 2))
                        last.then_inc(proj_ps, 1)

                def half_count(n, par):
                    return 8 * (n - par) + 16

                def turn(n, par, r):
                    lo_tile = 4 * (r % 2)
                    pe.wait_ge(tok_rdy, TOK0 + NT * n + lo_tile + 4)
                    if r:
                        pe.wait_ge(low_rdy, 4 * n + r)
                    else:
                        pe.wait_ge(o_rdy, O0 + n - 1 if not (isinstance(n, int) and n == 0) else O0)
                    for j in range(4):
                        src = tok[:, par, lo_tile + j, 1 if r < 2 else 0, :]
                        for copy in range(2):
                            last = nc.tensor.matmul(turn_b[copy * DH:(copy + 1) * DH, j * P:(j + 1) * P], src, ident[:, :], start=True, stop=True)
                    last.then_inc(turn_ps, 1)

                def scores(n, par, i):
                    if i == 0:
                        pe.wait_ge(low_rdy, 4 * n + 4)
                        if with_max:
                            query_max(n, par)
                    pe.wait_ge(exp_rdy, EXP0 + NT * n + i - 1)
                    for lo, hi in HALVES:
                        last = nc.tensor.matmul(score_b[i % 2][:, lo:hi], kk[:, par, i * P:(i + 1) * P], qh[:, par, lo:hi], start=True, stop=False)
                        last = nc.tensor.matmul(score_b[i % 2][:, lo:hi], kk[:, par, i * P:(i + 1) * P], ql[:, par, lo:hi], start=False, stop=not with_max)
                        if with_max:
                            last = nc.tensor.matmul(score_b[i % 2][:, lo:hi], ones[0:1, :], neg_max[:, lo:hi], start=False, stop=True)
                    last.then_inc(score_ps, 1)

                def query_max(n, par):
                    pe.wait_ge(exp_rdy, EXP0 + NT * n)
                    for qt in range(NT):
                        if qt >= 2:
                            pe.wait_ge(max_rdy, NT * n + qt - 1)
                        for lo, hi in HALVES:
                            nc.tensor.matmul(score_b[qt % 2][:, lo:hi], qh[:, par, qt * P:(qt + 1) * P], kk[:, par, lo:hi], start=True, stop=False)
                            last = nc.tensor.matmul(score_b[qt % 2][:, lo:hi], ql[:, par, qt * P:(qt + 1) * P], kk[:, par, lo:hi], start=False, stop=True)
                        last.then_inc(max_ps, 1)
                    pe.wait_ge(max_rdy, NT * (n + 1))
                    for half in range(2):
                        if half:
                            pe.wait_ge(neg_rdy, 2 * n + 1)
                        for j in range(4):
                            last = nc.tensor.matmul(turn_b[0:1, j * P:(j + 1) * P], mx[:, 4 * half + j:4 * half + j + 1], ident[:, :], start=True, stop=True)
                        last.then_inc(neg_ps, 1)
                    pe.wait_ge(neg_rdy, 2 * n + 2)

                def products(n, par, i):
                    pe.wait_ge(exp_rdy, EXP0 + NT * n + i + 1)
                    if i == 0:
                        pe.wait_ge(acc_sb, ACC0 + n)
                        pe.wait_ge(vals_rdy, VALS0 + n + 1)
                    for half, (lo, hi) in enumerate(HALVES):
                        last = nc.tensor.matmul(acc_b[DH * half:DH * half + DH, :], vals[:, par, i, :], probs[:, i % 4, lo:hi], start=(i == 0), stop=(i == NT - 1))
                    last.then_inc(pv_done, 1)

                def sum_probs(n, par):
                    pe.wait_ge(psum_rdy, PSUM0 + (NT - 1) * (n + 1))
                    for j in range(4):
                        last = nc.tensor.matmul(turn_b[32 * j:32 * j + 32, 0:2 * P], ones[:, 0:32], psum[:, par, j * 2 * P:(j + 1) * 2 * P], start=True, stop=True)
                    last.then_inc(sum_ps, 1)

                def turn_sums(n):
                    pe.wait_ge(sum_sb, n + 1)
                    for j in range(2):
                        last = nc.tensor.transpose(turn_b[:, j * P:(j + 1) * P], sums[:, j * P:(j + 1) * P], ident[:, :])
                    last.then_inc(sumT_ps, 1)

                def turn_acc(n):
                    pe.wait_ge(recip_rdy, n + 1)
                    pe.wait_ge(acc_sb, ACC0 + n + 1)
                    for j in range(4):
                        last = nc.tensor.transpose(turn_b[:, j * P:(j + 1) * P], acc[:, j * P:(j + 1) * P], ident[:, :])
                    last.then_inc(accT_ps, 1)

                def turn_z(b, t, units):
                    pe.wait_ge(mult, MULT0 + units)
                    pe.wait_ge(z_rdy, Z0 + 2 * NH * (b + 1))
                    if t:
                        pe.wait_ge(zT_sb, 2 * (NT * b + t))
                    flat = z[:, t, :, :].rearrange("p e d -> p (e d)")
                    for k in range(3):
                        n_rows = min(P, ED - k * P)
                        last = nc.tensor.transpose(proj_b[0][0:n_rows, k * P:(k + 1) * P], flat[:, k * P:k * P + n_rows], ident[:, :])
                    last.then_inc(zT_ps, 1)

                def project_z(b, t):
                    pe.wait_ge(zT_sb, 2 * (NT * b + t + 1))
                    for k in range(3):
                        n_rows = min(P, ED - k * P)
                        last = nc.tensor.matmul(proj_b[1][:, 0:D], zT[0:n_rows, k, :], wo[0:n_rows, k, :], start=(k == 0), stop=(k == 2))
                    last.then_inc(out_ps, 1)

                def period(n, b, par, share, ahead, start, has_next, projecting, prep, project_out, first_head):
                    for i in range(NT):
                        js = ((), (), (0, 1, 2)) if project_out else ((0,), (1,), (2,))
                        if project_out:
                            turn_z(b - 1, i, U * (n + 2) + 3 * i)
                        if prep and i == 0:
                            prepare(b + 1)
                        if projecting:
                            project(n + 2, par, i, js[0])
                        if not start and i == 1:
                            sum_probs(n - 1, 1 - par)
                        if not start and i == 2:
                            turn_acc(n - 1)
                        if 3 <= i < 7 and has_next:
                            turn(n + 1, 1 - par, i - 3)
                        scores(n, par, i)
                        if projecting:
                            project(n + 2, par, i, js[1])
                        if not start and i == 1:
                            turn_sums(n - 1)
                        if i or not start:
                            products(*((n, par, i - 1) if i else (n - 1, 1 - par, NT - 1)))
                        if project_out:
                            project_z(b - 1, i)
                            pe.wait_ge(y_rdy, NT * (b - 1) + i + 1)
                        if projecting:
                            project(n + 2, par, i, js[2])

                pe.wait_ge(w_in, 16 * (2 + E))
                pe.wait_ge(clear, 2)
                prepare(0)
                for n in range(2):
                    for t in range(NT):
                        project(n, n, t)
                for r in range(4):
                    turn(0, 0, r)
                run_periods(pe, period)
                last_n = B * NH - 1
                products(last_n, last_n % 2, NT - 1)
                sum_probs(last_n, last_n % 2)
                turn_sums(last_n)
                turn_acc(last_n)
                for t in range(NT):
                    turn_z(B - 1, t, U * B * NH)
                    project_z(B - 1, t)
                    pe.wait_ge(y_rdy, NT * (B - 1) + t + 1)
                if not with_max:
                    turn_counts(nc, pe, judged, good, ident, turn_b[0:1, 0:P])

        @block.vector
        def _(dve):
            with only_if(dve, redo):
                dve.sem_inc(mult, MULT0)
                dve.sem_inc(tok_rdy, TOK0)
                dve.sem_inc(o_rdy, O0)
                dve.sem_inc(z_rdy, Z0)
                dve.sem_inc(norm_steps, ONE)
                for h in range(NH):
                    par = h % 2
                    dve.wait_ge(raw_in[par], 32 * (h // 2 + 1))
                    if h >= 2:
                        dve.wait_ge(w_out[par], 16 * (h // 2))
                    nc.vector.tensor_copy(w[:, par, 0, :, :], raw_w[par]).then_inc(w_high, 1)
                    dve.wait_ge(w_high, h + 1)
                    nc.vector.tensor_tensor(w[:, par, 1, :, :], raw_w[par], w[:, par, 0, :, :].bitcast(F32), ALU.subtract).then_inc(w_low, 1)
                dve.wait_ge(w_low, NH)

                def prepare(b):
                    st = Steps(dve, steps, GATE_STEPS * b)
                    for r, (lo, hi) in enumerate(HALVES):
                        dve.wait_ge(xT_sb, 2 * b + r + 1)
                        nc.vector.tensor_copy(xh[:, lo:hi], xT[:, lo:hi]).then_inc(x_split, 1)
                        dve.wait_ge(x_split, 4 * b + 2 * r + 1)
                        nc.vector.tensor_tensor(xl[:, lo:hi], xT[:, lo:hi], xh[:, lo:hi].bitcast(F32), ALU.subtract).then_inc(x_split, 1)
                    dve.wait_ge(gate_exp, 2 * b + 2)
                    st.link(nc.vector.tensor_scalar(gate[:, :, :], gate[:, :, :], 1.0, None, ALU.add))
                    st.link(nc.vector.reciprocal(gate[:, :, :], gate[:, :, :]))
                    g = gate[:, :, :].rearrange("p t (g e) -> p (t g) e", e=E)
                    for e in range(E):
                        for lo, hi, op in ((0, e, ALU.is_ge), (e + 1, E, ALU.is_gt)):
                            if lo < hi:
                                st.done(nc.vector.tensor_tensor(beats[:, :, e, lo:hi], g[:, :, lo:hi], g[:, :, e:e + 1].broadcast_to([P, NT * NG, hi - lo]), op))
                    st.settle()
                    st.link(nc.vector.reduce_sum(mask[:, :, :], beats[:, :, :, :], AX.X))
                    st.link(nc.vector.tensor_scalar(mask[:, :, :], mask[:, :, :], float(TOP), None, ALU.is_lt))
                    m = mask[:, :, :].rearrange("p (t s g) e -> p t s (g e)", t=NT, s=2)
                    st.done(nc.vector.tensor_copy(picked[:, bass.ds(b, 1), :, :].rearrange("p b t c -> p (b t) c"), m[:, :, 1, :]))
                    gs, gd = gate[:, :, 0:NH * E], gate[:, :, NH * E:]
                    st.done(nc.vector.tensor_tensor(gs, gs, m[:, :, 0, :], ALU.mult))
                    st.done(nc.vector.scalar_tensor_tensor(gd, gd, float(DH) ** -0.5, m[:, :, 1, :], ALU.mult, ALU.mult))
                    st.settle()
                    assert st.n == GATE_STEPS, st.n

                def gate_part(n, par, h, t, j):
                    if j == 0:
                        dve.wait_ge(tok_rdy, TOK0 + NT * n + t - 1)
                    u = 3 * t + j
                    dve.wait_ge(proj_ps, U * n + u + 1)
                    g = gate[:, t, bass.ds(h * E + (NH * E if j == 0 else 0), E)]
                    nc.vector.tensor_tensor(gated[:, t % 2, j, :].rearrange("p (e d) -> p e d", e=E), proj_b[u % 2][:, 0:ED].rearrange("p (e d) -> p e d", e=E),
                                            g.unsqueeze(2).broadcast_to([P, E, DH]), ALU.mult).then_inc(mult, 1)

                def sum_experts(n, par, t):
                    dve.wait_ge(mult, MULT0 + U * n + 3 * t + 3)
                    if t == 0:
                        dve.wait_ge(vals_rdy, VALS0 + n - 1)
                    nc.vector.tensor_reduce(tok[:, par, t, :, :], gated[:, t % 2, :, :].rearrange("p j (e d) -> p j d e", e=E), AX.X, ALU.add).then_inc(tok_rdy, 1)

                def low_part(n, par, r):
                    dve.wait_ge(high_rdy, 4 * n + r + 1)
                    lo, hi = HALVES[r % 2]
                    if r < 2:
                        nc.vector.tensor_tensor(kk[DH:P, par, lo:hi], turn_b[DH:P, :], kk[DH:P, par, lo:hi].bitcast(F32), ALU.subtract).then_inc(low_rdy, 1)
                    else:
                        nc.vector.tensor_tensor(ql[:, par, lo:hi], turn_b, qh[:, par, lo:hi].bitcast(F32), ALU.subtract).then_inc(low_rdy, 1)

                def reciprocals(n):
                    dve.wait_ge(sumT_ps, SUMT0 + n + 1)
                    nc.vector.reciprocal(recips[:, bass.ds(n * NT, NT)].rearrange("p (j m) -> p j m", j=4), turn_b[:, 0:2 * P].rearrange("p (m j c) -> p j m c", m=2, j=4)[:, :, :, 0]).then_inc(recip_rdy, 1)

                def normalize(n):
                    dve.wait_ge(accT_ps, ACCT0 + n + 1)
                    dve.wait_ge(recip_rdy, n + 1)
                    dve.wait_ge(share_rdy, SHARE0 + n)
                    nc.vector.tensor_tensor(o[:, :, :].rearrange("p (f j) d -> p f j d", f=2), turn_b.rearrange("p (j f d) -> p f j d", j=4, f=2),
                                            recips[:, bass.ds(n * NT, NT)].rearrange("p (f j) -> p f j", f=2).unsqueeze(3).broadcast_to([P, 2, 4, DH]), ALU.mult).then_inc(o_rdy, 1)

                def add_share(n, b, first_head, half):
                    dve.wait_ge(share_rdy, SHARE0 + n + 1)
                    dve.wait_ge(z_rdy, Z0 + 2 * n)
                    zf, sf = (a[:, half * (NT // 2):(half + 1) * (NT // 2), :, :].rearrange("p t e d -> p (t e d)") for a in (z, share))
                    if first_head:
                        dve.wait_ge(zT_ps, ZT0 + NT * b)
                        nc.vector.tensor_copy(zf, sf).then_inc(z_rdy, 1)
                    else:
                        nc.vector.tensor_tensor(zf, zf, sf, ALU.add).then_inc(z_rdy, 1)

                def residual(b, t):
                    dve.wait_ge(out_ps, NT * b + t + 1)
                    nc.vector.tensor_tensor(y[:, t, :], proj_b[1][:, 0:D], x[:, bass.ds(b * NT + t, 1), :].rearrange("p t c -> p (t c)"), ALU.add).then_inc(y_rdy, 1)

                def norm(b):
                    dve.wait_ge(y_rdy, NT * (b + 1))
                    st = Steps(dve, norm_steps, ONE + NORM_STEPS * b)
                    layer_norm(nc, st, y, out[:, bass.ds(b * NT, NT), :], stats, mv, rs, tmp)
                    st.settle_apart()
                    assert st.n == NORM_STEPS

                def max_rows(n):
                    for qt in range(NT):
                        dve.wait_ge(max_ps, NT * n + qt + 1)
                        nc.vector.reduce_max(mx[:, qt:qt + 1], score_b[qt % 2], AX.X).then_inc(max_rdy, 1)
                    for half, (lo, hi) in enumerate(HALVES):
                        dve.wait_ge(neg_ps, 2 * n + half + 1)
                        nc.vector.tensor_scalar(neg_max[:, lo:hi], turn_b[0:1, :], -1.0, None, ALU.mult).then_inc(neg_rdy, 1)

                def period(n, b, par, share, ahead, start, has_next, projecting, prep, project_out, first_head):
                    if with_max:
                        max_rows(n)
                    def between(i):
                        if prep and i == 0:
                            prepare(b + 1)
                        if not start and i == 1:
                            reciprocals(n - 1)
                        if not start and i == 2:
                            normalize(n - 1)
                        if 3 <= i < 7 and has_next:
                            low_part(n + 1, 1 - par, i - 3)

                    for i in range(NT):
                        if project_out:
                            residual(b - 1, i)
                        if prep and i == 0 or not projecting or project_out:
                            between(i)
                        if projecting:
                            for j in range(3):
                                gate_part(n + 2, par, ahead, i, j)
                                if j == (0 if i == 2 else 1) and not (prep and i == 0 or project_out):
                                    between(i)
                            sum_experts(n + 2, par, i)
                        if not start and i in (5, 7) and not project_out:
                            add_share(n - 1, b, first_head, int(i == 7))
                    if project_out:
                        for half in range(2):
                            add_share(n - 1, b, True, half)
                        norm(b - 1)

                dve.wait_ge(clear, 2)
                prepare(0)
                for n in range(2):
                    for t in range(NT):
                        for j in range(3):
                            gate_part(n, n, n, t, j)
                        sum_experts(n, n, t)
                for r in range(4):
                    low_part(0, 0, r)
                run_periods(dve, period)
                last_n = B * NH - 1
                reciprocals(last_n)
                normalize(last_n)
                for half in range(2):
                    add_share(last_n, B - 1, False, half)
                for t in range(NT):
                    residual(B - 1, t)
                norm(B - 1)
                if not with_max:
                    count_safe(nc, dve, judged, recips, ok, good)
                    raise_flag(nc, dve, judged, turn_b[0:1, 0:P], total, P * B * NH * NT, flag)


def rotary_attention(nc, x, out, ps, ident, I, redo, flag, tag):
    G = 4
    NG = H // G
    STEPS = G // 2 * NT
    NP = H // 2
    with_max = redo is not None
    ctx = ExitStack()
    with ctx:
        sb = lambda name, shape, dt=F32: ctx.enter_context(nc.sbuf_tensor(tag + name, shape, dt))
        sems, sem = semaphores(nc, ctx, tag)
        wq, wk, wv, wo, wq_sw, wk_sw = (sb(n, [P, D]) for n in ("wq", "wk", "wv", "wo", "wq_sw", "wk_sw"))
        rows = sb("rows", [1, 6, D])
        b_col = sb("b_col", [P, 4])
        b_all = sb("b_all", [P, 2, D])
        cos, sin = sb("cos", [P, T]), sb("sin", [P, T])
        ones = sb("ones", [1, P])
        xs, xT, xb = sb("xs", [P, NT, D]), sb("xT", [P, T]), sb("xb", [P, NT, D])
        rot, part = sb("rot", [P, 2, T]), sb("part", [P, 2, T])
        split = sb("split", [P, 4, T], F32R)
        keys = sb("keys", [P, 2, T], F32R)
        qpad = sb("qpad", [P, 2, G, T], F32R)
        v = sb("v", [P, NT, D])
        vg = sb("vg", [P, 2, NT, G, 32])
        probs = sb("probs", [P, 2, 2, T])
        acc = sb("acc", [P, 2, HALF])
        ao, aoT = sb("ao", [P, NT, D]), sb("aoT", [P, T])
        y = sb("y", [P, NT, D])
        stats, mv, rs, tmp = sb("stats", [P, NT, 6]), sb("mv", [P, NT, 2]), sb("rs", [P, NT]), sb("tmp", [P, 2, NT])
        recips, ok, good, total = sb("recips", [P, B * H * NT]), sb("ok", [P, B * H * NT]), sb("good", [P, 1]), sb("total", [1, 1])
        judged, mark = sem("judged"), sem("mark")
        if with_max:
            mx, neg_max = sb("mx", [P, 2, NT]), sb("neg_max", [1, 2, T])
            max_ps, max_rdy, neg_ps, neg_rdy = map(sem, ("max_ps", "max", "neg_ps", "neg"))

        w_in, swapped, clear, bias_ps, bias_sb = map(sem, ("w_in", "swapped", "clear", "bias_ps", "bias_sb"))
        x_in, xT_ps, xT_sb, proj_ps, rot_rdy, split_rdy = map(sem, ("x_in", "xT_ps", "xT_sb", "proj_ps", "rot", "split"))
        v_ps, v_rdy, xb_rdy, vg_rdy = map(sem, ("v_ps", "v_rdy", "xb_rdy", "vg_rdy"))
        staged = [sem("staged0"), sem("staged1")]
        laid_out = sem("laid_out")
        score_ps, exp_rdy, pv_done, acc_sb, accT_ps, recip_rdy, ao_rdy = map(sem, ("score_ps", "exp", "pv", "acc_sb", "accT_ps", "recip_rdy", "ao_rdy"))
        aoT_ps, aoT_sb, o_ps, y_rdy, steps = map(sem, ("aoT_ps", "aoT_sb", "o_ps", "y_rdy", "steps"))
        bank2 = lambda i: ps[:, i:i + 2, :].rearrange("p a n -> p (a n)")
        tr_ps, q_ps, qs_ps, k_ps, ks_ps, vt_ps, o2_ps = (bank2(i) for i in (0, 2, 4, 6, 0, 2, 2))
        score_b = [bank2(0), bank2(2)]
        acc_b = [ps[:, 4, :], ps[:, 5, :]]
        accT_b = ps[:, 6, :]
        W_IN = 16 * 10
        SC, VC = 2 * STEPS, STEPS
        V_STEPS = 2 + LN_STEPS
        DMAS = 1 + G
        heads_dram = nc.dram_tensor(tag + "heads", [2, H, 4, HD, T], F32).ap()

        ctx.callback(clear_semaphores, nc, sems)
        block = ctx.enter_context(nc.Block())

        @block.sync
        def _(sp):
            with only_if(sp, redo):
                sp.sem_inc(laid_out, ONE)
                for dst, src in ((wq, "L1_attn_Wq"), (wk, "L1_attn_Wk"), (wv, "L1_attn_Wv"), (wo, "L1_attn_Wo"), (cos, "cos"), (sin, "sin")):
                    sp.dma_start(dst[:, :], I[src]).then_inc(w_in, 16)
                for j, src in enumerate(("L1_attn_bq", "L1_attn_bk", "L1_attn_bv", "L1_attn_bo")):
                    sp.dma_start(rows[:, j, :], I[src].rearrange("(o n) -> o n", o=1)).then_inc(w_in, 16)
                sp.wait_ge(clear, 4)
                with sp.Fori(0, B) as b:
                    sp.wait_ge(y_rdy, ONE + b)
                    sp.dma_start(xs[:, :, :], x[:, bass.ds(b * NT, NT), :]).then_inc(x_in, 16)
                    for j in range(2):
                        for lo in range(2):
                            sp.wait_ge(split_rdy, 4 * b + 2 * j + lo + 1)
                            for c in ((2 * lo, 2 * lo + 1) if j == 0 else (lo, lo + 2)):
                                sp.dma_start(heads_dram[j, :, c, :, :], split[:, 2 * j + lo, :].bitcast(F32)).then_inc(laid_out, 16)
                    sp.wait_ge(laid_out, ONE + 16 * 8 * (b + 1))
                    sp.sem_inc(mark, 1)
                    with sp.Fori(0, NG // 2) as gp:
                        for par in range(2):
                            g = gp * 2 + par
                            sp.wait_ge(score_ps, ONE + SC * (b * NG + g))
                            sp.dma_start(keys[:, par, :].bitcast(F32), heads_dram[1, bass.ds(g * G, G), :, :, :].rearrange("h c d t -> (h c d) t")).then_inc(staged[par], 16)
                            for hh in range(G):
                                sp.dma_start(qpad[32 * hh:32 * hh + 32, par, hh, :].bitcast(F32), heads_dram[0, bass.ds(g * G + hh, 1), :, :, :].rearrange("h c d t -> (h c d) t")).then_inc(staged[par], 16)
                    for par in range(2):
                        sp.wait_ge(staged[par], 16 * DMAS * (NG // 2) * (b + 1))
                    sp.sem_inc(mark, 1)

        @block.gpsimd
        def _(pool):
            with only_if(pool, redo):
                pool.sem_inc(vg_rdy, ONE)
                nc.gpsimd.memset(qpad[:, :, :, :].bitcast(F32), 0.0).then_inc(clear, 1)
                nc.gpsimd.memset(vg[:, :, :, :, :], 0.0).then_inc(clear, 1)
                nc.gpsimd.memset(ones[:, :], 1.0).then_inc(clear, 1)
                pool.wait_ge(clear, 3)
                nc.gpsimd.memset(vg[:, :, :, :, HD:HD + 1], 1.0).then_inc(clear, 1)
                pool.wait_ge(w_in, W_IN)
                for src, dst in ((wq[:, :], wq_sw[:, :]), (wk[:, :], wk_sw[:, :]), (rows[:, 0, :], rows[:, 4, :]), (rows[:, 1, :], rows[:, 5, :])):
                    s2, d2 = src.rearrange("p (n two) -> p n two", two=2), dst.rearrange("p (n two) -> p n two", two=2)
                    nc.gpsimd.tensor_copy(d2[:, :, 0], s2[:, :, 1]).then_inc(swapped, 1)
                    nc.gpsimd.tensor_copy(d2[:, :, 1], s2[:, :, 0]).then_inc(swapped, 1)
                pool.wait_ge(bias_sb, 3)
                pool.wait_ge(clear, 4)
                with pool.Fori(0, B) as b:
                    pool.wait_ge(x_in, 16 * b + 16)
                    pool.wait_ge(y_rdy, ONE + b)
                    nc.gpsimd.tensor_tensor(xb[:, :, :], xs[:, :, :], b_all[:, 1, :].unsqueeze(1).broadcast_to([P, NT, D]), ALU.add).then_inc(xb_rdy, 1)
                    pool.wait_ge(v_rdy, b + 1)
                    pool.sem_inc(mark, 1)
                    with pool.Fori(0, NG // 2) as gp:
                        for par in range(2):
                            g = gp * 2 + par
                            pool.wait_ge(pv_done, ONE + VC * (b * NG + g))
                            for hh in range(G):
                                nc.gpsimd.tensor_copy(vg[:, par, :, hh, 0:HD], v[:, :, bass.ds(g * (G * HD) + hh * HD, HD)]).then_inc(vg_rdy, 1)

        @block.scalar
        def _(act):
            with only_if(act, redo):
                act.sem_inc(exp_rdy, ONE)
                nc.scalar.preload_act_table(ACT.Exp)
                with act.Fori(0, B) as b:
                    act.wait_ge(xT_ps, b + 1)
                    nc.scalar.copy(xT[:, :], tr_ps).then_inc(xT_sb, 1)
                    with act.Fori(0, NP) as pair:
                        for kt in range(NT):
                            step = (b * NP + pair) * NT + kt
                            act.wait_ge(pv_done, ONE + VC - 1 + step)
                            for s in range(2):
                                act.wait_ge(score_ps, ONE + SC + 2 * step + s + 1)
                                nc.scalar.activation(probs[:, kt % 2, s, :], score_b[s], ACT.Exp, scale=float(HD) ** -0.5).then_inc(exp_rdy, 1)
                    act.wait_ge(aoT_ps, b + 1)
                    nc.scalar.copy(aoT[:, :], tr_ps).then_inc(aoT_sb, 1)

        @block.tensor
        def _(pe):
            with only_if(pe, redo):
                pe.sem_inc(score_ps, ONE + SC)
                pe.sem_inc(pv_done, ONE + VC)
                pe.wait_ge(w_in, W_IN)
                pe.wait_ge(clear, 4)
                pe.wait_ge(swapped, 8)
                for j, src in enumerate((0, 1, 4, 5)):
                    last = nc.tensor.matmul(ps[:, 0, j:j + 1], rows[:, src, :], ones[0:1, 0:1], start=True, stop=True)
                last.then_inc(bias_ps, 1)
                for j in range(2):
                    nc.tensor.matmul(ps[:, 1 + j, 0:D], ones[0:1, 0:P], rows[:, 2 + j, :], start=True, stop=True).then_inc(bias_ps, 1)
                pe.wait_ge(bias_sb, 3)

                def query_max(par, hh, s, pair_no):
                    head = 2 * pair_no + s
                    for qt in range(NT):
                        if qt >= 2:
                            pe.wait_ge(max_rdy, NT * head + qt - 1)
                        for c in range(0, T, HALF):
                            last = nc.tensor.matmul(score_b[qt % 2][:, c:c + HALF], qpad[:, par, hh, qt * P:(qt + 1) * P], keys[:, par, c:c + HALF], start=True, stop=True)
                        last.then_inc(max_ps, 1)
                    pe.wait_ge(max_rdy, NT * head + NT)
                    for half in range(2):
                        if half:
                            pe.wait_ge(neg_rdy, 2 * head + 1)
                        for j in range(NT // 2):
                            qt = half * (NT // 2) + j
                            last = nc.tensor.matmul(ps[0:1, 7, j * P:(j + 1) * P], mx[:, s, qt:qt + 1], ident[:, :], start=True, stop=True)
                        last.then_inc(neg_ps, 1)
                    pe.wait_ge(neg_rdy, 2 * head + 2)

                with pe.Fori(0, B) as b:
                    pe.wait_ge(x_in, 16 * b + 16)
                    pe.wait_ge(y_rdy, ONE + b)
                    for t in range(NT):
                        last = nc.tensor.transpose(tr_ps[:, t * P:(t + 1) * P], xs[:, t, :], ident[:, :])
                    last.then_inc(xT_ps, 1)
                    pe.wait_ge(xT_sb, b + 1)
                    for w, dst in ((wq, q_ps), (wq_sw, qs_ps), (wk, k_ps), (wk_sw, ks_ps)):
                        for c in range(0, T, HALF):
                            last = nc.tensor.matmul(dst[:, c:c + HALF], w[:, :], xT[:, c:c + HALF], start=True, stop=True)
                        last.then_inc(proj_ps, 1)
                    pe.wait_ge(rot_rdy, 4 * b + 1)
                    for t in range(NT):
                        last = nc.tensor.matmul(vt_ps[:, t * P:(t + 1) * P], xT[:, t * P:(t + 1) * P], wv[:, :], start=True, stop=True)
                    last.then_inc(v_ps, 1)
                    pe.wait_ge(rot_rdy, 4 * b + 4)
                    pe.wait_ge(v_rdy, b + 1)
                    pe.sem_inc(mark, 1)
                    with pe.Fori(0, NG // 2) as gp:
                        first = (b * NG + gp * 2) * STEPS
                        pair0 = b * NP + gp * G

                        def scores(i):
                            par, pp, kt = i // STEPS, i // NT % (G // 2), i % NT
                            if i % STEPS == 0:
                                pe.wait_ge(staged[par], 16 * DMAS * (b * (NG // 2) + gp + 1))
                                pe.wait_ge(vg_rdy, ONE + G * (b * NG + gp * 2 + par + 1))
                            if with_max and kt == 0:
                                pe.wait_ge(exp_rdy, ONE + 2 * (first + i))
                                for s in range(2):
                                    query_max(par, 2 * pp + s, s, pair0 + i // NT)
                            for s in range(2):
                                hh = 2 * pp + s
                                pe.wait_ge(exp_rdy, ONE + (2 * (first + i) + s - 1 if i else 2 * first))
                                for c in range(0, T, HALF):
                                    last = nc.tensor.matmul(score_b[s][:, c:c + HALF], keys[:, par, kt * P:(kt + 1) * P], qpad[:, par, hh, c:c + HALF], start=True, stop=not with_max)
                                    if with_max:
                                        last = nc.tensor.matmul(score_b[s][:, c:c + HALF], ones[0:1, :], neg_max[:, s, c:c + HALF], start=False, stop=True)
                                last.then_inc(score_ps, 1)

                        def products(i):
                            par, pp, kt, pair = i // STEPS, i // NT % (G // 2), i % NT, i // NT
                            pe.wait_ge(exp_rdy, ONE + 2 * (first + i) + 2)
                            if kt == 0:
                                pe.wait_ge(acc_sb, ONE + (pair0 + pair - 1 if pair else pair0))
                            for s in range(2):
                                for half in range(2):
                                    at = 64 * s + 32 * half
                                    last = nc.tensor.matmul(acc_b[pair % 2][at:at + 32, :], vg[:, par, kt, 2 * pp + s, :], probs[:, kt % 2, s, half * HALF:(half + 1) * HALF],
                                                            start=(kt == 0), stop=(kt == NT - 1))
                            last.then_inc(pv_done, 1)

                        def turn(pair):
                            pe.wait_ge(acc_sb, ONE + pair0 + pair + 1)
                            pe.wait_ge(ao_rdy, ONE + 2 * (pair0 + pair))
                            for j in range(4):
                                last = nc.tensor.transpose(accT_b[:, j * P:(j + 1) * P], acc[:, pair % 2, j * P:(j + 1) * P], ident[:, :])
                            last.then_inc(accT_ps, 1)

                        for i in range(2 * STEPS):
                            if with_max and i and i % NT == 0:
                                products(i - 1)
                                turn(i // NT - 1)
                                scores(i)
                                continue
                            scores(i)
                            if i:
                                products(i - 1)
                            if not with_max and i % NT == 2 and i > NT:
                                turn(i // NT - 1)
                        products(2 * STEPS - 1)
                        turn(2 * STEPS // NT - 1)
                    pe.wait_ge(ao_rdy, ONE + 2 * NP * (b + 1))
                    for t in range(NT):
                        last = nc.tensor.transpose(tr_ps[:, t * P:(t + 1) * P], ao[:, t, :], ident[:, :])
                    last.then_inc(aoT_ps, 1)
                    pe.wait_ge(aoT_sb, b + 1)
                    for t in range(NT):
                        last = nc.tensor.matmul(o2_ps[:, t * P:(t + 1) * P], aoT[:, t * P:(t + 1) * P], wo[:, :], start=True, stop=True)
                    last.then_inc(o_ps, 1)
                if not with_max:
                    turn_counts(nc, pe, judged, good, ident, accT_b[0:1, 0:P])

        @block.vector
        def _(dve):
            with only_if(dve, redo):
                dve.sem_inc(y_rdy, ONE)
                dve.sem_inc(acc_sb, ONE)
                dve.sem_inc(ao_rdy, ONE)
                dve.wait_ge(bias_ps, 3)
                nc.vector.tensor_copy(b_col[:, :], ps[:, 0, 0:4]).then_inc(bias_sb, 1)
                for j in range(2):
                    nc.vector.tensor_copy(b_all[:, j, :], ps[:, 1 + j, 0:D]).then_inc(bias_sb, 1)
                dve.wait_ge(bias_sb, 3)
                dve.wait_ge(w_in, W_IN)

                def row_max(s, head):
                    for qt in range(NT):
                        dve.wait_ge(max_ps, NT * head + qt + 1)
                        nc.vector.reduce_max(mx[:, s, qt:qt + 1], score_b[qt % 2], AX.X).then_inc(max_rdy, 1)
                    for half in range(2):
                        dve.wait_ge(neg_ps, 2 * head + half + 1)
                        nc.vector.tensor_scalar(neg_max[:, s, half * HALF:(half + 1) * HALF], ps[0:1, 7, :], -1.0, None, ALU.mult).then_inc(neg_rdy, 1)

                def finish_pair(b, pair, par):
                    n = b * NP + pair
                    dve.wait_ge(pv_done, ONE + VC + NT * (n + 1))
                    nc.vector.tensor_copy(acc[:, par, :], acc_b[par]).then_inc(acc_sb, 1)
                    dve.wait_ge(accT_ps, n + 1)
                    t5 = accT_b.rearrange("p (j s f c) -> p s f j c", j=4, s=2, f=2)
                    recip = recips[:, bass.ds(n * 2 * NT, 2 * NT)].rearrange("p (s f j) -> p s f j", s=2, f=2)
                    nc.vector.reciprocal(recip, t5[:, :, :, :, HD]).then_inc(recip_rdy, 1)
                    dve.wait_ge(recip_rdy, n + 1)
                    for s in range(2):
                        o = ao[:, :, bass.ds(pair * (2 * HD) + s * HD, HD)].rearrange("p (f j) c -> p f j c", f=2)
                        nc.vector.tensor_tensor(o, t5[:, s, :, :, 0:HD], recip[:, s, :, :].unsqueeze(3).broadcast_to([P, 2, 4, HD]), ALU.mult).then_inc(ao_rdy, 1)

                with dve.Fori(0, B) as b:
                    st = Steps(dve, steps, b * V_STEPS)
                    dve.wait_ge(laid_out, ONE + 16 * 8 * b)
                    for j, (src, src_sw, w) in enumerate(((q_ps, qs_ps, 0), (k_ps, ks_ps, 2))):
                        dve.wait_ge(proj_ps, 4 * b + 2 * j + 1)
                        nc.vector.scalar_tensor_tensor(rot[:, j, :], src, b_col[:, j:j + 1], cos[:, :], ALU.add, ALU.mult).then_inc(rot_rdy, 1)
                        dve.wait_ge(proj_ps, 4 * b + 2 * j + 2)
                        nc.vector.scalar_tensor_tensor(part[:, j, :], src_sw, b_col[:, 2 + j:3 + j], sin[:, :], ALU.add, ALU.mult).then_inc(rot_rdy, 1)
                        dve.wait_ge(rot_rdy, 4 * b + 2 * j + 2)
                        st.link(nc.vector.tensor_tensor(rot[:, j, :], rot[:, j, :], part[:, j, :], ALU.add))
                        nc.vector.tensor_copy(split[:, w, :], rot[:, j, :]).then_inc(split_rdy, 1)
                        dve.wait_ge(split_rdy, 4 * b + 2 * j + 1)
                        nc.vector.tensor_tensor(split[:, w + 1, :], rot[:, j, :], split[:, w, :].bitcast(F32), ALU.subtract).then_inc(split_rdy, 1)
                    dve.wait_ge(v_ps, b + 1)
                    dve.wait_ge(vg_rdy, ONE + G * NG * b)
                    nc.vector.tensor_tensor(v[:, :, :], vt_ps.rearrange("p (t c) -> p t c", t=NT), b_all[:, 0, :].unsqueeze(1).broadcast_to([P, NT, D]), ALU.add).then_inc(v_rdy, 1)
                    with dve.Fori(0, NP // 2) as pp:
                        for par in range(2):
                            if with_max:
                                for s in range(2):
                                    row_max(s, 2 * (b * NP + pp * 2 + par) + s)
                            finish_pair(b, pp * 2 + par, par)
                    dve.wait_ge(o_ps, b + 1)
                    dve.wait_ge(xb_rdy, b + 1)
                    nc.vector.tensor_tensor(y[:, :, :].rearrange("p t c -> p (t c)"), o2_ps, xb[:, :, :].rearrange("p t c -> p (t c)"), ALU.add).then_inc(y_rdy, 1)
                    dve.wait_ge(y_rdy, ONE + b + 1)
                    layer_norm(nc, st, y, out[:, bass.ds(b * NT, NT), :], stats, mv, rs, tmp)
                    st.settle()
                    assert st.n == V_STEPS, st.n
                if not with_max:
                    count_safe(nc, dve, judged, recips, ok, good)
                    raise_flag(nc, dve, judged, accT_b[0:1, 0:P], total, P * B * H * NT, flag)


def depth_ffn(nc, x, out_dram, ps, ident, I):
    FF = 512
    NB = FF // P
    K = T // 2
    ctx = ExitStack()
    with ctx:
        sb = lambda name, shape, dt=F32: ctx.enter_context(nc.sbuf_tensor("d_" + name, shape, dt))
        sems, sem = semaphores(nc, ctx, "d_")
        w1, w2 = sb("w1", [P, FF]), sb("w2", [P, NB, D])
        b1, b2 = sb("b1", [P, NB]), sb("b2", [P, 1])
        wr, wr_rep, br = sb("wr", [P, 1]), sb("wr_rep", [P, P]), sb("br", [P, 1])
        xs, xT = sb("xs", [P, NT, D]), sb("xT", [P, T])
        w_row, w_col, ge = sb("w_row", [P, T]), sb("w_col", [P, NT]), sb("ge", [P, 2, T])
        count, sel, keep = sb("count", [P, NT]), sb("sel", [P, NT]), sb("keep", [P, NT])
        hid, blk = sb("hid", [P, NB, T]), sb("blk", [P, T])
        kept, y, yo = sb("kept", [P, NT, D]), sb("y", [P, NT, D]), sb("yo", [P, NT, D])
        stats, mv, rs, tmp = sb("stats", [P, NT, 6]), sb("mv", [P, NT, 2]), sb("rs", [P, NT]), sb("tmp", [P, 2, NT])

        w_in, wr_rdy, x_in, x_used, xT_ps, xT_sb = map(sem, ("w_in", "wr", "x_in", "x_used", "xT_ps", "xT_sb"))
        row_ps, row_sb, col_ps, col_sb = map(sem, ("row_ps", "row_sb", "col_ps", "col_sb"))
        hid_ps, hid_sb, blk_ps, blk_sb, blkT_ps = map(sem, ("hid_ps", "hid_sb", "blk_ps", "blk_sb", "blkT_ps"))
        y_rdy, out_rdy, out_done, steps = map(sem, ("y", "out", "out_done", "steps"))
        bank2 = lambda i: ps[:, i:i + 2, :].rearrange("p a n -> p (a n)")
        tr_ps, row_b, hid_b = bank2(0), bank2(2), [bank2(4), bank2(6)]
        W_IN = 16 * 6
        V_STEPS = NT + 2 + (NT - 1) + (NT - 1) + LN_STEPS

        ctx.callback(clear_semaphores, nc, sems)
        block = ctx.enter_context(nc.Block())

        @block.sync
        def _(sp):
            sp.sem_inc(out_done, ONE)
            sp.dma_start(wr[:, :], I["L1_ffn_w_r"]).then_inc(w_in, 16)
            sp.dma_start(br[:, :], I["L1_ffn_b_r"].rearrange("(o n) -> o n", o=1).broadcast_to([P, 1])).then_inc(w_in, 16)
            sp.dma_start(w1[:, :], I["L1_ffn_W1"]).then_inc(w_in, 16)
            sp.dma_start(w2[:, :, :], I["L1_ffn_W2"].rearrange("(n p) c -> p n c", p=P)).then_inc(w_in, 16)
            with nc.allow_non_contiguous_dma("two bias vectors onto partitions"):
                sp.dma_start(b1[:, :], I["L1_ffn_b1"].rearrange("(n p) -> p n", p=P)).then_inc(w_in, 16)
                sp.dma_start(b2[:, :], I["L1_ffn_b2"].rearrange("(p o) -> p o", o=1)).then_inc(w_in, 16)
            with sp.Fori(0, B) as b:
                sp.wait_ge(x_used, ONE + b)
                sp.wait_ge(xT_ps, ONE + b)
                sp.dma_start(xs[:, :, :], x[:, bass.ds(b * NT, NT), :]).then_inc(x_in, 16)
                sp.wait_ge(out_rdy, b + 1)
                sp.dma_start(out_dram[b].rearrange("(t p) c -> p t c", p=P), yo[:, :, :]).then_inc(out_done, 16)
            sp.wait_ge(out_done, ONE + 16 * B)

        @block.gpsimd
        def _(pool):
            pool.wait_ge(w_in, W_IN)
            nc.gpsimd.tensor_copy(wr_rep[:, :], wr[:, 0:1].broadcast_to([P, P])).then_inc(wr_rdy, 1)

        @block.scalar
        def _(act):
            nc.scalar.preload_act_table(ACT.Gelu)
            act.wait_ge(w_in, W_IN)
            with act.Fori(0, B) as b:
                act.wait_ge(xT_ps, ONE + b + 1)
                nc.scalar.copy(xT[:, :], tr_ps).then_inc(xT_sb, 1)
                act.wait_ge(blk_ps, ONE + b)
                for n in range(NB):
                    act.wait_ge(hid_ps, NB * b + n + 1)
                    nc.scalar.activation(hid[:, n, :], hid_b[n % 2], ACT.Gelu, bias=b1[:, n:n + 1]).then_inc(hid_sb, 1)

        @block.tensor
        def _(pe):
            pe.sem_inc(blk_ps, ONE)
            pe.sem_inc(xT_ps, ONE)
            pe.wait_ge(w_in, W_IN)
            pe.wait_ge(wr_rdy, 1)
            with pe.Fori(0, B) as b:
                pe.wait_ge(x_in, 16 * b + 16)
                pe.wait_ge(blk_sb, ONE + b)
                for t in range(NT):
                    last = nc.tensor.transpose(tr_ps[:, t * P:(t + 1) * P], xs[:, t, :], ident[:, :])
                last.then_inc(xT_ps, 1)
                pe.wait_ge(xT_sb, b + 1)
                pe.wait_ge(y_rdy, ONE + b)
                for s in range(0, T, HALF):
                    last = nc.tensor.matmul(row_b[:, s:s + HALF], wr_rep[:, :], xT[:, s:s + HALF], start=True, stop=True)
                last.then_inc(row_ps, 1)
                for n in range(NB):
                    if n >= 2:
                        pe.wait_ge(hid_sb, NB * b + n - 1)
                    for s in range(0, T, HALF):
                        last = nc.tensor.matmul(hid_b[n % 2][:, s:s + HALF], w1[:, n * P:(n + 1) * P], xT[:, s:s + HALF], start=True, stop=True)
                    last.then_inc(hid_ps, 1)
                    if n == 1:
                        pe.wait_ge(row_sb, b + 1)
                        for t in range(NT):
                            last = nc.tensor.transpose(row_b[:, t * P:(t + 1) * P], w_row[:, t * P:(t + 1) * P], ident[:, :])
                        last.then_inc(col_ps, 1)
                for n in range(NB):
                    pe.wait_ge(hid_sb, NB * b + n + 1)
                    for s in range(0, T, HALF):
                        last = nc.tensor.matmul(tr_ps[:, s:s + HALF], w2[:, n, :], hid[:, n, s:s + HALF], start=(n == 0), stop=(n == NB - 1))
                last.then_inc(blk_ps, 1)
                pe.wait_ge(blk_sb, ONE + b + 1)
                pe.wait_ge(col_sb, b + 1)
                for t in range(NT):
                    last = nc.tensor.transpose(row_b[:, t * P:(t + 1) * P], blk[:, t * P:(t + 1) * P], ident[:, :])
                last.then_inc(blkT_ps, 1)

        @block.vector
        def _(dve):
            dve.sem_inc(blk_sb, ONE)
            dve.sem_inc(y_rdy, ONE)
            dve.sem_inc(x_used, ONE)
            dve.wait_ge(w_in, W_IN)
            with dve.Fori(0, B) as b:
                st = Steps(dve, steps, b * V_STEPS)
                dve.wait_ge(row_ps, b + 1)
                nc.vector.tensor_scalar(w_row[:, :], row_b, br[:, 0:1], None, ALU.add).then_inc(row_sb, 1)
                dve.wait_ge(col_ps, b + 1)
                nc.vector.tensor_copy(w_col[:, :], row_b.rearrange("p (t r) -> p t r", r=P)[:, :, 0]).then_inc(col_sb, 1)
                dve.wait_ge(col_sb, b + 1)
                for t in range(NT):
                    if t >= 2:
                        dve.wait_ge(steps, b * V_STEPS + t - 1)
                    st.done(nc.vector.tensor_scalar(ge[:, t % 2, :], w_row[:, :], w_col[:, t:t + 1], None, ALU.is_ge, ALU.add,
                                                    accum_out=count[:, t:t + 1]))
                st.settle()
                st.link(nc.vector.tensor_scalar(sel[:, :], count[:, :], float(K), None, ALU.is_lt))
                st.link(nc.vector.tensor_scalar(keep[:, :], sel[:, :], -1.0, 2.0, ALU.mult, ALU.add))
                dve.wait_ge(x_in, 16 * b + 16)
                for t in range(NT):
                    last = nc.vector.tensor_scalar(kept[:, t, :], xs[:, t, :], keep[:, t:t + 1], None, ALU.mult)
                    if t < NT - 1:
                        st.done(last)
                last.then_inc(x_used, 1)
                dve.wait_ge(x_used, ONE + b + 1)
                st.settle()
                dve.wait_ge(blk_ps, ONE + b + 1)
                nc.vector.tensor_scalar(blk[:, :], tr_ps, b2[:, 0:1], None, ALU.add).then_inc(blk_sb, 1)
                dve.wait_ge(blkT_ps, b + 1)
                for t in range(NT):
                    last = nc.vector.scalar_tensor_tensor(y[:, t, :], row_b[:, t * P:(t + 1) * P], sel[:, t:t + 1], kept[:, t, :], ALU.mult, ALU.add)
                    if t < NT - 1:
                        st.done(last)
                last.then_inc(y_rdy, 1)
                dve.wait_ge(y_rdy, ONE + b + 1)
                st.settle()
                dve.wait_ge(out_done, ONE + 16 * b)
                layer_norm(nc, st, y, yo[:, :, :], stats, mv, rs, tmp)
                st.settle()
                nc.vector.tensor_copy(tmp[:, 0, :], mv[:, :, 1]).then_inc(out_rdy, 1)
                assert st.n == V_STEPS, st.n


def program(nc, I, out_dram):
    ctx = ExitStack()
    with ctx:
        ps = ctx.enter_context(nc.psum_tensor("banks", [P, 8, HALF], F32))
        ident = ctx.enter_context(nc.sbuf_tensor("ident", [P, P], F32))
        flag = ctx.enter_context(nc.sbuf_tensor("flag", [1, 1], I32))
        r1 = ctx.enter_context(nc.sbuf_tensor("r1", [P, B * NT, D], F32))
        r2 = ctx.enter_context(nc.sbuf_tensor("r2", [P, B * NT, D], F32))
        linear_attention(nc, I["L0_attn_x"], r1, ps, ident, I)
        for attention, x, y, tag in ((switch_attention, r1, r2, "b"), (rotary_attention, r2, r1, "c")):
            attention(nc, x, y, ps, ident, I, None, flag, tag + "_")
            attention(nc, x, y, ps, ident, I, flag, flag, tag + "_redo_")
        depth_ffn(nc, r1, out_dram, ps, ident, I)


def constants():
    import numpy as np

    ident = np.eye(P, dtype=np.float32)
    row, col = np.arange(P)[:, None], np.arange(P)[None, :]
    same_head = row // HD == col // HD
    sel = np.stack([same_head & (col % HD == m) for m in range(HD)] + [same_head], axis=1).astype(np.float32)
    inv = (1.0 / np.float32(10000.0) ** (np.arange(0, HD, 2, dtype=np.float32) / HD)).astype(np.float32)
    freqs = np.arange(T, dtype=np.float32)[:, None] * inv[None, :]
    ang = np.concatenate((freqs, freqs), axis=-1)[:, ::2].astype(np.float64)
    pair = np.arange(D) % HD // 2
    cos = np.cos(ang)[:, pair].T.astype(np.float32)
    sin = (np.sin(ang)[:, pair] * np.where(np.arange(D) % 2 == 0, -1, 1)).T.astype(np.float32)
    return {"ident": ident, "sel": sel, "cos": np.ascontiguousarray(cos), "sin": np.ascontiguousarray(sin)}


_NAMES = ("L0_attn_x", "L0_attn_Wq", "L0_attn_bq", "L0_attn_Wk", "L0_attn_bk", "L0_attn_Wv", "L0_attn_bv",
          "L0_attn_Wo", "L0_attn_bo", "L0_ffn_Wq", "L0_ffn_Wkv", "L0_ffn_Ws", "L0_ffn_Wd", "L0_ffn_Wo",
          "L1_attn_Wq", "L1_attn_bq", "L1_attn_Wk", "L1_attn_bk", "L1_attn_Wv", "L1_attn_bv",
          "L1_attn_Wo", "L1_attn_bo", "L1_ffn_w_r", "L1_ffn_b_r", "L1_ffn_W1", "L1_ffn_b1",
          "L1_ffn_W2", "L1_ffn_b2")


def kernel(**inputs):
    import numpy as _np
    import concourse.bacc as _bacc
    from concourse import mybir as _mybir
    from concourse.bass_utils import run_bass_kernel_spmd as _run

    nc = _bacc.Bacc("TRN2", target_bir_lowering=False, num_devices=1)
    arrays, aps = {}, {}
    given = {name: inputs[name] for name in _NAMES}
    given.update(constants())
    for name, value in given.items():
        a = _np.ascontiguousarray(value)
        arrays[f"in_{name}"] = a
        aps[name] = nc.dram_tensor(f"in_{name}", a.shape, _mybir.dt.from_np(a.dtype), kind="ExternalInput").ap()
    out = nc.dram_tensor("out", (B, T, D), F32, kind="ExternalOutput").ap()
    program(nc, aps, out)
    r = _run(nc, [arrays], core_ids=[0])
    return r.results[0]["out"]
```

```python
import concourse.bass as bass
from concourse import mybir
from contextlib import ExitStack, nullcontext

F32 = mybir.dt.float32
F32R = mybir.dt.float32r
I32 = mybir.dt.int32
ALU = mybir.AluOpType
ACT = mybir.ActivationFunctionType
AX = mybir.AxisListType

P = 128
B, T, D = 4, 1024, 128
NT = T // P
HALF = 512
LN_EPS = 1e-5
H = 16
HD = D // H


ONE = 1


class Steps:

    def __init__(self, eng, sem, base=0):
        self.eng, self.sem, self.base, self.n = eng, sem, base, 0

    def done(self, ins):
        ins.then_inc(self.sem, 1)
        self.n += 1
        return ins

    def settle(self):
        self.eng.wait_ge(self.sem, self.base + self.n)

    def settle_apart(self):
        self.settle()
        self.eng.sem_inc(self.sem, 1)
        self.n += 1

    def link(self, ins):
        self.done(ins)
        self.settle()


def layer_norm(nc, st, y, out, stats, mv, rs, tmp):
    st.settle()
    for t in range(NT):
        st.done(nc.vector.bn_stats(stats[:, t, :], y[:, t, :]))
    st.settle_apart()
    for t in range(NT):
        st.done(nc.vector.bn_aggr(mv[:, t, :], stats[:, t, :]))
    st.settle()
    var = tmp[:, 0, :]
    half_step = tmp[:, 1, :]
    st.link(nc.vector.tensor_scalar(var, mv[:, :, 1], LN_EPS, None, ALU.add))
    st.link(nc.vector.tensor_scalar(rs[:, :].bitcast(I32), var.bitcast(I32), -0.5, float(0x5F3759DF),
                                    ALU.mult, ALU.add))
    for _ in range(3):
        st.link(nc.vector.tensor_tensor(half_step, rs[:, :], rs[:, :], ALU.mult))
        st.link(nc.vector.scalar_tensor_tensor(half_step, half_step, -0.5, var, ALU.mult, ALU.mult))
        st.link(nc.vector.scalar_tensor_tensor(rs[:, :], half_step, 1.5, rs[:, :], ALU.add, ALU.mult))
    for t in range(NT):
        st.done(nc.vector.tensor_scalar(out[:, t, :], y[:, t, :], mv[:, t, 0:1], rs[:, t:t + 1],
                                        ALU.subtract, ALU.mult))


LN_STEPS = 3 * NT + 3 + 9


def semaphores(nc, ctx, tag):
    sems = []

    def sem(name):
        sems.append(ctx.enter_context(nc.semaphore(tag + name)))
        return sems[-1]

    return sems, sem


def clear_semaphores(nc, sems):
    with nc.Block() as block:
        @block.gpsimd
        def _(pool):
            for sem in sems:
                pool.sem_clear(sem)


SAFE_LOW, SAFE_HIGH = 1e-18, 1e18


def only_if(eng, flag):
    return nullcontext() if flag is None else eng.If(eng.value_load(flag[0:1, 0:1], min_val=0, max_val=1))


def count_safe(nc, dve, judged, recips, ok, good):
    nc.vector.tensor_scalar(ok[:, :], recips[:, :], SAFE_LOW, None, ALU.is_ge).then_inc(judged, 1)
    dve.wait_ge(judged, 1)
    nc.vector.scalar_tensor_tensor(ok[:, :], recips[:, :], SAFE_HIGH, ok[:, :], ALU.is_le, ALU.mult).then_inc(judged, 1)
    dve.wait_ge(judged, 2)
    nc.vector.reduce_sum(good[:, 0:1], ok[:, :], AX.X).then_inc(judged, 1)


def turn_counts(nc, pe, judged, good, ident, row):
    pe.wait_ge(judged, 3)
    nc.tensor.matmul(row, good[:, 0:1], ident[:, :], start=True, stop=True).then_inc(judged, 1)


def raise_flag(nc, dve, judged, row, total, count, flag):
    dve.wait_ge(judged, 4)
    nc.vector.reduce_sum(total[0:1, 0:1], row, AX.X).then_inc(judged, 1)
    dve.wait_ge(judged, 5)
    nc.vector.tensor_scalar(flag[0:1, 0:1], total[0:1, 0:1], float(count), None, ALU.is_lt).then_inc(judged, 1)
    dve.wait_ge(judged, 6)


def linear_attention(nc, x_dram, out, ps, ident, I):
    ctx = ExitStack()
    with ctx:
        sb = lambda name, shape, dt=F32: ctx.enter_context(nc.sbuf_tensor(name, shape, dt))
        sems, sem = semaphores(nc, ctx, "a_")
        wq, wk, wv, wo = (sb(f"a_{n}", [P, D]) for n in ("wq", "wk", "wv", "wo"))
        wv_rep = sb("a_wv_rep", [P, HD, H, HD])
        bq, bk = sb("a_bq", [P, 1]), sb("a_bk", [P, 1])
        rows = sb("a_rows", [1, 2, D])
        bv_rep = sb("a_bv_rep", [1, HD, H, HD])
        bv_col = sb("a_bv_col", [P, HD])
        bo_all = sb("a_bo_all", [P, D])
        sel = sb("a_sel", [P, HD + 1, P])
        ones = sb("a_ones", [P, T])
        xs, xT = sb("a_xs", [P, NT, D]), sb("a_xT", [P, T])
        low, relu, expo = (sb(f"a_{n}", [P, 2, T]) for n in ("low", "relu", "expo"))
        q, k = sb("a_q", [P, T]), sb("a_k", [P, T])
        kv, scan, qscan = sb("a_kv", [P, T]), sb("a_scan", [P, 2, T]), sb("a_qscan", [P, 2, T])
        rden, vals = sb("a_rden", [P, T]), sb("a_vals", [P, T])
        xb, y = sb("a_xb", [P, NT, D]), sb("a_y", [P, NT, D])
        stats, mv, rs, tmp = sb("a_stats", [P, NT, 6]), sb("a_mv", [P, NT, 2]), sb("a_rs", [P, NT]), sb("a_tmp", [P, 2, NT])

        x_in, w_in, ones_rdy, reps, bias_ps, bias_sb = map(sem, ("x_in", "w_in", "ones", "reps", "bias_ps", "bias_sb"))
        xT_ps, xT_sb, qk_ps, low_rdy, exp_rdy, q_rdy = map(sem, ("xT_ps", "xT_sb", "qk_ps", "low", "exp", "q"))
        v_ps, kv_rdy, scan_rdy, qs_rdy, acc_ps = map(sem, ("v_ps", "kv", "scan", "qs", "acc_ps"))
        den_read, vals_rdy, o_ps, xb_rdy, y_rdy, steps = map(sem, ("den_read", "vals", "o_ps", "xb", "y", "steps"))
        NJ = HD + 1
        bank2 = lambda i: ps[:, i:i + 2, :].rearrange("p a n -> p (a n)")
        tr_ps, q_ps, k_ps = bank2(0), bank2(2), bank2(4)
        vb_ps = [bank2(6), bank2(0)]
        num_ps, den_ps, o2_ps = q_ps, k_ps, bank2(0)
        V_STEPS = 2 + 2 + LN_STEPS
        W_IN = 16 * 10

        ctx.callback(clear_semaphores, nc, sems)
        block = ctx.enter_context(nc.Block())

        @block.sync
        def _(sp):
            sp.dma_start(ident[:, :], I["ident"]).then_inc(w_in, 16)
            for dst, src in ((wq, "L0_attn_Wq"), (wk, "L0_attn_Wk"), (wv, "L0_attn_Wv"), (wo, "L0_attn_Wo")):
                sp.dma_start(dst[:, :], I[src]).then_inc(w_in, 16)
            for dst, src in ((bq, "L0_attn_bq"), (bk, "L0_attn_bk")):
                sp.dma_start(dst[:, :], I[src].rearrange("(p o) -> p o", o=1)).then_inc(w_in, 16)
            for j, src in enumerate(("L0_attn_bv", "L0_attn_bo")):
                sp.dma_start(rows[:, j, :], I[src].rearrange("(o n) -> o n", o=1)).then_inc(w_in, 16)
            sp.dma_start(sel[:, :, :], I["sel"]).then_inc(w_in, 16)
            with sp.Fori(0, B) as b:
                sp.wait_ge(y_rdy, ONE + b)
                sp.dma_start(xs[:, :, :], x_dram[b].rearrange("(t p) c -> p t c", p=P)).then_inc(x_in, 16)

        @block.gpsimd
        def _(pool):
            nc.gpsimd.memset(ones[:, :], 1.0).then_inc(ones_rdy, 1)
            pool.wait_ge(w_in, W_IN)
            for m in range(HD):
                nc.gpsimd.tensor_copy(wv_rep[:, m, :, :],
                                      wv[:, :].rearrange("p (h m) -> p m h", h=H)[:, m, :].unsqueeze(2).broadcast_to([P, H, HD])).then_inc(reps, 1)
                nc.gpsimd.tensor_copy(bv_rep[:, m, :, :],
                                      rows[:, 0, :].rearrange("p (h m) -> p m h", h=H)[:, m, :].unsqueeze(2).broadcast_to([1, H, HD])).then_inc(reps, 1)
            pool.wait_ge(bias_sb, 2)
            with pool.Fori(0, B) as b:
                pool.wait_ge(x_in, 16 * b + 16)
                pool.wait_ge(y_rdy, ONE + b)
                nc.gpsimd.tensor_tensor(xb[:, :, :], xs[:, :, :],
                                        bo_all[:, :].unsqueeze(1).broadcast_to([P, NT, D]), ALU.add).then_inc(xb_rdy, 1)
                for j in range(NJ):
                    pool.wait_ge(scan_rdy, b * NJ + j + 1)
                    if j >= 2:
                        pool.wait_ge(acc_ps, b * NJ + j - 1)
                    nc.gpsimd.tensor_tensor(qscan[:, j % 2, :], scan[:, j % 2, :], q[:, :], ALU.mult).then_inc(qs_rdy, 1)

        @block.scalar
        def _(act):
            nc.scalar.preload_act_table(ACT.Exp)
            with act.Fori(0, B) as b:
                act.wait_ge(xT_ps, b + 1)
                nc.scalar.copy(xT[:, :], tr_ps).then_inc(xT_sb, 1)
                for j in range(2):
                    act.wait_ge(low_rdy, 2 * b + j + 1)
                    nc.scalar.activation(expo[:, j, :], low[:, j, :], ACT.Exp).then_inc(exp_rdy, 1)

        @block.tensor
        def _(pe):
            pe.wait_ge(w_in, W_IN)
            pe.wait_ge(ones_rdy, 1)
            pe.wait_ge(reps, 2 * HD)
            for m in range(HD):
                last = nc.tensor.matmul(ps[:, 0, m:m + 1], bv_rep[:, m, :, :].rearrange("p h d -> p (h d)"), ones[0:1, 0:1], start=True, stop=True)
            last.then_inc(bias_ps, 1)
            nc.tensor.matmul(ps[:, 1, 0:D], ones[0:1, 0:P], rows[:, 1, :], start=True, stop=True).then_inc(bias_ps, 1)
            pe.wait_ge(bias_sb, 2)
            with pe.Fori(0, B) as b:
                pe.wait_ge(x_in, 16 * b + 16)
                pe.wait_ge(y_rdy, ONE + b)
                for t in range(NT):
                    last = nc.tensor.transpose(tr_ps[:, t * P:(t + 1) * P], xs[:, t, :], ident[:, :])
                last.then_inc(xT_ps, 1)
                pe.wait_ge(xT_sb, b + 1)
                for w, dst in ((wq, q_ps), (wk, k_ps)):
                    for s in range(0, T, HALF):
                        last = nc.tensor.matmul(dst[:, s:s + HALF], w[:, :], xT[:, s:s + HALF], start=True, stop=True)
                    last.then_inc(qk_ps, 1)

                def value_column(m):
                    if m >= 2:
                        pe.wait_ge(kv_rdy, b * HD + m - 1)
                    for s in range(0, T, HALF):
                        last = nc.tensor.matmul(vb_ps[m % 2][:, s:s + HALF], wv_rep[:, m, :, :].rearrange("p h d -> p (h d)"), xT[:, s:s + HALF], start=True, stop=True)
                    last.then_inc(v_ps, 1)

                value_column(0)
                value_column(1)
                pe.wait_ge(q_rdy, 2 * b + 2)
                for j in range(NJ):
                    pe.wait_ge(qs_rdy, b * NJ + j + 1)
                    dst, pick = (den_ps, HD) if j == 0 else (num_ps, j - 1)
                    for s in range(0, T, HALF):
                        last = nc.tensor.matmul(dst[:, s:s + HALF], sel[:, pick, :], qscan[:, j % 2, s:s + HALF], start=(j <= 1), stop=(j in (0, HD)))
                    last.then_inc(acc_ps, 1)
                    if j + 2 < HD:
                        value_column(j + 2)
                pe.wait_ge(vals_rdy, b + 1)
                for t in range(NT):
                    last = nc.tensor.matmul(o2_ps[:, t * P:(t + 1) * P], vals[:, t * P:(t + 1) * P], wo[:, :], start=True, stop=True)
                last.then_inc(o_ps, 1)

        @block.vector
        def _(dve):
            dve.sem_inc(y_rdy, ONE)
            dve.wait_ge(bias_ps, 1)
            nc.vector.tensor_copy(bv_col[:, :], ps[:, 0, 0:HD]).then_inc(bias_sb, 1)
            dve.wait_ge(bias_ps, 2)
            nc.vector.tensor_copy(bo_all[:, :], ps[:, 1, 0:D]).then_inc(bias_sb, 1)
            dve.wait_ge(bias_sb, 2)
            with dve.Fori(0, B) as b:
                st = Steps(dve, steps, b * V_STEPS)
                for j, (src, bias) in enumerate(((q_ps, bq), (k_ps, bk))):
                    dve.wait_ge(qk_ps, 2 * b + j + 1)
                    nc.vector.tensor_scalar(low[:, j, :], src, bias[:, 0:1], 0.0, ALU.add, ALU.min).then_inc(low_rdy, 1)
                    st.done(nc.vector.tensor_scalar(relu[:, j, :], src, bias[:, 0:1], 0.0, ALU.add, ALU.max))
                st.settle()
                for j, dst in enumerate((q, k)):
                    dve.wait_ge(exp_rdy, 2 * b + j + 1)
                    nc.vector.tensor_tensor(dst[:, :], relu[:, j, :], expo[:, j, :], ALU.add).then_inc(q_rdy, 1)
                dve.wait_ge(q_rdy, 2 * b + 2)
                for j in range(NJ):
                    if j >= 1:
                        dve.wait_ge(v_ps, b * HD + j)
                        nc.vector.scalar_tensor_tensor(kv[:, :], vb_ps[(j - 1) % 2], bv_col[:, j - 1:j], k[:, :], ALU.add, ALU.mult).then_inc(kv_rdy, 1)
                        dve.wait_ge(kv_rdy, b * HD + j)
                    if j >= 2:
                        dve.wait_ge(qs_rdy, b * NJ + j - 1)
                    nc.vector.tensor_tensor_scan(scan[:, j % 2, :], ones[:, :], (k if j == 0 else kv)[:, :], 0.0, ALU.mult, ALU.add).then_inc(scan_rdy, 1)
                    if j >= 1:
                        dve.wait_ge(scan_rdy, b * NJ + j + 1)
                    if j == 3:
                        dve.wait_ge(acc_ps, b * NJ + 1)
                        st.link(nc.vector.tensor_scalar(rden[:, :], den_ps, 1e-6, None, ALU.add))
                        st.link(nc.vector.reciprocal(rden[:, :], rden[:, :]))
                dve.wait_ge(acc_ps, b * NJ + NJ)
                nc.vector.tensor_tensor(vals[:, :], num_ps, rden[:, :], ALU.mult).then_inc(vals_rdy, 1)
                dve.wait_ge(o_ps, b + 1)
                dve.wait_ge(xb_rdy, b + 1)
                nc.vector.tensor_tensor(y[:, :, :].rearrange("p t c -> p (t c)"), o2_ps, xb[:, :, :].rearrange("p t c -> p (t c)"), ALU.add).then_inc(y_rdy, 1)
                dve.wait_ge(y_rdy, ONE + b + 1)
                layer_norm(nc, st, y, out[:, bass.ds(b * NT, NT), :], stats, mv, rs, tmp)
                st.settle()
                assert st.n == V_STEPS, st.n



def switch_attention(nc, x, out, ps, ident, I, redo, flag, tag):
    NH, E, DH, TOP = 8, 5, 64, 3
    ED = E * DH
    U = 3 * NT
    NG = 2 * NH
    HALVES = ((0, HALF), (HALF, T))
    with_max = redo is not None
    ctx = ExitStack()
    with ctx:
        sb = lambda name, shape, dt=F32: ctx.enter_context(nc.sbuf_tensor(tag + name, shape, dt))
        sems, sem = semaphores(nc, ctx, tag)
        w = sb("w", [P, 2, 2, 3, ED], F32R)
        wg = sb("wg", [P, NG * E])
        wo = sb("wo", [P, 3, D])
        ones = sb("ones", [P, P])
        xs, xT = sb("xs", [P, NT, D]), sb("xT", [P, T])
        xh, xl = sb("xh", [P, T], F32R), sb("xl", [P, T], F32R)
        gate = sb("gate", [P, NT, NG * E])
        beats = sb("beats", [P, NT * NG, E, E])
        mask = sb("mask", [P, NT * NG, E])
        picked = sb("picked", [P, B, NT, NH * E])
        gated = sb("gated", [P, 2, 3, ED])
        tok = sb("tok", [P, 2, NT, 3, DH])
        kk = sb("kk", [P, 2, T], F32R)
        qh, ql = sb("qh", [P, 2, T], F32R), sb("ql", [P, 2, T], F32R)
        vals = sb("vals", [P, 2, NT, DH])
        probs = sb("probs", [P, 4, T])
        psum = sb("psum", [P, 2, T])
        acc, sums = sb("acc", [P, HALF]), sb("sums", [P, 2 * P])
        o = sb("o", [P, NT, DH])
        share, z = sb("share", [P, NT, E, DH]), sb("z", [P, NT, E, DH])
        zT = sb("zT", [P, 3, P])
        y = sb("y", [P, NT, D])
        stats, mv, rs, tmp = sb("stats", [P, NT, 6]), sb("mv", [P, NT, 2]), sb("rs", [P, NT]), sb("tmp", [P, 2, NT])
        w_dram = nc.dram_tensor(tag + "w_split", [NH, P, 2 * 3 * ED], F32).ap()
        recips, ok, good, total = sb("recips", [P, B * NH * NT]), sb("ok", [P, B * NH * NT]), sb("good", [P, 1]), sb("total", [1, 1])
        judged = sem("judged")
        if with_max:
            mx, neg_max = sb("mx", [P, NT]), sb("neg_max", [1, T])
            max_ps, max_rdy, neg_ps, neg_rdy = map(sem, ("max_ps", "max", "neg_ps", "neg"))

        w_in, clear = sem("w_in"), sem("clear")
        raw_in = [sem("raw_in0"), sem("raw_in1")]
        w_high, w_low = sem("w_high"), sem("w_low")
        w_out = [sem("w_out0"), sem("w_out1")]
        w_rdy = [sem("w_rdy0"), sem("w_rdy1")]
        x_in, xT_ps, xT_sb, x_split, gate_ps, gate_exp, gate_rdy = map(sem, ("x_in", "xT_ps", "xT_sb", "x_split", "gate_ps", "gate_exp", "gate_rdy"))
        proj_ps, mult, tok_rdy = map(sem, ("proj_ps", "mult", "tok_rdy"))
        turn_ps, high_rdy, low_rdy, vals_rdy = map(sem, ("turn_ps", "high", "low", "vals_rdy"))
        score_ps, exp_rdy, pv_done, psum_rdy = map(sem, ("score_ps", "exp", "pv", "psum_rdy"))
        acc_sb, sum_ps, sum_sb, sumT_ps, recip_rdy, accT_ps, o_rdy = map(sem, ("acc_sb", "sum_ps", "sum_sb", "sumT_ps", "recip_rdy", "accT_ps", "o_rdy"))
        share_rdy, z_rdy, zT_ps, zT_sb, out_ps, y_rdy, steps = map(sem, ("share_rdy", "z_rdy", "zT_ps", "zT_sb", "out_ps", "y_rdy", "steps"))
        norm_steps = sem("norm_steps")

        proj_b = [ps[:, 0, :], ps[:, 1, :]]
        turn_b, acc_b = ps[:, 2, :], ps[:, 3, :]
        score_b = [ps[:, i:i + 2, :].rearrange("p a n -> p (a n)") for i in (4, 6)]
        MULT0, TOK0, VALS0, EXP0, PV0, PSUM0, SUM0 = 2, 2, 2, 2, 4, NT - 1, 2
        ACC0 = ACCT0 = SUMT0 = O0 = SHARE0 = Z0 = ZT0 = 1
        NORM_STEPS = LN_STEPS + 1
        GATE_STEPS = 2 + 2 * (E - 1) + 2 + 3
        raw_w = [probs[:, 2 * i, 0:3 * ED].rearrange("p (j n) -> p j n", j=3) for i in range(2)]

        def pairs(eng, b, body):
            body(b, 0)
            with eng.Fori(1, NH // 2 - 1) as hp:
                body(b, hp)
            body(b, NH // 2 - 1)

        def batches(eng, body):
            body(0, True, False)
            with eng.Fori(1, B - 1) as b:
                body(b, False, False)
            body(B - 1, False, True)

        def picked_of(b, h):
            return picked[:, bass.ds(b, 1), :, bass.ds(h * E, E)].rearrange("p b t e -> p (b t) e")

        def run_periods(eng, period):
            def batch(b, first, last):
                def pair(b, hp):
                    for par in range(2):
                        at0 = isinstance(hp, int) and hp == 0
                        at3 = isinstance(hp, int) and hp == NH // 2 - 1
                        period(b * NH + hp * 2 + par, b, par,
                               share=(b - 1, NH - 1) if at0 and par == 0 else (b, hp * 2 + par - 1),
                               ahead=par if at3 else hp * 2 + par + 2,
                               start=first and at0 and par == 0,
                               has_next=not (last and at3 and par == 1),
                               projecting=not (last and at3),
                               prep=at3 and par == 0 and not last,
                               project_out=at0 and par == 1 and not first,
                               first_head=at0 and par == 1)
                pairs(eng, b, pair)
            batches(eng, batch)

        ctx.callback(clear_semaphores, nc, sems)
        block = ctx.enter_context(nc.Block())

        @block.sync
        def _(sp):
            with only_if(sp, redo):
                sp.dma_start(xs[:, :, :], x[:, 0:NT, :]).then_inc(x_in, 16)
                sp.dma_start(wg[:, 0:NH * E], I["L0_ffn_Ws"]).then_inc(w_in, 16)
                sp.dma_start(wg[:, NH * E:], I["L0_ffn_Wd"]).then_inc(w_in, 16)
                for e in range(E):
                    at = DH * (e % 2)
                    sp.dma_start(wo[at:at + DH, e // 2, :], I["L0_ffn_Wo"][:, e * D:(e + 1) * D]).then_inc(w_in, 16)
                wq_h = I["L0_ffn_Wq"].rearrange("c (h n) -> h c n", h=NH)
                wkv_h = I["L0_ffn_Wkv"].rearrange("c (j h n) -> h c j n", j=2, h=NH)

                def raw(h):
                    if h >= 2:
                        sp.wait_ge(w_low, h - 1)
                    sp.dma_start(raw_w[h % 2][:, 0, :], wq_h[h]).then_inc(raw_in[h % 2], 16)
                    sp.dma_start(raw_w[h % 2][:, 1:3, :], wkv_h[h]).then_inc(raw_in[h % 2], 16)

                raw(0)
                raw(1)
                for h in range(NH):
                    sp.wait_ge(w_low, h + 1)
                    sp.dma_start(w_dram[h], w[:, h % 2, :, :, :].rearrange("p a j n -> p (a j n)").bitcast(F32)).then_inc(w_out[h % 2], 16)
                    if h + 2 < NH:
                        raw(h + 2)
                for par in range(2):
                    sp.wait_ge(w_out[par], 8 * NH)

                def weights(h, par):
                    sp.dma_start(w[:, par, :, :, :].rearrange("p a j n -> p (a j n)").bitcast(F32), w_dram[h]).then_inc(w_rdy[par], 16)

                weights(0, 0)
                weights(1, 1)

                def batch(b, first, last):
                    def pair(b, hp):
                        for par in range(2):
                            n = b * NH + hp * 2 + par
                            ahead = isinstance(hp, int) and hp == NH // 2 - 1
                            if ahead and last:
                                continue
                            if ahead and par == 0:
                                sp.wait_ge(xT_ps, 2 * (b + 1))
                                sp.dma_start(xs[:, :, :], x[:, bass.ds((b + 1) * NT, NT), :]).then_inc(x_in, 16)
                            sp.wait_ge(proj_ps, U * (n + 1))
                            h2 = par if ahead else hp * 2 + par + 2
                            weights(h2, par) if isinstance(h2, int) else \
                                sp.dma_start(w[:, par, :, :, :].rearrange("p a j n -> p (a j n)").bitcast(F32),
                                             w_dram[bass.ds(h2, 1), :, :].rearrange("h p n -> p (h n)")).then_inc(w_rdy[par], 16)
                    pairs(sp, b, pair)

                batches(sp, batch)

        @block.gpsimd
        def _(pool):
            with only_if(pool, redo):
                pool.sem_inc(psum_rdy, PSUM0)
                pool.sem_inc(share_rdy, SHARE0)
                nc.gpsimd.memset(ones[:, :], 1.0).then_inc(clear, 1)
                nc.gpsimd.memset(beats[:, :, :, :], 0.0).then_inc(clear, 1)

                def add_probs(n, par, i):
                    pool.wait_ge(exp_rdy, EXP0 + NT * n + i + 1)
                    if i == 1:
                        pool.wait_ge(sum_ps, SUM0 + n - 1)
                        prev = probs[:, 0, :]
                    else:
                        pool.wait_ge(psum_rdy, PSUM0 + (NT - 1) * n + i - 1)
                        prev = psum[:, par, :]
                    nc.gpsimd.tensor_tensor(psum[:, par, :], prev, probs[:, i % 4, :], ALU.add).then_inc(psum_rdy, 1)

                def gated_share(n, b, h):
                    pool.wait_ge(o_rdy, O0 + n + 1)
                    pool.wait_ge(z_rdy, Z0 + 2 * n)
                    nc.gpsimd.tensor_tensor(share[:, :, :, :], o[:, :, :].unsqueeze(2).broadcast_to([P, NT, E, DH]),
                                            picked_of(b, h).unsqueeze(3).broadcast_to([P, NT, E, DH]), ALU.mult).then_inc(share_rdy, 1)

                def period(n, b, par, share, ahead, start, has_next, projecting, prep, project_out, first_head):
                    for i in range(1, NT):
                        add_probs(n, par, i)
                        if i == 3 and not start:
                            gated_share(n - 1, *share)

                run_periods(pool, period)
                gated_share(B * NH - 1, B - 1, NH - 1)

        @block.scalar
        def _(act):
            with only_if(act, redo):
                nc.scalar.preload_act_table(ACT.Exp)
                act.sem_inc(exp_rdy, EXP0)
                act.sem_inc(vals_rdy, VALS0)
                act.sem_inc(acc_sb, ACC0)

                def prepare(b):
                    for r, (lo, hi) in enumerate(HALVES):
                        act.wait_ge(xT_ps, 2 * b + r + 1)
                        nc.scalar.copy(xT[:, lo:hi], turn_b).then_inc(xT_sb, 1)
                    for r in range(2):
                        act.wait_ge(gate_ps, 2 * b + r + 1)
                        act.wait_ge(tok_rdy, TOK0 + NT * NH * b)
                        nc.scalar.activation(gate[:, 4 * r:4 * r + 4, :], turn_b[:, 0:4 * NG * E].rearrange("p (t c) -> p t c", t=4), ACT.Exp, scale=-1.0).then_inc(gate_exp, 1)

                def high_part(n, par, r):
                    act.wait_ge(turn_ps, 4 * n + r + 1)
                    lo, hi = HALVES[r % 2]
                    nc.scalar.copy((kk if r < 2 else qh)[:, par, lo:hi], turn_b).then_inc(high_rdy, 1)

                def copy_values(n, par):
                    act.wait_ge(tok_rdy, TOK0 + NT * (n + 1))
                    nc.scalar.copy(vals[:, par, :, :], tok[:, par, :, 2, :]).then_inc(vals_rdy, 1)

                def copy_acc(n):
                    act.wait_ge(pv_done, PV0 + NT * (n + 1))
                    act.wait_ge(accT_ps, ACCT0 + n)
                    nc.scalar.copy(acc[:, :], acc_b).then_inc(acc_sb, 1)

                def copy_sums(n):
                    act.wait_ge(sum_ps, SUM0 + n + 1)
                    act.wait_ge(sumT_ps, SUMT0 + n)
                    nc.scalar.copy(sums[:, :], turn_b[:, 0:2 * P]).then_inc(sum_sb, 1)

                def copy_zT(b, t):
                    act.wait_ge(zT_ps, ZT0 + NT * b + t + 1)
                    nc.scalar.copy(zT[:, 0:2, :], proj_b[0][:, 0:2 * P].rearrange("p (k c) -> p k c", k=2)).then_inc(zT_sb, 1)
                    nc.scalar.copy(zT[0:DH, 2, :], proj_b[0][0:DH, 2 * P:3 * P]).then_inc(zT_sb, 1)

                def period(n, b, par, share, ahead, start, has_next, projecting, prep, project_out, first_head):
                    for i in range(NT):
                        if project_out and not with_max:
                            copy_zT(b - 1, i)
                        if i == 0 and prep:
                            prepare(b + 1)
                        if i == 1 and not start:
                            copy_sums(n - 1)
                        if 3 <= i < 7 and has_next:
                            high_part(n + 1, 1 - par, i - 3)
                        act.wait_ge(score_ps, NT * n + i + 1)
                        act.wait_ge(pv_done, PV0 + NT * n + i - 3)
                        act.wait_ge(psum_rdy, PSUM0 + (NT - 1) * n + (max(i - 4, 1) if i >= 4 else i - 3))
                        nc.scalar.activation(probs[:, i % 4, :], score_b[i % 2], ACT.Exp).then_inc(exp_rdy, 1)
                        if project_out and with_max:
                            copy_zT(b - 1, i)
                        if i == 0 and not start:
                            copy_acc(n - 1)
                        if i == 2 and has_next:
                            copy_values(n + 1, 1 - par)

                prepare(0)
                for r in range(4):
                    high_part(0, 0, r)
                copy_values(0, 0)
                run_periods(act, period)
                copy_acc(B * NH - 1)
                copy_sums(B * NH - 1)
                for t in range(NT):
                    copy_zT(B - 1, t)

        @block.tensor
        def _(pe):
            with only_if(pe, redo):
                pe.sem_inc(pv_done, PV0)
                pe.sem_inc(sum_ps, SUM0)
                pe.sem_inc(sumT_ps, SUMT0)
                pe.sem_inc(accT_ps, ACCT0)
                pe.sem_inc(zT_ps, ZT0)

                def prepare(b):
                    pe.wait_ge(x_in, 16 * (b + 1))
                    for r in range(2):
                        if r == 0:
                            turn_free(b)
                        else:
                            pe.wait_ge(xT_sb, 2 * b + 1)
                        for j in range(4):
                            last = nc.tensor.transpose(turn_b[:, j * P:(j + 1) * P], xs[:, 4 * r + j, :], ident[:, :])
                        last.then_inc(xT_ps, 1)
                    for r in range(2):
                        if r == 0:
                            pe.wait_ge(xT_sb, 2 * b + 2)
                        else:
                            pe.wait_ge(gate_exp, 2 * b + 1)
                        for j in range(4):
                            t = 4 * r + j
                            last = nc.tensor.matmul(turn_b[:, j * NG * E:(j + 1) * NG * E], xT[:, t * P:(t + 1) * P], wg[:, :], start=True, stop=True)
                        last.then_inc(gate_ps, 1)
                    pe.wait_ge(gate_exp, 2 * b + 2)
                    pe.wait_ge(x_split, 4 * b + 4)

                def turn_free(b):
                    if not (isinstance(b, int) and b == 0):
                        pe.wait_ge(low_rdy, 4 * (NH * b - 1))

                def project(n, par, t, js=(0, 1, 2)):
                    if t == 0 and 0 in js:
                        pe.wait_ge(w_rdy[par], half_count(n, par))
                    for j in js:
                        u = 3 * t + j
                        pe.wait_ge(mult, MULT0 + U * n + u - 1)
                        for i, (a, part) in enumerate(((xh, 0), (xl, 0), (xh, 1))):
                            last = nc.tensor.matmul(proj_b[u % 2][:, 0:ED], a[:, t * P:(t + 1) * P], w[:, par, part, j, :], start=(i == 0), stop=(i == 2))
                        last.then_inc(proj_ps, 1)

                def half_count(n, par):
                    return 8 * (n - par) + 16

                def turn(n, par, r):
                    lo_tile = 4 * (r % 2)
                    pe.wait_ge(tok_rdy, TOK0 + NT * n + lo_tile + 4)
                    if r:
                        pe.wait_ge(low_rdy, 4 * n + r)
                    else:
                        pe.wait_ge(o_rdy, O0 + n - 1 if not (isinstance(n, int) and n == 0) else O0)
                    for j in range(4):
                        src = tok[:, par, lo_tile + j, 1 if r < 2 else 0, :]
                        for copy in range(2):
                            last = nc.tensor.matmul(turn_b[copy * DH:(copy + 1) * DH, j * P:(j + 1) * P], src, ident[:, :], start=True, stop=True)
                    last.then_inc(turn_ps, 1)

                def scores(n, par, i):
                    if i == 0:
                        pe.wait_ge(low_rdy, 4 * n + 4)
                        if with_max:
                            query_max(n, par)
                    pe.wait_ge(exp_rdy, EXP0 + NT * n + i - 1)
                    for lo, hi in HALVES:
                        last = nc.tensor.matmul(score_b[i % 2][:, lo:hi], kk[:, par, i * P:(i + 1) * P], qh[:, par, lo:hi], start=True, stop=False)
                        last = nc.tensor.matmul(score_b[i % 2][:, lo:hi], kk[:, par, i * P:(i + 1) * P], ql[:, par, lo:hi], start=False, stop=not with_max)
                        if with_max:
                            last = nc.tensor.matmul(score_b[i % 2][:, lo:hi], ones[0:1, :], neg_max[:, lo:hi], start=False, stop=True)
                    last.then_inc(score_ps, 1)

                def query_max(n, par):
                    pe.wait_ge(exp_rdy, EXP0 + NT * n)
                    for qt in range(NT):
                        if qt >= 2:
                            pe.wait_ge(max_rdy, NT * n + qt - 1)
                        for lo, hi in HALVES:
                            nc.tensor.matmul(score_b[qt % 2][:, lo:hi], qh[:, par, qt * P:(qt + 1) * P], kk[:, par, lo:hi], start=True, stop=False)
                            last = nc.tensor.matmul(score_b[qt % 2][:, lo:hi], ql[:, par, qt * P:(qt + 1) * P], kk[:, par, lo:hi], start=False, stop=True)
                        last.then_inc(max_ps, 1)
                    pe.wait_ge(max_rdy, NT * (n + 1))
                    for half in range(2):
                        if half:
                            pe.wait_ge(neg_rdy, 2 * n + 1)
                        for j in range(4):
                            last = nc.tensor.matmul(turn_b[0:1, j * P:(j + 1) * P], mx[:, 4 * half + j:4 * half + j + 1], ident[:, :], start=True, stop=True)
                        last.then_inc(neg_ps, 1)
                    pe.wait_ge(neg_rdy, 2 * n + 2)

                def products(n, par, i):
                    pe.wait_ge(exp_rdy, EXP0 + NT * n + i + 1)
                    if i == 0:
                        pe.wait_ge(acc_sb, ACC0 + n)
                        pe.wait_ge(vals_rdy, VALS0 + n + 1)
                    for half, (lo, hi) in enumerate(HALVES):
                        last = nc.tensor.matmul(acc_b[DH * half:DH * half + DH, :], vals[:, par, i, :], probs[:, i % 4, lo:hi], start=(i == 0), stop=(i == NT - 1))
                    last.then_inc(pv_done, 1)

                def sum_probs(n, par):
                    pe.wait_ge(psum_rdy, PSUM0 + (NT - 1) * (n + 1))
                    for j in range(4):
                        last = nc.tensor.matmul(turn_b[32 * j:32 * j + 32, 0:2 * P], ones[:, 0:32], psum[:, par, j * 2 * P:(j + 1) * 2 * P], start=True, stop=True)
                    last.then_inc(sum_ps, 1)

                def turn_sums(n):
                    pe.wait_ge(sum_sb, n + 1)
                    for j in range(2):
                        last = nc.tensor.transpose(turn_b[:, j * P:(j + 1) * P], sums[:, j * P:(j + 1) * P], ident[:, :])
                    last.then_inc(sumT_ps, 1)

                def turn_acc(n):
                    pe.wait_ge(recip_rdy, n + 1)
                    pe.wait_ge(acc_sb, ACC0 + n + 1)
                    for j in range(4):
                        last = nc.tensor.transpose(turn_b[:, j * P:(j + 1) * P], acc[:, j * P:(j + 1) * P], ident[:, :])
                    last.then_inc(accT_ps, 1)

                def turn_z(b, t, units):
                    pe.wait_ge(mult, MULT0 + units)
                    pe.wait_ge(z_rdy, Z0 + 2 * NH * (b + 1))
                    if t:
                        pe.wait_ge(zT_sb, 2 * (NT * b + t))
                    flat = z[:, t, :, :].rearrange("p e d -> p (e d)")
                    for k in range(3):
                        n_rows = min(P, ED - k * P)
                        last = nc.tensor.transpose(proj_b[0][0:n_rows, k * P:(k + 1) * P], flat[:, k * P:k * P + n_rows], ident[:, :])
                    last.then_inc(zT_ps, 1)

                def project_z(b, t):
                    pe.wait_ge(zT_sb, 2 * (NT * b + t + 1))
                    for k in range(3):
                        n_rows = min(P, ED - k * P)
                        last = nc.tensor.matmul(proj_b[1][:, 0:D], zT[0:n_rows, k, :], wo[0:n_rows, k, :], start=(k == 0), stop=(k == 2))
                    last.then_inc(out_ps, 1)

                def period(n, b, par, share, ahead, start, has_next, projecting, prep, project_out, first_head):
                    for i in range(NT):
                        js = ((), (), (0, 1, 2)) if project_out else ((0,), (1,), (2,))
                        if project_out:
                            turn_z(b - 1, i, U * (n + 2) + 3 * i)
                        if prep and i == 0:
                            prepare(b + 1)
                        if projecting:
                            project(n + 2, par, i, js[0])
                        if not start and i == 1:
                            sum_probs(n - 1, 1 - par)
                        if not start and i == 2:
                            turn_acc(n - 1)
                        if 3 <= i < 7 and has_next:
                            turn(n + 1, 1 - par, i - 3)
                        scores(n, par, i)
                        if projecting:
                            project(n + 2, par, i, js[1])
                        if not start and i == 1:
                            turn_sums(n - 1)
                        if i or not start:
                            products(*((n, par, i - 1) if i else (n - 1, 1 - par, NT - 1)))
                        if project_out:
                            project_z(b - 1, i)
                            pe.wait_ge(y_rdy, NT * (b - 1) + i + 1)
                        if projecting:
                            project(n + 2, par, i, js[2])

                pe.wait_ge(w_in, 16 * (2 + E))
                pe.wait_ge(clear, 2)
                prepare(0)
                for n in range(2):
                    for t in range(NT):
                        project(n, n, t)
                for r in range(4):
                    turn(0, 0, r)
                run_periods(pe, period)
                last_n = B * NH - 1
                products(last_n, last_n % 2, NT - 1)
                sum_probs(last_n, last_n % 2)
                turn_sums(last_n)
                turn_acc(last_n)
                for t in range(NT):
                    turn_z(B - 1, t, U * B * NH)
                    project_z(B - 1, t)
                    pe.wait_ge(y_rdy, NT * (B - 1) + t + 1)
                if not with_max:
                    turn_counts(nc, pe, judged, good, ident, turn_b[0:1, 0:P])

        @block.vector
        def _(dve):
            with only_if(dve, redo):
                dve.sem_inc(mult, MULT0)
                dve.sem_inc(tok_rdy, TOK0)
                dve.sem_inc(o_rdy, O0)
                dve.sem_inc(z_rdy, Z0)
                dve.sem_inc(norm_steps, ONE)
                for h in range(NH):
                    par = h % 2
                    dve.wait_ge(raw_in[par], 32 * (h // 2 + 1))
                    if h >= 2:
                        dve.wait_ge(w_out[par], 16 * (h // 2))
                    nc.vector.tensor_copy(w[:, par, 0, :, :], raw_w[par]).then_inc(w_high, 1)
                    dve.wait_ge(w_high, h + 1)
                    nc.vector.tensor_tensor(w[:, par, 1, :, :], raw_w[par], w[:, par, 0, :, :].bitcast(F32), ALU.subtract).then_inc(w_low, 1)
                dve.wait_ge(w_low, NH)

                def prepare(b):
                    st = Steps(dve, steps, GATE_STEPS * b)
                    for r, (lo, hi) in enumerate(HALVES):
                        dve.wait_ge(xT_sb, 2 * b + r + 1)
                        nc.vector.tensor_copy(xh[:, lo:hi], xT[:, lo:hi]).then_inc(x_split, 1)
                        dve.wait_ge(x_split, 4 * b + 2 * r + 1)
                        nc.vector.tensor_tensor(xl[:, lo:hi], xT[:, lo:hi], xh[:, lo:hi].bitcast(F32), ALU.subtract).then_inc(x_split, 1)
                    dve.wait_ge(gate_exp, 2 * b + 2)
                    st.link(nc.vector.tensor_scalar(gate[:, :, :], gate[:, :, :], 1.0, None, ALU.add))
                    st.link(nc.vector.reciprocal(gate[:, :, :], gate[:, :, :]))
                    g = gate[:, :, :].rearrange("p t (g e) -> p (t g) e", e=E)
                    for e in range(E):
                        for lo, hi, op in ((0, e, ALU.is_ge), (e + 1, E, ALU.is_gt)):
                            if lo < hi:
                                st.done(nc.vector.tensor_tensor(beats[:, :, e, lo:hi], g[:, :, lo:hi], g[:, :, e:e + 1].broadcast_to([P, NT * NG, hi - lo]), op))
                    st.settle()
                    st.link(nc.vector.reduce_sum(mask[:, :, :], beats[:, :, :, :], AX.X))
                    st.link(nc.vector.tensor_scalar(mask[:, :, :], mask[:, :, :], float(TOP), None, ALU.is_lt))
                    m = mask[:, :, :].rearrange("p (t s g) e -> p t s (g e)", t=NT, s=2)
                    st.done(nc.vector.tensor_copy(picked[:, bass.ds(b, 1), :, :].rearrange("p b t c -> p (b t) c"), m[:, :, 1, :]))
                    gs, gd = gate[:, :, 0:NH * E], gate[:, :, NH * E:]
                    st.done(nc.vector.tensor_tensor(gs, gs, m[:, :, 0, :], ALU.mult))
                    st.done(nc.vector.scalar_tensor_tensor(gd, gd, float(DH) ** -0.5, m[:, :, 1, :], ALU.mult, ALU.mult))
                    st.settle()
                    assert st.n == GATE_STEPS, st.n

                def gate_part(n, par, h, t, j):
                    if j == 0:
                        dve.wait_ge(tok_rdy, TOK0 + NT * n + t - 1)
                    u = 3 * t + j
                    dve.wait_ge(proj_ps, U * n + u + 1)
                    g = gate[:, t, bass.ds(h * E + (NH * E if j == 0 else 0), E)]
                    nc.vector.tensor_tensor(gated[:, t % 2, j, :].rearrange("p (e d) -> p e d", e=E), proj_b[u % 2][:, 0:ED].rearrange("p (e d) -> p e d", e=E),
                                            g.unsqueeze(2).broadcast_to([P, E, DH]), ALU.mult).then_inc(mult, 1)

                def sum_experts(n, par, t):
                    dve.wait_ge(mult, MULT0 + U * n + 3 * t + 3)
                    if t == 0:
                        dve.wait_ge(vals_rdy, VALS0 + n - 1)
                    nc.vector.tensor_reduce(tok[:, par, t, :, :], gated[:, t % 2, :, :].rearrange("p j (e d) -> p j d e", e=E), AX.X, ALU.add).then_inc(tok_rdy, 1)

                def low_part(n, par, r):
                    dve.wait_ge(high_rdy, 4 * n + r + 1)
                    lo, hi = HALVES[r % 2]
                    if r < 2:
                        nc.vector.tensor_tensor(kk[DH:P, par, lo:hi], turn_b[DH:P, :], kk[DH:P, par, lo:hi].bitcast(F32), ALU.subtract).then_inc(low_rdy, 1)
                    else:
                        nc.vector.tensor_tensor(ql[:, par, lo:hi], turn_b, qh[:, par, lo:hi].bitcast(F32), ALU.subtract).then_inc(low_rdy, 1)

                def reciprocals(n):
                    dve.wait_ge(sumT_ps, SUMT0 + n + 1)
                    nc.vector.reciprocal(recips[:, bass.ds(n * NT, NT)].rearrange("p (j m) -> p j m", j=4), turn_b[:, 0:2 * P].rearrange("p (m j c) -> p j m c", m=2, j=4)[:, :, :, 0]).then_inc(recip_rdy, 1)

                def normalize(n):
                    dve.wait_ge(accT_ps, ACCT0 + n + 1)
                    dve.wait_ge(recip_rdy, n + 1)
                    dve.wait_ge(share_rdy, SHARE0 + n)
                    nc.vector.tensor_tensor(o[:, :, :].rearrange("p (f j) d -> p f j d", f=2), turn_b.rearrange("p (j f d) -> p f j d", j=4, f=2),
                                            recips[:, bass.ds(n * NT, NT)].rearrange("p (f j) -> p f j", f=2).unsqueeze(3).broadcast_to([P, 2, 4, DH]), ALU.mult).then_inc(o_rdy, 1)

                def add_share(n, b, first_head, half):
                    dve.wait_ge(share_rdy, SHARE0 + n + 1)
                    dve.wait_ge(z_rdy, Z0 + 2 * n)
                    zf, sf = (a[:, half * (NT // 2):(half + 1) * (NT // 2), :, :].rearrange("p t e d -> p (t e d)") for a in (z, share))
                    if first_head:
                        dve.wait_ge(zT_ps, ZT0 + NT * b)
                        nc.vector.tensor_copy(zf, sf).then_inc(z_rdy, 1)
                    else:
                        nc.vector.tensor_tensor(zf, zf, sf, ALU.add).then_inc(z_rdy, 1)

                def residual(b, t):
                    dve.wait_ge(out_ps, NT * b + t + 1)
                    nc.vector.tensor_tensor(y[:, t, :], proj_b[1][:, 0:D], x[:, bass.ds(b * NT + t, 1), :].rearrange("p t c -> p (t c)"), ALU.add).then_inc(y_rdy, 1)

                def norm(b):
                    dve.wait_ge(y_rdy, NT * (b + 1))
                    st = Steps(dve, norm_steps, ONE + NORM_STEPS * b)
                    layer_norm(nc, st, y, out[:, bass.ds(b * NT, NT), :], stats, mv, rs, tmp)
                    st.settle_apart()
                    assert st.n == NORM_STEPS

                def max_rows(n):
                    for qt in range(NT):
                        dve.wait_ge(max_ps, NT * n + qt + 1)
                        nc.vector.reduce_max(mx[:, qt:qt + 1], score_b[qt % 2], AX.X).then_inc(max_rdy, 1)
                    for half, (lo, hi) in enumerate(HALVES):
                        dve.wait_ge(neg_ps, 2 * n + half + 1)
                        nc.vector.tensor_scalar(neg_max[:, lo:hi], turn_b[0:1, :], -1.0, None, ALU.mult).then_inc(neg_rdy, 1)

                def period(n, b, par, share, ahead, start, has_next, projecting, prep, project_out, first_head):
                    if prep:
                        prepare(b + 1)
                    if with_max:
                        max_rows(n)
                    def between(i):
                        if not start and i == 1:
                            reciprocals(n - 1)
                        if not start and i == 2:
                            normalize(n - 1)
                        if 3 <= i < 7 and has_next:
                            low_part(n + 1, 1 - par, i - 3)

                    for i in range(NT):
                        if project_out:
                            residual(b - 1, i)
                        if not projecting or project_out:
                            between(i)
                        if projecting:
                            for j in range(3):
                                gate_part(n + 2, par, ahead, i, j)
                                if j == (0 if i == 2 else 1) and not project_out:
                                    between(i)
                            sum_experts(n + 2, par, i)
                        if not start and i in (5, 7) and not project_out:
                            add_share(n - 1, b, first_head, int(i == 7))
                    if project_out:
                        for half in range(2):
                            add_share(n - 1, b, True, half)
                        norm(b - 1)

                dve.wait_ge(clear, 2)
                prepare(0)
                for n in range(2):
                    for t in range(NT):
                        for j in range(3):
                            gate_part(n, n, n, t, j)
                        sum_experts(n, n, t)
                for r in range(4):
                    low_part(0, 0, r)
                run_periods(dve, period)
                last_n = B * NH - 1
                reciprocals(last_n)
                normalize(last_n)
                for half in range(2):
                    add_share(last_n, B - 1, False, half)
                for t in range(NT):
                    residual(B - 1, t)
                norm(B - 1)
                if not with_max:
                    count_safe(nc, dve, judged, recips, ok, good)
                    raise_flag(nc, dve, judged, turn_b[0:1, 0:P], total, P * B * NH * NT, flag)


def rotary_attention(nc, x, out, ps, ident, I, redo, flag, tag):
    G = 4
    NG = H // G
    STEPS = G // 2 * NT
    BS = NG * STEPS
    NP = H // 2
    Z_PIECES = [(kind, half) for half in range(2) for kind in ("turn_out", "project_out")]
    X_PIECES = ([("turn_x", 0), ("turn_x", 1)] + [(kind, half) for kinds in (("q", "q_sw"), ("k", "k_sw")) for half in range(2) for kind in kinds]
                + [("v", 0), ("v", 1)])
    NZ, NX = len(Z_PIECES), len(X_PIECES)
    TURN = 4
    Z_AT, NORM_AT, X_AT = 5, 9, 14
    with_max = redo is not None
    ctx = ExitStack()
    with ctx:
        sb = lambda name, shape, dt=F32: ctx.enter_context(nc.sbuf_tensor(tag + name, shape, dt))
        sems, sem = semaphores(nc, ctx, tag)
        wq, wk, wv, wo, wq_sw, wk_sw = (sb(n, [P, D]) for n in ("wq", "wk", "wv", "wo", "wq_sw", "wk_sw"))
        rows = sb("rows", [1, 6, D])
        b_col = sb("b_col", [P, 4])
        b_all = sb("b_all", [P, 2, D])
        cos, sin = sb("cos", [P, T]), sb("sin", [P, T])
        ones = sb("ones", [1, P])
        xs, xT, xb = sb("xs", [P, NT, D]), sb("xT", [P, T]), sb("xb", [P, NT, D])
        rot, part = sb("rot", [P, HALF]), sb("part", [P, HALF])
        split = sb("split", [P, 4, T], F32R)
        keys = sb("keys", [P, 2, T], F32R)
        qpad = sb("qpad", [P, 2, G, T], F32R)
        v = sb("v", [P, B * NT, D])
        vg = sb("vg", [P, 2, NT, G, 32])
        probs = sb("probs", [P, 2, 2, T])
        acc = sb("acc", [P, 2, HALF])
        ao, aoT = sb("ao", [P, NT, D]), sb("aoT", [P, T])
        y = sb("y", [P, NT, D])
        stats, mv, rs, tmp = sb("stats", [P, NT, 6]), sb("mv", [P, NT, 2]), sb("rs", [P, NT]), sb("tmp", [P, 2, NT])
        recips, ok, good, total = sb("recips", [P, B * H * NT]), sb("ok", [P, B * H * NT]), sb("good", [P, 1]), sb("total", [1, 1])
        judged, mark = sem("judged"), sem("mark")
        if with_max:
            mx, neg_max = sb("mx", [P, 2, NT]), sb("neg_max", [1, 2, T])
            max_ps, max_rdy, neg_ps, neg_rdy = map(sem, ("max_ps", "max", "neg_ps", "neg"))

        w_in, swapped, clear, bias_ps, bias_sb = map(sem, ("w_in", "swapped", "clear", "bias_ps", "bias_sb"))
        x_in, filled, used, rope_steps = map(sem, ("x_in", "filled", "used", "rope_steps"))
        xb_rdy, vg_rdy, laid_out = map(sem, ("xb_rdy", "vg_rdy", "laid_out"))
        staged = [sem("staged0"), sem("staged1")]
        score_ps, exp_rdy, pv_done, acc_sb, accT_ps, recip_rdy, ao_rdy, norm_steps = map(sem, ("score_ps", "exp", "pv", "acc_sb", "accT_ps", "recip_rdy", "ao_rdy", "norm_steps"))
        score_b = [ps[:, i:i + 2, :].rearrange("p a n -> p (a n)") for i in (0, 2)]
        acc_b = [ps[:, 4, :], ps[:, 5, :]]
        accT_b, piece_b = ps[:, 6, :], ps[:, 7, :]
        W_IN = 16 * 10
        SC, VC = 2 * STEPS, STEPS
        NORM_STEPS = LN_STEPS + 1
        ROPE_STEPS = 2 * 2 * 5
        DMAS = 1 + G
        heads_dram = nc.dram_tensor(tag + "heads", [B, 2, H, 4, HD, T], F32).ap()

        def z_index(b, k):
            return NX + (NZ + NX) * b + k

        def x_index(xb_no, k):
            return k if isinstance(xb_no, int) and xb_no == 0 else z_index(xb_no - 1, NZ + k)

        def pieces(b, first, last):
            at = {}
            if not first:
                at.update({Z_AT + k: (z_index(b, k), kind, half, b - 1) for k, (kind, half) in enumerate(Z_PIECES)})
            if not last:
                at.update({X_AT + k: (x_index(b + 1, k), kind, half, b + 1) for k, (kind, half) in enumerate(X_PIECES)})
            return at

        def batches(eng, body):
            body(0, True, False)
            with eng.Fori(1, B - 1) as b:
                body(b, False, False)
            body(B - 1, False, True)

        ctx.callback(clear_semaphores, nc, sems)
        block = ctx.enter_context(nc.Block())

        @block.sync
        def _(sp):
            with only_if(sp, redo):
                sp.sem_inc(laid_out, ONE)
                sp.dma_start(xs[:, :, :], x[:, 0:NT, :]).then_inc(x_in, 16)
                for dst, src in ((wq, "L1_attn_Wq"), (wk, "L1_attn_Wk"), (wv, "L1_attn_Wv"), (wo, "L1_attn_Wo"), (cos, "cos"), (sin, "sin")):
                    sp.dma_start(dst[:, :], I[src]).then_inc(w_in, 16)
                for j, src in enumerate(("L1_attn_bq", "L1_attn_bk", "L1_attn_bv", "L1_attn_bo")):
                    sp.dma_start(rows[:, j, :], I[src].rearrange("(o n) -> o n", o=1)).then_inc(w_in, 16)
                sp.wait_ge(clear, 4)

                def lay_out(b):
                    for j in range(2):
                        sp.wait_ge(rope_steps, ROPE_STEPS * b + ROPE_STEPS // 2 * (j + 1))
                        for lo in range(2):
                            for c in ((2 * lo, 2 * lo + 1) if j == 0 else (lo, lo + 2)):
                                sp.dma_start(heads_dram[bass.ds(b, 1), j, :, c, :, :].rearrange("b h d t -> (b h) d t"), split[:, 2 * j + lo, :].bitcast(F32)).then_inc(laid_out, 16)

                def stage(b, g):
                    par = g % 2
                    sp.wait_ge(score_ps, ONE + SC * (b * NG + g))
                    sp.dma_start(keys[:, par, :].bitcast(F32), heads_dram[bass.ds(b, 1), 1, g * G:g * G + G, :, :, :].rearrange("b h c d t -> (b h c d) t")).then_inc(staged[par], 16)
                    for hh in range(G):
                        sp.dma_start(qpad[32 * hh:32 * hh + 32, par, hh, :].bitcast(F32), heads_dram[bass.ds(b, 1), 0, g * G + hh:g * G + hh + 1, :, :, :].rearrange("b h c d t -> (b h c d) t")).then_inc(staged[par], 16)

                lay_out(0)

                def batch(b, first, last):
                    sp.wait_ge(laid_out, ONE + 16 * 8 * (b + 1))
                    stage(b, 0)
                    stage(b, 1)
                    if not last:
                        sp.wait_ge(filled, x_index(b, 1) + 1)
                        sp.dma_start(xs[:, :, :], x[:, bass.ds((b + 1) * NT, NT), :]).then_inc(x_in, 16)
                        lay_out(b + 1)
                    stage(b, 2)
                    stage(b, 3)

                batches(sp, batch)

        @block.gpsimd
        def _(pool):
            with only_if(pool, redo):
                pool.sem_inc(vg_rdy, ONE)
                nc.gpsimd.memset(qpad[:, :, :, :].bitcast(F32), 0.0).then_inc(clear, 1)
                nc.gpsimd.memset(vg[:, :, :, :, :], 0.0).then_inc(clear, 1)
                nc.gpsimd.memset(ones[:, :], 1.0).then_inc(clear, 1)
                pool.wait_ge(clear, 3)
                nc.gpsimd.memset(vg[:, :, :, :, HD:HD + 1], 1.0).then_inc(clear, 1)
                pool.wait_ge(w_in, W_IN)
                for src, dst in ((wq[:, :], wq_sw[:, :]), (wk[:, :], wk_sw[:, :]), (rows[:, 0, :], rows[:, 4, :]), (rows[:, 1, :], rows[:, 5, :])):
                    s2, d2 = src.rearrange("p (n two) -> p n two", two=2), dst.rearrange("p (n two) -> p n two", two=2)
                    nc.gpsimd.tensor_copy(d2[:, :, 0], s2[:, :, 1]).then_inc(swapped, 1)
                    nc.gpsimd.tensor_copy(d2[:, :, 1], s2[:, :, 0]).then_inc(swapped, 1)
                pool.wait_ge(bias_sb, 3)
                pool.wait_ge(clear, 4)

                def residual(b):
                    pool.wait_ge(used, z_index(b, NZ))
                    nc.gpsimd.tensor_tensor(xb[:, :, :], x[:, bass.ds(b * NT, NT), :], b_all[:, 1, :].unsqueeze(1).broadcast_to([P, NT, D]), ALU.add).then_inc(xb_rdy, 1)

                def batch(b, first, last):
                    pool.wait_ge(used, z_index(b, 0))
                    for g in range(NG):
                        pool.wait_ge(pv_done, ONE + VC * (b * NG + g))
                        for hh in range(G):
                            at = (g * G + hh) * HD
                            nc.gpsimd.tensor_copy(vg[:, g % 2, :, hh, 0:HD], v[:, bass.ds(b * NT, NT), at:at + HD]).then_inc(vg_rdy, 1)
                        if g == 2:
                            residual(b)

                batches(pool, batch)

        @block.scalar
        def _(act):
            with only_if(act, redo):
                act.sem_inc(exp_rdy, ONE)
                nc.scalar.preload_act_table(ACT.Exp)
                with act.Fori(0, B * NP) as pair:
                    for kt in range(NT):
                        step = pair * NT + kt
                        act.wait_ge(pv_done, ONE + VC - 1 + step)
                        for s in range(2):
                            act.wait_ge(score_ps, ONE + SC + 2 * step + s + 1)
                            nc.scalar.activation(probs[:, kt % 2, s, :], score_b[s], ACT.Exp, scale=float(HD) ** -0.5).then_inc(exp_rdy, 1)

        @block.tensor
        def _(pe):
            with only_if(pe, redo):
                pe.sem_inc(score_ps, ONE + SC)
                pe.sem_inc(pv_done, ONE + VC)
                pe.wait_ge(w_in, W_IN)
                pe.wait_ge(clear, 4)
                pe.wait_ge(swapped, 8)
                for j, src in enumerate((0, 1, 4, 5)):
                    last = nc.tensor.matmul(ps[:, 0, j:j + 1], rows[:, src, :], ones[0:1, 0:1], start=True, stop=True)
                last.then_inc(bias_ps, 1)
                for j in range(2):
                    nc.tensor.matmul(ps[:, 1 + j, 0:D], ones[0:1, 0:P], rows[:, 2 + j, :], start=True, stop=True).then_inc(bias_ps, 1)
                pe.wait_ge(bias_sb, 3)

                def piece(index, kind, half, b):
                    if not (isinstance(index, int) and index == 0):
                        pe.wait_ge(used, index)
                    c = half * HALF
                    if kind == "turn_x" and half == 0:
                        pe.wait_ge(x_in, 16 * (b + 1))
                    if kind == "turn_out" and half == 0:
                        pe.wait_ge(ao_rdy, ONE + 2 * NP * (b + 1))
                    if kind in ("q", "q_sw", "k", "k_sw"):
                        w = {"q": wq, "q_sw": wq_sw, "k": wk, "k_sw": wk_sw}[kind]
                        last = nc.tensor.matmul(piece_b, w[:, :], xT[:, c:c + HALF], start=True, stop=True)
                    for j in range(4):
                        t, cols = 4 * half + j, piece_b[:, j * P:(j + 1) * P]
                        if kind == "turn_x":
                            last = nc.tensor.transpose(cols, xs[:, t, :], ident[:, :])
                        elif kind == "turn_out":
                            last = nc.tensor.transpose(cols, ao[:, t, :], ident[:, :])
                        elif kind == "v":
                            last = nc.tensor.matmul(cols, xT[:, t * P:(t + 1) * P], wv[:, :], start=True, stop=True)
                        elif kind == "project_out":
                            last = nc.tensor.matmul(cols, aoT[:, t * P:(t + 1) * P], wo[:, :], start=True, stop=True)
                    last.then_inc(filled, 1)

                def query_max(par, hh, s, pair_no):
                    head = 2 * pair_no + s
                    for qt in range(NT):
                        if qt >= 2:
                            pe.wait_ge(max_rdy, NT * head + qt - 1)
                        for c in range(0, T, HALF):
                            last = nc.tensor.matmul(score_b[qt % 2][:, c:c + HALF], qpad[:, par, hh, qt * P:(qt + 1) * P], keys[:, par, c:c + HALF], start=True, stop=True)
                        last.then_inc(max_ps, 1)
                    pe.wait_ge(max_rdy, NT * head + NT)
                    for half in range(2):
                        if half:
                            pe.wait_ge(neg_rdy, 2 * head + 1)
                        for j in range(NT // 2):
                            qt = half * (NT // 2) + j
                            last = nc.tensor.matmul(piece_b[0:1, j * P:(j + 1) * P], mx[:, s, qt:qt + 1], ident[:, :], start=True, stop=True)
                        last.then_inc(neg_ps, 1)
                    pe.wait_ge(neg_rdy, 2 * head + 2)

                def scores(b, i, first, pieces_before):
                    g, pp, kt = i // STEPS, i // NT % (G // 2), i % NT
                    par, step = g % 2, b * BS + i
                    if i % STEPS == 0:
                        pe.wait_ge(staged[par], 16 * DMAS * (b * (NG // 2) + g // 2 + 1))
                        pe.wait_ge(vg_rdy, ONE + G * (b * NG + g + 1))
                    if with_max and kt == 0:
                        pe.wait_ge(exp_rdy, ONE + 2 * step)
                        pe.wait_ge(used, z_index(b, 0) + pieces_before)
                        for s in range(2):
                            query_max(par, 2 * pp + s, s, b * NP + i // NT)
                    for s in range(2):
                        hh = 2 * pp + s
                        if not (first and i == 0):
                            pe.wait_ge(exp_rdy, ONE + 2 * step + s - 1)
                        for c in range(0, T, HALF):
                            last = nc.tensor.matmul(score_b[s][:, c:c + HALF], keys[:, par, kt * P:(kt + 1) * P], qpad[:, par, hh, c:c + HALF], start=True, stop=not with_max)
                            if with_max:
                                last = nc.tensor.matmul(score_b[s][:, c:c + HALF], ones[0:1, :], neg_max[:, s, c:c + HALF], start=False, stop=True)
                        last.then_inc(score_ps, 1)

                def products(b, i):
                    par, pp, kt, pair = i // STEPS % 2, i // NT % (G // 2), i % NT, i // NT
                    pe.wait_ge(exp_rdy, ONE + 2 * (b * BS + i) + 2)
                    if kt == 0:
                        pe.wait_ge(acc_sb, ONE + b * NP + max(pair - 1, 0 if isinstance(b, int) and b == 0 else -1))
                    for s in range(2):
                        for half in range(2):
                            at = 64 * s + 32 * half
                            last = nc.tensor.matmul(acc_b[pair % 2][at:at + 32, :], vg[:, par, kt, 2 * pp + s, :], probs[:, kt % 2, s, half * HALF:(half + 1) * HALF],
                                                    start=(kt == 0), stop=(kt == NT - 1))
                    last.then_inc(pv_done, 1)

                def turn(b, pair):
                    n = b * NP + pair
                    pe.wait_ge(acc_sb, ONE + n + 1)
                    pe.wait_ge(ao_rdy, ONE + 2 * n)
                    for j in range(4):
                        last = nc.tensor.transpose(accT_b[:, j * P:(j + 1) * P], acc[:, pair % 2, j * P:(j + 1) * P], ident[:, :])
                    last.then_inc(accT_ps, 1)

                for k, (kind, half) in enumerate(X_PIECES):
                    piece(k, kind, half, 0)
                pe.wait_ge(used, NX)
                pe.sem_inc(filled, NZ)

                def batch(b, first, last):
                    at = pieces(b, first, last)
                    for i in range(BS):
                        scores(b, i, first, (NZ if first else 0) + sum(j < i for j in at))
                        if i:
                            products(b, i - 1)
                        elif not first:
                            products(b - 1, BS - 1)
                        if i % NT == TURN and not (first and i == TURN):
                            turn(*((b, i // NT - 1) if i > TURN else (b - 1, NP - 1)))
                        if i in at:
                            piece(*at[i])

                batches(pe, batch)
                products(B - 1, BS - 1)
                turn(B - 1, NP - 1)
                for k, (kind, half) in enumerate(Z_PIECES):
                    piece(z_index(B, k) - NX, kind, half, B - 1)
                if not with_max:
                    turn_counts(nc, pe, judged, good, ident, accT_b[0:1, 0:P])

        @block.vector
        def _(dve):
            with only_if(dve, redo):
                dve.sem_inc(acc_sb, ONE)
                dve.sem_inc(ao_rdy, ONE)
                dve.sem_inc(norm_steps, ONE)
                dve.wait_ge(bias_ps, 3)
                nc.vector.tensor_copy(b_col[:, :], ps[:, 0, 0:4]).then_inc(bias_sb, 1)
                for j in range(2):
                    nc.vector.tensor_copy(b_all[:, j, :], ps[:, 1 + j, 0:D]).then_inc(bias_sb, 1)
                dve.wait_ge(bias_sb, 3)
                dve.wait_ge(w_in, W_IN)

                def piece(index, kind, half, b):
                    dve.wait_ge(filled, index + 1)
                    cols = slice(half * HALF, (half + 1) * HALF)
                    tiles = piece_b.rearrange("p (t c) -> p t c", t=4)
                    if kind == "turn_x":
                        nc.vector.tensor_copy(xT[:, cols], piece_b).then_inc(used, 1)
                    elif kind == "turn_out":
                        nc.vector.tensor_copy(aoT[:, cols], piece_b).then_inc(used, 1)
                    elif kind == "v":
                        nc.vector.tensor_tensor(v[:, bass.ds(b * NT + 4 * half, 4), :], tiles, b_all[:, 0, :].unsqueeze(1).broadcast_to([P, 4, D]), ALU.add).then_inc(used, 1)
                    elif kind == "project_out":
                        if half == 0:
                            dve.wait_ge(xb_rdy, b + 1)
                        nc.vector.tensor_tensor(y[:, 4 * half:4 * half + 4, :], tiles, xb[:, 4 * half:4 * half + 4, :], ALU.add).then_inc(used, 1)
                    elif kind in ("q", "k"):
                        j = "qk".index(kind)
                        if half == 0 and j == 0:
                            dve.wait_ge(laid_out, ONE + 16 * 8 * b)
                        nc.vector.scalar_tensor_tensor(rot[:, :], piece_b, b_col[:, j:j + 1], cos[:, cols], ALU.add, ALU.mult).then_inc(used, 1)
                    else:
                        j = ("q_sw", "k_sw").index(kind)
                        st = Steps(dve, rope_steps, ROPE_STEPS * b + 10 * j + 5 * half)
                        nc.vector.scalar_tensor_tensor(part[:, :], piece_b, b_col[:, 2 + j:3 + j], sin[:, cols], ALU.add, ALU.mult).then_inc(used, 1)
                        dve.wait_ge(used, index + 1)
                        st.link(nc.vector.tensor_tensor(rot[:, :], rot[:, :], part[:, :], ALU.add))
                        st.link(nc.vector.tensor_copy(split[:, 2 * j, cols], rot[:, :]))
                        st.link(nc.vector.tensor_tensor(split[:, 2 * j + 1, cols], rot[:, :], split[:, 2 * j, cols].bitcast(F32), ALU.subtract))
                        dve.sem_inc(rope_steps, 2)

                def norm(b):
                    dve.wait_ge(used, z_index(b + 1, NZ) if not (isinstance(b, int) and b == B - 1) else z_index(B, NZ) - NX)
                    st = Steps(dve, norm_steps, ONE + NORM_STEPS * b)
                    layer_norm(nc, st, y, out[:, bass.ds(b * NT, NT), :], stats, mv, rs, tmp)
                    st.settle_apart()
                    assert st.n == NORM_STEPS, st.n

                def row_max(s, head):
                    for qt in range(NT):
                        dve.wait_ge(max_ps, NT * head + qt + 1)
                        nc.vector.reduce_max(mx[:, s, qt:qt + 1], score_b[qt % 2], AX.X).then_inc(max_rdy, 1)
                    for half in range(2):
                        dve.wait_ge(neg_ps, 2 * head + half + 1)
                        nc.vector.tensor_scalar(neg_max[:, s, half * HALF:(half + 1) * HALF], piece_b[0:1, :], -1.0, None, ALU.mult).then_inc(neg_rdy, 1)

                def copy_acc(b, pair):
                    dve.wait_ge(pv_done, ONE + VC + NT * (b * NP + pair + 1))
                    nc.vector.tensor_copy(acc[:, pair % 2, :], acc_b[pair % 2]).then_inc(acc_sb, 1)

                def normalize(b, pair):
                    n = b * NP + pair
                    dve.wait_ge(accT_ps, n + 1)
                    t5 = accT_b.rearrange("p (j s f c) -> p s f j c", j=4, s=2, f=2)
                    recip = recips[:, bass.ds(n * 2 * NT, 2 * NT)].rearrange("p (s f j) -> p s f j", s=2, f=2)
                    nc.vector.reciprocal(recip, t5[:, :, :, :, HD]).then_inc(recip_rdy, 1)
                    dve.wait_ge(recip_rdy, n + 1)
                    for s in range(2):
                        at = pair * 2 * HD + s * HD
                        o = ao[:, :, at:at + HD].rearrange("p (f j) c -> p f j c", f=2)
                        nc.vector.tensor_tensor(o, t5[:, s, :, :, 0:HD], recip[:, s, :, :].unsqueeze(3).broadcast_to([P, 2, 4, HD]), ALU.mult).then_inc(ao_rdy, 1)

                for k, (kind, half) in enumerate(X_PIECES):
                    piece(k, kind, half, 0)
                dve.wait_ge(used, NX)
                dve.sem_inc(used, NZ)

                def batch(b, first, last):
                    at = pieces(b, first, last)
                    for i in range(BS):
                        if with_max and i % NT == 0:
                            for s in range(2):
                                row_max(s, 2 * (b * NP + i // NT) + s)
                        before = (b, i // NT - 1) if i >= NT else (b - 1, NP - 1)
                        if i % NT == 1 and not (first and i < NT):
                            copy_acc(*before)
                        if i % NT == TURN and not (first and i < NT):
                            normalize(*before)
                        if i in at:
                            piece(*at[i])
                        if i == NORM_AT and not first:
                            norm(b - 1)

                batches(dve, batch)
                copy_acc(B - 1, NP - 1)
                normalize(B - 1, NP - 1)
                for k, (kind, half) in enumerate(Z_PIECES):
                    piece(z_index(B, k) - NX, kind, half, B - 1)
                norm(B - 1)
                if not with_max:
                    count_safe(nc, dve, judged, recips, ok, good)
                    raise_flag(nc, dve, judged, accT_b[0:1, 0:P], total, P * B * H * NT, flag)



def depth_ffn(nc, x, out_dram, ps, ident, I):
    FF = 512
    NB = FF // P
    K = T // 2
    ctx = ExitStack()
    with ctx:
        sb = lambda name, shape, dt=F32: ctx.enter_context(nc.sbuf_tensor("d_" + name, shape, dt))
        sems, sem = semaphores(nc, ctx, "d_")
        w1, w2 = sb("w1", [P, FF]), sb("w2", [P, NB, D])
        b1, b2 = sb("b1", [P, NB]), sb("b2", [P, 1])
        wr, wr_rep, br = sb("wr", [P, 1]), sb("wr_rep", [P, P]), sb("br", [P, 1])
        xs, xT = sb("xs", [P, NT, D]), sb("xT", [P, T])
        w_row, w_col, ge = sb("w_row", [P, T]), sb("w_col", [P, NT]), sb("ge", [P, 2, T])
        count, sel, keep = sb("count", [P, NT]), sb("sel", [P, NT]), sb("keep", [P, NT])
        hid, blk = sb("hid", [P, NB, T]), sb("blk", [P, T])
        kept, y, yo = sb("kept", [P, NT, D]), sb("y", [P, NT, D]), sb("yo", [P, NT, D])
        stats, mv, rs, tmp = sb("stats", [P, NT, 6]), sb("mv", [P, NT, 2]), sb("rs", [P, NT]), sb("tmp", [P, 2, NT])

        w_in, wr_rdy, x_in, x_used, xT_ps, xT_sb = map(sem, ("w_in", "wr", "x_in", "x_used", "xT_ps", "xT_sb"))
        row_ps, row_sb, col_ps, col_sb = map(sem, ("row_ps", "row_sb", "col_ps", "col_sb"))
        hid_ps, hid_sb, blk_ps, blk_sb, blkT_ps = map(sem, ("hid_ps", "hid_sb", "blk_ps", "blk_sb", "blkT_ps"))
        y_rdy, out_rdy, out_done, steps = map(sem, ("y", "out", "out_done", "steps"))
        bank2 = lambda i: ps[:, i:i + 2, :].rearrange("p a n -> p (a n)")
        tr_ps, row_b, hid_b = bank2(0), bank2(2), [bank2(4), bank2(6)]
        W_IN = 16 * 6
        V_STEPS = NT + 2 + (NT - 1) + (NT - 1) + LN_STEPS

        ctx.callback(clear_semaphores, nc, sems)
        block = ctx.enter_context(nc.Block())

        @block.sync
        def _(sp):
            sp.sem_inc(out_done, ONE)
            sp.dma_start(wr[:, :], I["L1_ffn_w_r"]).then_inc(w_in, 16)
            sp.dma_start(br[:, :], I["L1_ffn_b_r"].rearrange("(o n) -> o n", o=1).broadcast_to([P, 1])).then_inc(w_in, 16)
            sp.dma_start(w1[:, :], I["L1_ffn_W1"]).then_inc(w_in, 16)
            sp.dma_start(w2[:, :, :], I["L1_ffn_W2"].rearrange("(n p) c -> p n c", p=P)).then_inc(w_in, 16)
            with nc.allow_non_contiguous_dma("two bias vectors onto partitions"):
                sp.dma_start(b1[:, :], I["L1_ffn_b1"].rearrange("(n p) -> p n", p=P)).then_inc(w_in, 16)
                sp.dma_start(b2[:, :], I["L1_ffn_b2"].rearrange("(p o) -> p o", o=1)).then_inc(w_in, 16)
            with sp.Fori(0, B) as b:
                sp.wait_ge(x_used, ONE + b)
                sp.wait_ge(xT_ps, ONE + b)
                sp.dma_start(xs[:, :, :], x[:, bass.ds(b * NT, NT), :]).then_inc(x_in, 16)
                sp.wait_ge(out_rdy, b + 1)
                sp.dma_start(out_dram[b].rearrange("(t p) c -> p t c", p=P), yo[:, :, :]).then_inc(out_done, 16)
            sp.wait_ge(out_done, ONE + 16 * B)

        @block.gpsimd
        def _(pool):
            pool.wait_ge(w_in, W_IN)
            nc.gpsimd.tensor_copy(wr_rep[:, :], wr[:, 0:1].broadcast_to([P, P])).then_inc(wr_rdy, 1)

        @block.scalar
        def _(act):
            nc.scalar.preload_act_table(ACT.Gelu)
            act.wait_ge(w_in, W_IN)
            with act.Fori(0, B) as b:
                act.wait_ge(xT_ps, ONE + b + 1)
                nc.scalar.copy(xT[:, :], tr_ps).then_inc(xT_sb, 1)
                act.wait_ge(blk_ps, ONE + b)
                for n in range(NB):
                    act.wait_ge(hid_ps, NB * b + n + 1)
                    nc.scalar.activation(hid[:, n, :], hid_b[n % 2], ACT.Gelu, bias=b1[:, n:n + 1]).then_inc(hid_sb, 1)

        @block.tensor
        def _(pe):
            pe.sem_inc(blk_ps, ONE)
            pe.sem_inc(xT_ps, ONE)
            pe.wait_ge(w_in, W_IN)
            pe.wait_ge(wr_rdy, 1)
            with pe.Fori(0, B) as b:
                pe.wait_ge(x_in, 16 * b + 16)
                pe.wait_ge(blk_sb, ONE + b)
                for t in range(NT):
                    last = nc.tensor.transpose(tr_ps[:, t * P:(t + 1) * P], xs[:, t, :], ident[:, :])
                last.then_inc(xT_ps, 1)
                pe.wait_ge(xT_sb, b + 1)
                pe.wait_ge(y_rdy, ONE + b)
                for s in range(0, T, HALF):
                    last = nc.tensor.matmul(row_b[:, s:s + HALF], wr_rep[:, :], xT[:, s:s + HALF], start=True, stop=True)
                last.then_inc(row_ps, 1)
                for n in range(NB):
                    if n >= 2:
                        pe.wait_ge(hid_sb, NB * b + n - 1)
                    for s in range(0, T, HALF):
                        last = nc.tensor.matmul(hid_b[n % 2][:, s:s + HALF], w1[:, n * P:(n + 1) * P], xT[:, s:s + HALF], start=True, stop=True)
                    last.then_inc(hid_ps, 1)
                    if n == 1:
                        pe.wait_ge(row_sb, b + 1)
                        for t in range(NT):
                            last = nc.tensor.transpose(row_b[:, t * P:(t + 1) * P], w_row[:, t * P:(t + 1) * P], ident[:, :])
                        last.then_inc(col_ps, 1)
                for n in range(NB):
                    pe.wait_ge(hid_sb, NB * b + n + 1)
                    for s in range(0, T, HALF):
                        last = nc.tensor.matmul(tr_ps[:, s:s + HALF], w2[:, n, :], hid[:, n, s:s + HALF], start=(n == 0), stop=(n == NB - 1))
                last.then_inc(blk_ps, 1)
                pe.wait_ge(blk_sb, ONE + b + 1)
                pe.wait_ge(col_sb, b + 1)
                for t in range(NT):
                    last = nc.tensor.transpose(row_b[:, t * P:(t + 1) * P], blk[:, t * P:(t + 1) * P], ident[:, :])
                last.then_inc(blkT_ps, 1)

        @block.vector
        def _(dve):
            dve.sem_inc(blk_sb, ONE)
            dve.sem_inc(y_rdy, ONE)
            dve.sem_inc(x_used, ONE)
            dve.wait_ge(w_in, W_IN)
            with dve.Fori(0, B) as b:
                st = Steps(dve, steps, b * V_STEPS)
                dve.wait_ge(row_ps, b + 1)
                nc.vector.tensor_scalar(w_row[:, :], row_b, br[:, 0:1], None, ALU.add).then_inc(row_sb, 1)
                dve.wait_ge(col_ps, b + 1)
                nc.vector.tensor_copy(w_col[:, :], row_b.rearrange("p (t r) -> p t r", r=P)[:, :, 0]).then_inc(col_sb, 1)
                dve.wait_ge(col_sb, b + 1)
                for t in range(NT):
                    if t >= 2:
                        dve.wait_ge(steps, b * V_STEPS + t - 1)
                    st.done(nc.vector.tensor_scalar(ge[:, t % 2, :], w_row[:, :], w_col[:, t:t + 1], None, ALU.is_ge, ALU.add,
                                                    accum_out=count[:, t:t + 1]))
                st.settle()
                st.link(nc.vector.tensor_scalar(sel[:, :], count[:, :], float(K), None, ALU.is_lt))
                st.link(nc.vector.tensor_scalar(keep[:, :], sel[:, :], -1.0, 2.0, ALU.mult, ALU.add))
                dve.wait_ge(x_in, 16 * b + 16)
                for t in range(NT):
                    last = nc.vector.tensor_scalar(kept[:, t, :], xs[:, t, :], keep[:, t:t + 1], None, ALU.mult)
                    if t < NT - 1:
                        st.done(last)
                last.then_inc(x_used, 1)
                dve.wait_ge(x_used, ONE + b + 1)
                st.settle()
                dve.wait_ge(blk_ps, ONE + b + 1)
                nc.vector.tensor_scalar(blk[:, :], tr_ps, b2[:, 0:1], None, ALU.add).then_inc(blk_sb, 1)
                dve.wait_ge(blkT_ps, b + 1)
                for t in range(NT):
                    last = nc.vector.scalar_tensor_tensor(y[:, t, :], row_b[:, t * P:(t + 1) * P], sel[:, t:t + 1], kept[:, t, :], ALU.mult, ALU.add)
                    if t < NT - 1:
                        st.done(last)
                last.then_inc(y_rdy, 1)
                dve.wait_ge(y_rdy, ONE + b + 1)
                st.settle()
                dve.wait_ge(out_done, ONE + 16 * b)
                layer_norm(nc, st, y, yo[:, :, :], stats, mv, rs, tmp)
                st.settle()
                nc.vector.tensor_copy(tmp[:, 0, :], mv[:, :, 1]).then_inc(out_rdy, 1)
                assert st.n == V_STEPS, st.n


def program(nc, I, out_dram):
    ctx = ExitStack()
    with ctx:
        ps = ctx.enter_context(nc.psum_tensor("banks", [P, 8, HALF], F32))
        ident = ctx.enter_context(nc.sbuf_tensor("ident", [P, P], F32))
        flag = ctx.enter_context(nc.sbuf_tensor("flag", [1, 1], I32))
        r1 = ctx.enter_context(nc.sbuf_tensor("r1", [P, B * NT, D], F32))
        r2 = ctx.enter_context(nc.sbuf_tensor("r2", [P, B * NT, D], F32))
        linear_attention(nc, I["L0_attn_x"], r1, ps, ident, I)
        for attention, x, y, tag in ((switch_attention, r1, r2, "b"), (rotary_attention, r2, r1, "c")):
            attention(nc, x, y, ps, ident, I, None, flag, tag + "_")
            attention(nc, x, y, ps, ident, I, flag, flag, tag + "_redo_")
        depth_ffn(nc, r1, out_dram, ps, ident, I)


def constants():
    import numpy as np

    ident = np.eye(P, dtype=np.float32)
    row, col = np.arange(P)[:, None], np.arange(P)[None, :]
    same_head = row // HD == col // HD
    sel = np.stack([same_head & (col % HD == m) for m in range(HD)] + [same_head], axis=1).astype(np.float32)
    inv = (1.0 / np.float32(10000.0) ** (np.arange(0, HD, 2, dtype=np.float32) / HD)).astype(np.float32)
    freqs = np.arange(T, dtype=np.float32)[:, None] * inv[None, :]
    ang = np.concatenate((freqs, freqs), axis=-1)[:, ::2].astype(np.float64)
    pair = np.arange(D) % HD // 2
    cos = np.cos(ang)[:, pair].T.astype(np.float32)
    sin = (np.sin(ang)[:, pair] * np.where(np.arange(D) % 2 == 0, -1, 1)).T.astype(np.float32)
    return {"ident": ident, "sel": sel, "cos": np.ascontiguousarray(cos), "sin": np.ascontiguousarray(sin)}


_NAMES = ("L0_attn_x", "L0_attn_Wq", "L0_attn_bq", "L0_attn_Wk", "L0_attn_bk", "L0_attn_Wv", "L0_attn_bv",
          "L0_attn_Wo", "L0_attn_bo", "L0_ffn_Wq", "L0_ffn_Wkv", "L0_ffn_Ws", "L0_ffn_Wd", "L0_ffn_Wo",
          "L1_attn_Wq", "L1_attn_bq", "L1_attn_Wk", "L1_attn_bk", "L1_attn_Wv", "L1_attn_bv",
          "L1_attn_Wo", "L1_attn_bo", "L1_ffn_w_r", "L1_ffn_b_r", "L1_ffn_W1", "L1_ffn_b1",
          "L1_ffn_W2", "L1_ffn_b2")


def kernel(**inputs):
    import numpy as _np
    import concourse.bacc as _bacc
    from concourse import mybir as _mybir
    from concourse.bass_utils import run_bass_kernel_spmd as _run

    nc = _bacc.Bacc("TRN2", target_bir_lowering=False, num_devices=1)
    arrays, aps = {}, {}
    given = {name: inputs[name] for name in _NAMES}
    given.update(constants())
    for name, value in given.items():
        a = _np.ascontiguousarray(value)
        arrays[f"in_{name}"] = a
        aps[name] = nc.dram_tensor(f"in_{name}", a.shape, _mybir.dt.from_np(a.dtype), kind="ExternalInput").ap()
    out = nc.dram_tensor("out", (B, T, D), F32, kind="ExternalOutput").ap()
    program(nc, aps, out)
    r = _run(nc, [arrays], core_ids=[0])
    return r.results[0]["out"]
```

```python
import concourse.bass as bass
from concourse import mybir
from contextlib import ExitStack, nullcontext

F32 = mybir.dt.float32
F32R = mybir.dt.float32r
BF16 = mybir.dt.bfloat16
I32 = mybir.dt.int32
ALU = mybir.AluOpType
ACT = mybir.ActivationFunctionType
AX = mybir.AxisListType

P = 128
B, T, D = 4, 1024, 128
NT = T // P
HALF = 512
LN_EPS = 1e-5
H = 16
HD = D // H


ONE = 1


class Steps:

    def __init__(self, eng, sem, base=0):
        self.eng, self.sem, self.base, self.n = eng, sem, base, 0

    def done(self, ins):
        ins.then_inc(self.sem, 1)
        self.n += 1
        return ins

    def settle(self):
        self.eng.wait_ge(self.sem, self.base + self.n)

    def settle_apart(self):
        self.settle()
        self.eng.sem_inc(self.sem, 1)
        self.n += 1

    def link(self, ins):
        self.done(ins)
        self.settle()


def layer_norm_parts(nc, st, y, out, stats, mv, rs, tmp):
    for half in range(2):
        for t in range(4 * half, 4 * half + 4):
            st.done(nc.vector.bn_stats(stats[:, t, :], y[:, t, :]))
        yield
    st.settle_apart()
    for t in range(NT):
        st.done(nc.vector.bn_aggr(mv[:, t, :], stats[:, t, :]))
    st.settle()
    yield
    var = tmp[:, 0, :]
    half_step = tmp[:, 1, :]
    st.link(nc.vector.tensor_scalar(var, mv[:, :, 1], LN_EPS, None, ALU.add))
    st.link(nc.vector.tensor_scalar(rs[:, :].bitcast(I32), var.bitcast(I32), -0.5, float(0x5F3759DF),
                                    ALU.mult, ALU.add))
    for _ in range(3):
        st.link(nc.vector.tensor_tensor(half_step, rs[:, :], rs[:, :], ALU.mult))
        st.link(nc.vector.scalar_tensor_tensor(half_step, half_step, -0.5, var, ALU.mult, ALU.mult))
        st.link(nc.vector.scalar_tensor_tensor(rs[:, :], half_step, 1.5, rs[:, :], ALU.add, ALU.mult))
        yield
    for half in range(2):
        for t in range(4 * half, 4 * half + 4):
            st.done(nc.vector.tensor_scalar(out[:, t, :], y[:, t, :], mv[:, t, 0:1], rs[:, t:t + 1],
                                            ALU.subtract, ALU.mult))
        yield


def layer_norm(nc, st, y, out, stats, mv, rs, tmp):
    st.settle()
    for _ in layer_norm_parts(nc, st, y, out, stats, mv, rs, tmp):
        pass


LN_PARTS = 8
LN_STEPS = 3 * NT + 3 + 9


def semaphores(nc, ctx, tag):
    sems = []

    def sem(name):
        sems.append(ctx.enter_context(nc.semaphore(tag + name)))
        return sems[-1]

    return sems, sem


def clear_semaphores(nc, sems):
    with nc.Block() as block:
        @block.gpsimd
        def _(pool):
            for sem in sems:
                pool.sem_clear(sem)


SAFE_LOW, SAFE_HIGH = 1e-18, 1e18


def only_if(eng, flag):
    return nullcontext() if flag is None else eng.If(eng.value_load(flag[0:1, 0:1], min_val=0, max_val=1))


def count_safe(nc, dve, judged, recips, ok, good):
    nc.vector.tensor_scalar(ok, recips, SAFE_LOW, None, ALU.is_ge).then_inc(judged, 1)
    dve.wait_ge(judged, 1)
    nc.vector.scalar_tensor_tensor(ok, recips, SAFE_HIGH, ok, ALU.is_le, ALU.mult).then_inc(judged, 1)
    dve.wait_ge(judged, 2)
    nc.vector.reduce_sum(good[:, 0:1], ok, AX.X).then_inc(judged, 1)


def turn_counts(nc, pe, judged, good, ident, row):
    pe.wait_ge(judged, 3)
    nc.tensor.matmul(row, good[:, 0:1], ident[:, :], start=True, stop=True).then_inc(judged, 1)


def raise_flag(nc, dve, judged, row, total, count, flag):
    dve.wait_ge(judged, 4)
    nc.vector.reduce_sum(total[0:1, 0:1], row, AX.X).then_inc(judged, 1)
    dve.wait_ge(judged, 5)
    nc.vector.tensor_scalar(flag[0:1, 0:1], total[0:1, 0:1], float(count), None, ALU.is_lt).then_inc(judged, 1)
    dve.wait_ge(judged, 6)


def linear_attention(nc, x_dram, out, ps, ident, I):
    ctx = ExitStack()
    with ctx:
        sb = lambda name, shape, dt=F32: ctx.enter_context(nc.sbuf_tensor(name, shape, dt))
        sems, sem = semaphores(nc, ctx, "a_")
        wq, wk, wv, wo = (sb(f"a_{n}", [P, D]) for n in ("wq", "wk", "wv", "wo"))
        wv_rep = sb("a_wv_rep", [P, HD, H, HD])
        bq, bk = sb("a_bq", [P, 1]), sb("a_bk", [P, 1])
        rows = sb("a_rows", [1, 2, D])
        bv_rep = sb("a_bv_rep", [1, HD, H, HD])
        bv_col = sb("a_bv_col", [P, HD])
        bo_all = sb("a_bo_all", [P, D])
        sel = sb("a_sel", [P, HD + 1, P])
        ones = sb("a_ones", [P, T])
        xs, xT = sb("a_xs", [P, NT, D]), sb("a_xT", [P, T])
        low, relu, expo = (sb(f"a_{n}", [P, 2, T]) for n in ("low", "relu", "expo"))
        q, k = sb("a_q", [P, T]), sb("a_k", [P, T])
        kv, scan, qscan = sb("a_kv", [P, T]), sb("a_scan", [P, 2, T]), sb("a_qscan", [P, 2, T])
        rden, vals = sb("a_rden", [P, T]), sb("a_vals", [P, T])
        xb, y = sb("a_xb", [P, NT, D]), sb("a_y", [P, NT, D])
        stats, mv, rs, tmp = sb("a_stats", [P, NT, 6]), sb("a_mv", [P, NT, 2]), sb("a_rs", [P, NT]), sb("a_tmp", [P, 2, NT])

        x_in, w_in, ones_rdy, reps, bias_ps, bias_sb = map(sem, ("x_in", "w_in", "ones", "reps", "bias_ps", "bias_sb"))
        xT_ps, xT_sb, qk_ps, low_rdy, exp_rdy, q_rdy = map(sem, ("xT_ps", "xT_sb", "qk_ps", "low", "exp", "q"))
        v_ps, kv_rdy, scan_rdy, qs_rdy, acc_ps = map(sem, ("v_ps", "kv", "scan", "qs", "acc_ps"))
        den_read, vals_rdy, o_ps, xb_rdy, y_rdy, steps = map(sem, ("den_read", "vals", "o_ps", "xb", "y", "steps"))
        norm_steps = sem("norm_steps")
        NJ = HD + 1
        bank2 = lambda i: ps[:, i:i + 2, :].rearrange("p a n -> p (a n)")
        tr_ps, q_ps, k_ps = bank2(6), bank2(2), bank2(4)
        vb_ps = [bank2(6), bank2(0)]
        num_ps, den_ps, o2_ps = q_ps, k_ps, bank2(0)
        V_STEPS = 2 + 1 + 4
        W_IN = 16 * 10

        ctx.callback(clear_semaphores, nc, sems)
        block = ctx.enter_context(nc.Block())

        @block.sync
        def _(sp):
            sp.dma_start(xs[:, :, :], x_dram[0].rearrange("(t p) c -> p t c", p=P)).then_inc(x_in, 16)
            sp.dma_start(ident[:, :], I["ident"]).then_inc(w_in, 16)
            for dst, src in ((wq, "L0_attn_Wq"), (wk, "L0_attn_Wk"), (wv, "L0_attn_Wv"), (wo, "L0_attn_Wo")):
                sp.dma_start(dst[:, :], I[src]).then_inc(w_in, 16)
            for dst, src in ((bq, "L0_attn_bq"), (bk, "L0_attn_bk")):
                sp.dma_start(dst[:, :], I[src].rearrange("(p o) -> p o", o=1)).then_inc(w_in, 16)
            for j, src in enumerate(("L0_attn_bv", "L0_attn_bo")):
                sp.dma_start(rows[:, j, :], I[src].rearrange("(o n) -> o n", o=1)).then_inc(w_in, 16)
            sp.dma_start(sel[:, :, :], I["sel"]).then_inc(w_in, 16)
            with sp.Fori(0, B - 1) as b:
                sp.wait_ge(xT_ps, b + 1)
                sp.wait_ge(xb_rdy, b + 1)
                sp.dma_start(xs[:, :, :], x_dram[b + 1].rearrange("(t p) c -> p t c", p=P)).then_inc(x_in, 16)

        @block.gpsimd
        def _(pool):
            nc.gpsimd.memset(ones[:, :], 1.0).then_inc(ones_rdy, 1)
            pool.wait_ge(w_in, W_IN)
            for m in range(HD):
                nc.gpsimd.tensor_copy(wv_rep[:, m, :, :],
                                      wv[:, :].rearrange("p (h m) -> p m h", h=H)[:, m, :].unsqueeze(2).broadcast_to([P, H, HD])).then_inc(reps, 1)
                nc.gpsimd.tensor_copy(bv_rep[:, m, :, :],
                                      rows[:, 0, :].rearrange("p (h m) -> p m h", h=H)[:, m, :].unsqueeze(2).broadcast_to([1, H, HD])).then_inc(reps, 1)
            pool.wait_ge(bias_sb, 2)
            with pool.Fori(0, B) as b:
                pool.wait_ge(x_in, 16 * b + 16)
                pool.wait_ge(y_rdy, ONE + b)
                nc.gpsimd.tensor_tensor(xb[:, :, :], xs[:, :, :],
                                        bo_all[:, :].unsqueeze(1).broadcast_to([P, NT, D]), ALU.add).then_inc(xb_rdy, 1)
                for j in range(NJ):
                    pool.wait_ge(scan_rdy, b * NJ + j + 1)
                    if j >= 2:
                        pool.wait_ge(acc_ps, b * NJ + j - 1)
                    nc.gpsimd.tensor_tensor(qscan[:, j % 2, :], scan[:, j % 2, :], q[:, :], ALU.mult).then_inc(qs_rdy, 1)

        @block.scalar
        def _(act):
            nc.scalar.preload_act_table(ACT.Exp)
            with act.Fori(0, B) as b:
                act.wait_ge(xT_ps, b + 1)
                nc.scalar.copy(xT[:, :], tr_ps).then_inc(xT_sb, 1)
                for j in range(2):
                    act.wait_ge(low_rdy, 2 * b + j + 1)
                    nc.scalar.activation(expo[:, j, :], low[:, j, :], ACT.Exp).then_inc(exp_rdy, 1)

        @block.tensor
        def _(pe):
            pe.wait_ge(w_in, W_IN)

            def turn_x(b):
                pe.wait_ge(x_in, 16 * b + 16)
                for t in range(NT):
                    last = nc.tensor.transpose(tr_ps[:, t * P:(t + 1) * P], xs[:, t, :], ident[:, :])
                last.then_inc(xT_ps, 1)

            def batch(b, more):
                pe.wait_ge(xT_sb, b + 1)
                for w, dst in ((wq, q_ps), (wk, k_ps)):
                    for s in range(0, T, HALF):
                        last = nc.tensor.matmul(dst[:, s:s + HALF], w[:, :], xT[:, s:s + HALF], start=True, stop=True)
                    last.then_inc(qk_ps, 1)

                def value_column(m):
                    if m >= 2:
                        pe.wait_ge(kv_rdy, b * HD + m - 1)
                    if m == 1:
                        pe.wait_ge(y_rdy, ONE + b)
                    for s in range(0, T, HALF):
                        last = nc.tensor.matmul(vb_ps[m % 2][:, s:s + HALF], wv_rep[:, m, :, :].rearrange("p h d -> p (h d)"), xT[:, s:s + HALF], start=True, stop=True)
                    last.then_inc(v_ps, 1)

                value_column(0)
                value_column(1)
                pe.wait_ge(q_rdy, 2 * b + 2)
                for j in range(NJ):
                    pe.wait_ge(qs_rdy, b * NJ + j + 1)
                    dst, pick = (den_ps, HD) if j == 0 else (num_ps, j - 1)
                    for s in range(0, T, HALF):
                        last = nc.tensor.matmul(dst[:, s:s + HALF], sel[:, pick, :], qscan[:, j % 2, s:s + HALF], start=(j <= 1), stop=(j in (0, HD)))
                    last.then_inc(acc_ps, 1)
                    if j + 2 < HD:
                        value_column(j + 2)
                    if j == HD - 1 and more:
                        pe.wait_ge(kv_rdy, b * HD + HD - 1)
                        turn_x(b + 1)
                pe.wait_ge(vals_rdy, b + 1)
                for t in range(NT):
                    last = nc.tensor.matmul(o2_ps[:, t * P:(t + 1) * P], vals[:, t * P:(t + 1) * P], wo[:, :], start=True, stop=True)
                last.then_inc(o_ps, 1)

            turn_x(0)
            pe.wait_ge(ones_rdy, 1)
            pe.wait_ge(reps, 2 * HD)
            for m in range(HD):
                last = nc.tensor.matmul(ps[:, 0, m:m + 1], bv_rep[:, m, :, :].rearrange("p h d -> p (h d)"), ones[0:1, 0:1], start=True, stop=True)
            last.then_inc(bias_ps, 1)
            nc.tensor.matmul(ps[:, 1, 0:D], ones[0:1, 0:P], rows[:, 1, :], start=True, stop=True).then_inc(bias_ps, 1)
            pe.wait_ge(bias_sb, 2)
            with pe.Fori(0, B - 1) as b:
                batch(b, True)
            batch(B - 1, False)

        @block.vector
        def _(dve):
            dve.sem_inc(y_rdy, ONE)
            dve.wait_ge(bias_ps, 1)
            nc.vector.tensor_copy(bv_col[:, :], ps[:, 0, 0:HD]).then_inc(bias_sb, 1)
            dve.wait_ge(bias_ps, 2)
            nc.vector.tensor_copy(bo_all[:, :], ps[:, 1, 0:D]).then_inc(bias_sb, 1)
            dve.wait_ge(bias_sb, 2)

            def norm_parts(b):
                dve.wait_ge(y_rdy, ONE + b + 1)
                st = Steps(dve, norm_steps, LN_STEPS * b)
                yield from layer_norm_parts(nc, st, y, out[:, bass.ds(b * NT, NT), :], stats, mv, rs, tmp)
                st.settle()
                assert st.n == LN_STEPS, st.n

            def batch(b, first):
                norm = iter(()) if first else norm_parts(b - 1)
                st = Steps(dve, steps, b * V_STEPS)
                for j, (src, bias) in enumerate(((q_ps, bq), (k_ps, bk))):
                    dve.wait_ge(qk_ps, 2 * b + j + 1)
                    nc.vector.tensor_scalar(low[:, j, :], src, bias[:, 0:1], 0.0, ALU.add, ALU.min).then_inc(low_rdy, 1)
                    st.done(nc.vector.tensor_scalar(relu[:, j, :], src, bias[:, 0:1], 0.0, ALU.add, ALU.max))
                st.settle()
                for j, dst in enumerate((q, k)):
                    dve.wait_ge(exp_rdy, 2 * b + j + 1)
                    nc.vector.tensor_tensor(dst[:, :], relu[:, j, :], expo[:, j, :], ALU.add).then_inc(q_rdy, 1)
                dve.wait_ge(q_rdy, 2 * b + 2)
                for j in range(NJ):
                    if j >= 1:
                        dve.wait_ge(v_ps, b * HD + j)
                        nc.vector.scalar_tensor_tensor(kv[:, :], vb_ps[(j - 1) % 2], bv_col[:, j - 1:j], k[:, :], ALU.add, ALU.mult).then_inc(kv_rdy, 1)
                        dve.wait_ge(kv_rdy, b * HD + j)
                    if j >= 2:
                        dve.wait_ge(qs_rdy, b * NJ + j - 1)
                    nc.vector.tensor_tensor_scan(scan[:, j % 2, :], ones[:, :], (k if j == 0 else kv)[:, :], 0.0, ALU.mult, ALU.add).then_inc(scan_rdy, 1)
                    if j >= 1:
                        dve.wait_ge(scan_rdy, b * NJ + j + 1)
                    if j == 3:
                        dve.wait_ge(acc_ps, b * NJ + 1)
                        st.link(nc.vector.tensor_scalar(rden[:, :], den_ps, 1e-6, None, ALU.add))
                    if 3 <= j < 7:
                        cols = slice((j - 3) * (T // 4), (j - 2) * (T // 4))
                        st.done(nc.vector.reciprocal(rden[:, cols], rden[:, cols]))
                    if j in (1, 2, 7, 8):
                        next(norm, None)
                for _ in norm:
                    pass
                st.settle()
                dve.wait_ge(acc_ps, b * NJ + NJ)
                nc.vector.tensor_tensor(vals[:, :], num_ps, rden[:, :], ALU.mult).then_inc(vals_rdy, 1)
                dve.wait_ge(o_ps, b + 1)
                dve.wait_ge(xb_rdy, b + 1)
                nc.vector.tensor_tensor(y[:, :, :].rearrange("p t c -> p (t c)"), o2_ps, xb[:, :, :].rearrange("p t c -> p (t c)"), ALU.add).then_inc(y_rdy, 1)
                assert st.n == V_STEPS, st.n

            batch(0, True)
            with dve.Fori(1, B) as b:
                batch(b, False)
            for _ in norm_parts(B - 1):
                pass



def switch_attention(nc, x, out, ps, ident, I, redo, flag, tag):
    NH, E, DH, TOP = 8, 5, 64, 3
    ED = E * DH
    U = 3 * NT
    NG = 2 * NH
    HALVES = ((0, HALF), (HALF, T))
    with_max = redo is not None
    ctx = ExitStack()
    with ctx:
        sb = lambda name, shape, dt=F32: ctx.enter_context(nc.sbuf_tensor(tag + name, shape, dt))
        sems, sem = semaphores(nc, ctx, tag)
        w = sb("w", [P, 2, 2, 3, ED], F32R)
        raw_w = sb("raw_w", [P, 2, 3, ED])
        wg = sb("wg", [P, NG * E])
        wo = sb("wo", [P, 3, D])
        ones = sb("ones", [P, P])
        xs, xT = sb("xs", [P, NT, D]), sb("xT", [P, T])
        xh, xl = sb("xh", [P, T], F32R), sb("xl", [P, T], F32R)
        gate = sb("gate", [P, B, NT, NG * E])
        beats = sb("beats", [P, NT * NG, E, E])
        mask = sb("mask", [P, NT * NG, E])
        picked = sb("picked", [P, B, NT, NH * E], BF16)
        gated = sb("gated", [P, 2, 3, ED])
        tok = sb("tok", [P, 2, NT, 3, DH])
        kk = sb("kk", [P, 2, T], F32R)
        qh, ql = sb("qh", [P, 2, T], F32R), sb("ql", [P, 2, T], F32R)
        vals = sb("vals", [P, 2, NT, DH])
        probs = sb("probs", [P, 4, T])
        psum = sb("psum", [P, 2, T])
        acc, sums = sb("acc", [P, HALF]), sb("sums", [P, 2 * P])
        o = sb("o", [P, NT, DH])
        share, z = sb("share", [P, NT, E, DH]), sb("z", [P, NT, E, DH])
        zT = sb("zT", [P, 2, 3, P])
        y = xT[:, :].rearrange("p (t c) -> p t c", t=NT)
        stats, mv, rs, tmp = sb("stats", [P, NT, 6]), sb("mv", [P, NT, 2]), sb("rs", [P, NT]), sb("tmp", [P, 2, NT])
        recips, good, total = sb("recips", [P, B * NH * NT]), sb("good", [P, 1]), sb("total", [1, 1])
        ok = share[:, :, :, :].rearrange("p t e d -> p (t e d)")[:, 0:B * NH * NT]
        judged = sem("judged")
        if with_max:
            mx, neg_max = sb("mx", [P, NT]), sb("neg_max", [1, T])
            max_ps, max_rdy, neg_ps, neg_rdy = map(sem, ("max_ps", "max", "neg_ps", "neg"))

        w_in, clear = sem("w_in"), sem("clear")
        raw_in = [sem("raw_in0"), sem("raw_in1")]
        w_high, w_low = sem("w_high"), sem("w_low")
        x_in, xT_ps, xT_sb, x_high, x_low, gate_ps, gate_exp = map(sem, ("x_in", "xT_ps", "xT_sb", "x_high", "x_low", "gate_ps", "gate_exp"))
        proj_ps, mult, tok_rdy = map(sem, ("proj_ps", "mult", "tok_rdy"))
        turn_ps, high_rdy, low_rdy, vals_rdy = map(sem, ("turn_ps", "high", "low", "vals_rdy"))
        score_ps, exp_rdy, pv_done, psum_rdy = map(sem, ("score_ps", "exp", "pv", "psum_rdy"))
        acc_sb, sum_ps, sum_sb, sumT_ps, recip_rdy, accT_ps, o_rdy = map(sem, ("acc_sb", "sum_ps", "sum_sb", "sumT_ps", "recip_rdy", "accT_ps", "o_rdy"))
        share_rdy, zT_ps, zT_sb, y_rdy, steps = map(sem, ("share_rdy", "zT_ps", "zT_sb", "y_rdy", "steps"))
        z_rdy = [sem("z_rdy0"), sem("z_rdy1")]
        norm_steps = sem("norm_steps")

        proj_b = [ps[:, 0, :], ps[:, 1, :]]
        turn_b, acc_b = ps[:, 2, :], ps[:, 3, :]
        score_b = [ps[:, i:i + 2, :].rearrange("p a n -> p (a n)") for i in (4, 6)]
        MULT0, TOK0, VALS0, EXP0, PV0, PSUM0, SUM0 = 2, 2, 2, 2, 4, NT - 1, 2
        ACC0 = ACCT0 = SUMT0 = O0 = SHARE0 = Z0 = ZT0 = 1
        NORM_STEPS = LN_STEPS + 1
        GATE_STEPS = 2 + 4 + 2 * (E - 1) + 4 + 1 + 3
        Z_COPIES = 3 * NT
        def picked_of(b, h):
            return picked[:, bass.ds(b, 1), :, h * E:(h + 1) * E].rearrange("p b t e -> p (b t) e")

        def batches(eng, body):
            body(0, True, False)
            with eng.Fori(1, B - 1) as b:
                body(b, False, False)
            body(B - 1, False, True)

        def run_periods(eng, period):
            def batch(b, first, last):
                for h in range(NH):
                    period(b * NH + h, b, h, h % 2,
                           share=(b - 1, NH - 1) if h == 0 else (b, h - 1),
                           ahead=(h + 2) % NH,
                           start=first and h == 0,
                           has_next=not (last and h == NH - 1),
                           projecting=not (last and h >= NH - 2),
                           project_out=h == 1 and not first,
                           splitting=not (last and h + 3 >= NH),
                           norm_last=h in (2, 3) and not first,
                           gates_next=h in (3, 4, 5) and not last,
                           new_x=h == NH - 2 and not last)
            batches(eng, batch)

        ctx.callback(clear_semaphores, nc, sems)
        block = ctx.enter_context(nc.Block())

        @block.sync
        def _(sp):
            with only_if(sp, redo):
                sp.dma_start(xs[:, :, :], x[:, 0:NT, :]).then_inc(x_in, 16)
                sp.dma_start(wg[:, 0:NH * E], I["L0_ffn_Ws"]).then_inc(w_in, 16)
                sp.dma_start(wg[:, NH * E:], I["L0_ffn_Wd"]).then_inc(w_in, 16)
                for e in range(E):
                    at = DH * (e % 2)
                    sp.dma_start(wo[at:at + DH, e // 2, :], I["L0_ffn_Wo"][:, e * D:(e + 1) * D]).then_inc(w_in, 16)
                wq_h = I["L0_ffn_Wq"].rearrange("c (h n) -> h c n", h=NH)
                wkv_h = I["L0_ffn_Wkv"].rearrange("c (j h n) -> h c j n", j=2, h=NH)

                def weights(n, h):
                    if not (isinstance(n, int) and n < 2):
                        sp.wait_ge(w_low, n - 1)
                    sp.dma_start(raw_w[:, h % 2, 0, :], wq_h[h]).then_inc(raw_in[h % 2], 16)
                    sp.dma_start(raw_w[:, h % 2, 1:3, :], wkv_h[h]).then_inc(raw_in[h % 2], 16)

                for n in range(3):
                    weights(n, n)

                def batch(b, first, last):
                    for h in range(NH):
                        if not (last and h + 3 >= NH):
                            weights(b * NH + h + 3, (h + 3) % NH)
                        if h == 1 and not last:
                            sp.wait_ge(xT_ps, 2 * (b + 1))
                            sp.dma_start(xs[:, :, :], x[:, bass.ds((b + 1) * NT, NT), :]).then_inc(x_in, 16)

                batches(sp, batch)

        @block.gpsimd
        def _(pool):
            with only_if(pool, redo):
                pool.sem_inc(psum_rdy, PSUM0)
                pool.sem_inc(share_rdy, SHARE0)
                nc.gpsimd.memset(ones[:, :], 1.0).then_inc(clear, 1)
                nc.gpsimd.memset(beats[:, :, :, :], 0.0).then_inc(clear, 1)

                def low_weights(n, par):
                    pool.wait_ge(w_high, n + 1)
                    nc.gpsimd.tensor_tensor(w[:, par, 1, :, :], raw_w[:, par, :, :], w[:, par, 0, :, :].bitcast(F32), ALU.subtract).then_inc(w_low, 1)

                def add_probs(n, par, i):
                    pool.wait_ge(exp_rdy, EXP0 + NT * n + i + 1)
                    if i == 1:
                        pool.wait_ge(sum_ps, SUM0 + n - 1)
                        prev = probs[:, 0, :]
                    else:
                        pool.wait_ge(psum_rdy, PSUM0 + (NT - 1) * n + i - 1)
                        prev = psum[:, par, :]
                    nc.gpsimd.tensor_tensor(psum[:, par, :], prev, probs[:, i % 4, :], ALU.add).then_inc(psum_rdy, 1)

                def gated_share(n, b, h):
                    pool.wait_ge(o_rdy, O0 + n + 1)
                    for half in range(2):
                        pool.wait_ge(z_rdy[half], Z0 + n)
                    nc.gpsimd.tensor_tensor(share[:, :, :, :], o[:, :, :].unsqueeze(2).broadcast_to([P, NT, E, DH]),
                                            picked_of(b, h).unsqueeze(3).broadcast_to([P, NT, E, DH]), ALU.mult).then_inc(share_rdy, 1)

                def period(n, b, h, par, share, ahead, start, has_next, projecting, splitting, project_out, norm_last, gates_next, new_x):
                    if norm_last and h == 2:
                        residual(b - 1)
                    for i in range(1, NT):
                        add_probs(n, par, i)
                        if i == 6 and splitting:
                            low_weights(n + 3, 1 - par)
                        if i == 3 and not start:
                            gated_share(n - 1, *share)

                def residual(b):
                    pool.wait_ge(zT_sb, Z_COPIES * (b + 1))
                    nc.gpsimd.tensor_tensor(y, y, x[:, bass.ds(b * NT, NT), :], ALU.add).then_inc(y_rdy, 1)

                for n in range(3):
                    low_weights(n, n % 2)
                run_periods(pool, period)
                gated_share(B * NH - 1, B - 1, NH - 1)
                residual(B - 1)

        @block.scalar
        def _(act):
            with only_if(act, redo):
                nc.scalar.preload_act_table(ACT.Exp)
                act.sem_inc(exp_rdy, EXP0)
                act.sem_inc(vals_rdy, VALS0)
                act.sem_inc(acc_sb, ACC0)

                def high_weights(n, par):
                    act.wait_ge(raw_in[par], 16 * (n - par) + 32)
                    if not (isinstance(n, int) and n < 2):
                        act.wait_ge(proj_ps, U * (n - 1))
                    nc.scalar.copy(w[:, par, 0, :, :], raw_w[:, par, :, :]).then_inc(w_high, 1)

                def turned_x(b, r):
                    act.wait_ge(xT_ps, 2 * b + r + 1)
                    if r == 0 and not (isinstance(b, int) and b == 0):
                        act.wait_ge(x_low, 2 * b)
                        act.wait_ge(norm_steps, ONE + NORM_STEPS * (b - 1))
                    lo, hi = HALVES[r]
                    nc.scalar.copy(xT[:, lo:hi], turn_b).then_inc(xT_sb, 1)

                def gate_exps(b, r):
                    act.wait_ge(gate_ps, 2 * b + r + 1)
                    nc.scalar.activation(gate[:, bass.ds(b, 1), 4 * r:4 * r + 4, :].rearrange("p b t c -> p (b t) c"), turn_b[:, 0:4 * NG * E].rearrange("p (t c) -> p t c", t=4), ACT.Exp, scale=-1.0).then_inc(gate_exp, 1)

                def split_x(b):
                    act.wait_ge(xT_sb, 2 * b + 2)
                    if not (isinstance(b, int) and b == 0):
                        act.wait_ge(proj_ps, U * NH * b)
                    for lo, hi in HALVES:
                        nc.scalar.copy(xh[:, lo:hi], xT[:, lo:hi]).then_inc(x_high, 1)

                def high_part(n, par, r):
                    act.wait_ge(turn_ps, 4 * n + r + 1)
                    lo, hi = HALVES[r % 2]
                    nc.scalar.copy((kk if r < 2 else qh)[:, par, lo:hi], turn_b).then_inc(high_rdy, 1)

                def copy_values(n, par):
                    act.wait_ge(tok_rdy, TOK0 + NT * (n + 1))
                    nc.scalar.copy(vals[:, par, :, :], tok[:, par, :, 2, :]).then_inc(vals_rdy, 1)

                def copy_acc(n):
                    act.wait_ge(pv_done, PV0 + NT * (n + 1))
                    act.wait_ge(accT_ps, ACCT0 + n)
                    nc.scalar.copy(acc[:, :], acc_b).then_inc(acc_sb, 1)

                def copy_sums(n):
                    act.wait_ge(sum_ps, SUM0 + n + 1)
                    act.wait_ge(sumT_ps, SUMT0 + n)
                    nc.scalar.copy(sums[:, :], turn_b[:, 0:2 * P]).then_inc(sum_sb, 1)

                def copy_z(b, t):
                    act.wait_ge(zT_ps, ZT0 + (NT + 1) * b + t + 1)
                    if t < NT:
                        nc.scalar.copy(zT[:, t % 2, 0:2, :], turn_b[:, 0:2 * P].rearrange("p (k c) -> p k c", k=2)).then_inc(zT_sb, 1)
                        nc.scalar.copy(zT[0:DH, t % 2, 2, :], turn_b[0:DH, 2 * P:3 * P]).then_inc(zT_sb, 1)
                    if t == 1:
                        act.wait_ge(norm_steps, ONE + NORM_STEPS * b)
                        act.wait_ge(x_low, 2 * (b + 1) if isinstance(b, int) and b == B - 1 else 2 * (b + 2))
                    if t:
                        nc.scalar.copy(y[:, t - 1, :], turn_b[:, 3 * P:4 * P]).then_inc(zT_sb, 1)

                def period(n, b, h, par, share, ahead, start, has_next, projecting, splitting, project_out, norm_last, gates_next, new_x):
                    for i in range(NT):
                        if new_x and i == 0:
                            split_x(b + 1)
                        if i == 1 and not start:
                            copy_sums(n - 1)
                        if 3 <= i < 7 and has_next:
                            high_part(n + 1, 1 - par, i - 3)
                        act.wait_ge(score_ps, NT * n + i + 1)
                        act.wait_ge(pv_done, PV0 + NT * n + i - 3)
                        act.wait_ge(psum_rdy, PSUM0 + (NT - 1) * n + (max(i - 4, 1) if i >= 4 else i - 3))
                        nc.scalar.activation(probs[:, i % 4, :], score_b[i % 2], ACT.Exp).then_inc(exp_rdy, 1)
                        if i == 0 and not start:
                            copy_acc(n - 1)
                        if i == 2 and has_next:
                            copy_values(n + 1, 1 - par)
                        if i == 4 and splitting:
                            high_weights(n + 3, 1 - par)
                        if project_out:
                            copy_z(b - 1, i)
                        if gates_next and h == 3 and i >= 4:
                            (turned_x if i < 6 else gate_exps)(b + 1, i % 2)
                    if project_out:
                        copy_z(b - 1, NT)

                for n in range(2):
                    high_weights(n, n)
                for work in (turned_x, gate_exps):
                    for r in range(2):
                        work(0, r)
                split_x(0)
                high_weights(2, 0)
                for r in range(4):
                    high_part(0, 0, r)
                copy_values(0, 0)
                run_periods(act, period)
                copy_acc(B * NH - 1)
                copy_sums(B * NH - 1)
                for t in range(NT + 1):
                    copy_z(B - 1, t)

        @block.tensor
        def _(pe):
            with only_if(pe, redo):
                pe.sem_inc(pv_done, PV0)
                pe.sem_inc(sum_ps, SUM0)
                pe.sem_inc(sumT_ps, SUMT0)
                pe.sem_inc(accT_ps, ACCT0)
                pe.sem_inc(zT_ps, ZT0)

                def prepare(b, k):
                    r = k % 2
                    if k == 0:
                        pe.wait_ge(x_in, 16 * (b + 1))
                    if k == 2:
                        pe.wait_ge(xT_sb, 2 * b + 2)
                    for j in range(4):
                        t = 4 * r + j
                        if k < 2:
                            last = nc.tensor.transpose(turn_b[:, j * P:(j + 1) * P], xs[:, t, :], ident[:, :])
                        else:
                            last = nc.tensor.matmul(turn_b[:, j * NG * E:(j + 1) * NG * E], xT[:, t * P:(t + 1) * P], wg[:, :], start=True, stop=True)
                    last.then_inc(xT_ps if k < 2 else gate_ps, 1)

                def prepared(b, k):
                    pe.wait_ge(xT_sb if k < 2 else gate_exp, 2 * b + k % 2 + 1)

                def project(n, par, t, js=(0, 1, 2), x_of=None):
                    if t == 0 and 0 in js:
                        pe.wait_ge(w_low, n + 1)
                    if t % 4 == 0 and 0 in js and x_of is not None:
                        pe.wait_ge(x_low, 2 * x_of + t // 4 + 1)
                    for j in js:
                        u = 3 * t + j
                        pe.wait_ge(mult, MULT0 + U * n + u - 1)
                        for i, (a, part) in enumerate(((xh, 0), (xl, 0), (xh, 1))):
                            last = nc.tensor.matmul(proj_b[u % 2][:, 0:ED], a[:, t * P:(t + 1) * P], w[:, par, part, j, :], start=(i == 0), stop=(i == 2))
                        last.then_inc(proj_ps, 1)

                def turn(n, par, r):
                    lo_tile = 4 * (r % 2)
                    pe.wait_ge(tok_rdy, TOK0 + NT * n + lo_tile + 4)
                    if r:
                        pe.wait_ge(low_rdy, 4 * n + r)
                    else:
                        pe.wait_ge(o_rdy, O0 + n - 1 if not (isinstance(n, int) and n == 0) else O0)
                    for j in range(4):
                        src = tok[:, par, lo_tile + j, 1 if r < 2 else 0, :]
                        for copy in range(2):
                            last = nc.tensor.matmul(turn_b[copy * DH:(copy + 1) * DH, j * P:(j + 1) * P], src, ident[:, :], start=True, stop=True)
                    last.then_inc(turn_ps, 1)

                def scores(n, par, i):
                    if i == 0:
                        pe.wait_ge(low_rdy, 4 * n + 4)
                        if with_max:
                            query_max(n, par)
                    pe.wait_ge(exp_rdy, EXP0 + NT * n + i - 1)
                    for lo, hi in HALVES:
                        last = nc.tensor.matmul(score_b[i % 2][:, lo:hi], kk[:, par, i * P:(i + 1) * P], qh[:, par, lo:hi], start=True, stop=False)
                        last = nc.tensor.matmul(score_b[i % 2][:, lo:hi], kk[:, par, i * P:(i + 1) * P], ql[:, par, lo:hi], start=False, stop=not with_max)
                        if with_max:
                            last = nc.tensor.matmul(score_b[i % 2][:, lo:hi], ones[0:1, :], neg_max[:, lo:hi], start=False, stop=True)
                    last.then_inc(score_ps, 1)

                def query_max(n, par):
                    pe.wait_ge(exp_rdy, EXP0 + NT * n)
                    for qt in range(NT):
                        if qt >= 2:
                            pe.wait_ge(max_rdy, NT * n + qt - 1)
                        for lo, hi in HALVES:
                            nc.tensor.matmul(score_b[qt % 2][:, lo:hi], qh[:, par, qt * P:(qt + 1) * P], kk[:, par, lo:hi], start=True, stop=False)
                            last = nc.tensor.matmul(score_b[qt % 2][:, lo:hi], ql[:, par, qt * P:(qt + 1) * P], kk[:, par, lo:hi], start=False, stop=True)
                        last.then_inc(max_ps, 1)
                    pe.wait_ge(max_rdy, NT * (n + 1))
                    for half in range(2):
                        if half:
                            pe.wait_ge(neg_rdy, 2 * n + 1)
                        for j in range(4):
                            last = nc.tensor.matmul(turn_b[0:1, j * P:(j + 1) * P], mx[:, 4 * half + j:4 * half + j + 1], ident[:, :], start=True, stop=True)
                        last.then_inc(neg_ps, 1)
                    pe.wait_ge(neg_rdy, 2 * n + 2)

                def products(n, par, i):
                    pe.wait_ge(exp_rdy, EXP0 + NT * n + i + 1)
                    if i == 0:
                        pe.wait_ge(acc_sb, ACC0 + n)
                        pe.wait_ge(vals_rdy, VALS0 + n + 1)
                    for half, (lo, hi) in enumerate(HALVES):
                        last = nc.tensor.matmul(acc_b[DH * half:DH * half + DH, :], vals[:, par, i, :], probs[:, i % 4, lo:hi], start=(i == 0), stop=(i == NT - 1))
                    last.then_inc(pv_done, 1)

                def sum_probs(n, par):
                    pe.wait_ge(psum_rdy, PSUM0 + (NT - 1) * (n + 1))
                    for j in range(4):
                        last = nc.tensor.matmul(turn_b[32 * j:32 * j + 32, 0:2 * P], ones[:, 0:32], psum[:, par, j * 2 * P:(j + 1) * 2 * P], start=True, stop=True)
                    last.then_inc(sum_ps, 1)

                def turn_sums(n):
                    pe.wait_ge(sum_sb, n + 1)
                    for j in range(2):
                        last = nc.tensor.transpose(turn_b[:, j * P:(j + 1) * P], sums[:, j * P:(j + 1) * P], ident[:, :])
                    last.then_inc(sumT_ps, 1)

                def turn_acc(n):
                    pe.wait_ge(recip_rdy, n + 1)
                    pe.wait_ge(acc_sb, ACC0 + n + 1)
                    for j in range(4):
                        last = nc.tensor.transpose(turn_b[:, j * P:(j + 1) * P], acc[:, j * P:(j + 1) * P], ident[:, :])
                    last.then_inc(accT_ps, 1)

                def project_out_piece(b, t):
                    if t == 0:
                        for half in range(2):
                            pe.wait_ge(z_rdy[half], Z0 + NH * (b + 1))
                    else:
                        pe.wait_ge(zT_sb, z_copied(b, t - 1))
                        for k in range(3):
                            n_rows = min(P, ED - k * P)
                            last = nc.tensor.matmul(turn_b[:, 3 * P:4 * P], zT[0:n_rows, (t - 1) % 2, k, :], wo[0:n_rows, k, :], start=(k == 0), stop=(k == 2))
                    if t < NT:
                        flat = z[:, t, :, :].rearrange("p e d -> p (e d)")
                        for k in range(3):
                            n_rows = min(P, ED - k * P)
                            last = nc.tensor.transpose(turn_b[0:n_rows, k * P:(k + 1) * P], flat[:, k * P:k * P + n_rows], ident[:, :])
                    last.then_inc(zT_ps, 1)

                def z_copied(b, t):
                    return Z_COPIES * b + (3 * t + 2 if t < NT else Z_COPIES)

                def period(n, b, h, par, share, ahead, start, has_next, projecting, splitting, project_out, norm_last, gates_next, new_x):
                    for i in range(NT):
                        if project_out and i:
                            pe.wait_ge(zT_sb, z_copied(b - 1, i - 1))
                        if norm_last and h == 2 and i == 0:
                            pe.wait_ge(zT_sb, z_copied(b - 1, NT))
                        if gates_next and (h, i) in ((3, 5), (3, 6), (3, 7), (4, 0)):
                            prepared(b + 1, (i - 5) % 8 if h == 3 else 3)
                        if projecting:
                            project(n + 2, par, i, (0,), b + 1 if new_x else None)
                        if not start and i == 1:
                            sum_probs(n - 1, 1 - par)
                        if not start and i == 2:
                            turn_acc(n - 1)
                        if 3 <= i < 7 and has_next:
                            turn(n + 1, 1 - par, i - 3)
                        scores(n, par, i)
                        if projecting:
                            project(n + 2, par, i, (1,))
                        if not start and i == 1:
                            turn_sums(n - 1)
                        if i or not start:
                            products(*((n, par, i - 1) if i else (n - 1, 1 - par, NT - 1)))
                        if project_out or gates_next and h == 3 and i >= 4:
                            if i == 1:
                                pe.wait_ge(recip_rdy, n)
                            if i == 2:
                                pe.wait_ge(o_rdy, O0 + n)
                            if 3 <= i < 7:
                                pe.wait_ge(low_rdy, 4 * (n + 1) + i - 2)
                            if project_out:
                                project_out_piece(b - 1, i)
                            else:
                                prepare(b + 1, i - 4)
                        if projecting:
                            project(n + 2, par, i, (2,))
                    if project_out:
                        pe.wait_ge(zT_sb, z_copied(b - 1, NT - 1))
                        project_out_piece(b - 1, NT)

                pe.wait_ge(w_in, 16 * (2 + E))
                pe.wait_ge(clear, 2)
                for k in range(4):
                    prepare(0, k)
                    prepared(0, k)
                for n in range(2):
                    for t in range(NT):
                        project(n, n, t, x_of=0)
                for r in range(4):
                    turn(0, 0, r)
                run_periods(pe, period)
                last_n = B * NH - 1
                products(last_n, last_n % 2, NT - 1)
                sum_probs(last_n, last_n % 2)
                turn_sums(last_n)
                turn_acc(last_n)
                pe.wait_ge(o_rdy, O0 + B * NH)
                for t in range(NT + 1):
                    if t:
                        pe.wait_ge(zT_sb, z_copied(B - 1, t - 1))
                    project_out_piece(B - 1, t)
                if not with_max:
                    turn_counts(nc, pe, judged, good, ident, turn_b[0:1, 0:P])

        @block.vector
        def _(dve):
            with only_if(dve, redo):
                dve.sem_inc(mult, MULT0)
                dve.sem_inc(tok_rdy, TOK0)
                dve.sem_inc(o_rdy, O0)
                for half in range(2):
                    dve.sem_inc(z_rdy[half], Z0)
                dve.sem_inc(norm_steps, ONE)
                def split_x(b):
                    for r, (lo, hi) in enumerate(HALVES):
                        dve.wait_ge(x_high, 2 * b + r + 1)
                        nc.vector.tensor_tensor(xl[:, lo:hi], xT[:, lo:hi], xh[:, lo:hi].bitcast(F32), ALU.subtract).then_inc(x_low, 1)

                def gate_parts(b):
                    st = Steps(dve, steps, GATE_STEPS * b)
                    dve.wait_ge(gate_exp, 2 * b + 2)
                    gb = gate[:, bass.ds(b, 1), :, :].rearrange("p b t c -> p (b t) c")
                    st.done(nc.vector.tensor_scalar(gb, gb, 1.0, None, ALU.add))
                    st.settle_apart()
                    for t in range(0, NT, 2):
                        st.done(nc.vector.reciprocal(gb[:, t:t + 2, :], gb[:, t:t + 2, :]))
                        yield
                    st.settle()
                    g = gb.rearrange("p t (g e) -> p (t g) e", e=E)
                    for e in range(E):
                        for lo, hi, op in ((0, e, ALU.is_ge), (e + 1, E, ALU.is_gt)):
                            if lo < hi:
                                st.done(nc.vector.tensor_tensor(beats[:, :, e, lo:hi], g[:, :, lo:hi], g[:, :, e:e + 1].broadcast_to([P, NT * NG, hi - lo]), op))
                        yield
                    st.settle()
                    for c in range(0, NT * NG, NT * NG // 4):
                        some = slice(c, c + NT * NG // 4)
                        st.done(nc.vector.reduce_sum(mask[:, some, :], beats[:, some, :, :], AX.X))
                        yield
                    st.settle()
                    st.link(nc.vector.tensor_scalar(mask[:, :, :], mask[:, :, :], float(TOP), None, ALU.is_lt))
                    m = mask[:, :, :].rearrange("p (t s g) e -> p t s (g e)", t=NT, s=2)
                    st.done(nc.vector.tensor_copy(picked[:, bass.ds(b, 1), :, :].rearrange("p b t c -> p (b t) c"), m[:, :, 1, :]))
                    yield
                    gs, gd = gb[:, :, 0:NH * E], gb[:, :, NH * E:]
                    st.done(nc.vector.tensor_tensor(gs, gs, m[:, :, 0, :], ALU.mult))
                    st.done(nc.vector.scalar_tensor_tensor(gd, gd, float(DH) ** -0.5, m[:, :, 1, :], ALU.mult, ALU.mult))
                    st.settle()
                    assert st.n == GATE_STEPS, st.n

                def gate_part(n, b, h, t, j):
                    if j == 0:
                        dve.wait_ge(tok_rdy, TOK0 + NT * n + t - 1)
                    u = 3 * t + j
                    dve.wait_ge(proj_ps, U * n + u + 1)
                    at = h * E + (NH * E if j == 0 else 0)
                    g = gate[:, bass.ds(b, 1), t, at:at + E].rearrange("p b e -> p (b e)")
                    nc.vector.tensor_tensor(gated[:, t % 2, j, :].rearrange("p (e d) -> p e d", e=E), proj_b[u % 2][:, 0:ED].rearrange("p (e d) -> p e d", e=E),
                                            g.unsqueeze(2).broadcast_to([P, E, DH]), ALU.mult).then_inc(mult, 1)

                def sum_experts(n, par, t):
                    dve.wait_ge(mult, MULT0 + U * n + 3 * t + 3)
                    if t == 0:
                        dve.wait_ge(vals_rdy, VALS0 + n - 1)
                    nc.vector.tensor_reduce(tok[:, par, t, :, :], gated[:, t % 2, :, :].rearrange("p j (e d) -> p j d e", e=E), AX.X, ALU.add).then_inc(tok_rdy, 1)

                def low_part(n, par, r):
                    dve.wait_ge(high_rdy, 4 * n + r + 1)
                    lo, hi = HALVES[r % 2]
                    if r < 2:
                        nc.vector.tensor_tensor(kk[DH:P, par, lo:hi], turn_b[DH:P, :], kk[DH:P, par, lo:hi].bitcast(F32), ALU.subtract).then_inc(low_rdy, 1)
                    else:
                        nc.vector.tensor_tensor(ql[:, par, lo:hi], turn_b, qh[:, par, lo:hi].bitcast(F32), ALU.subtract).then_inc(low_rdy, 1)

                def reciprocals(n):
                    dve.wait_ge(sumT_ps, SUMT0 + n + 1)
                    nc.vector.reciprocal(recips[:, bass.ds(n * NT, NT)].rearrange("p (j m) -> p j m", j=4), turn_b[:, 0:2 * P].rearrange("p (m j c) -> p j m c", m=2, j=4)[:, :, :, 0]).then_inc(recip_rdy, 1)

                def normalize(n):
                    dve.wait_ge(accT_ps, ACCT0 + n + 1)
                    dve.wait_ge(recip_rdy, n + 1)
                    dve.wait_ge(share_rdy, SHARE0 + n)
                    nc.vector.tensor_tensor(o[:, :, :].rearrange("p (f j) d -> p f j d", f=2), turn_b.rearrange("p (j f d) -> p f j d", j=4, f=2),
                                            recips[:, bass.ds(n * NT, NT)].rearrange("p (f j) -> p f j", f=2).unsqueeze(3).broadcast_to([P, 2, 4, DH]), ALU.mult).then_inc(o_rdy, 1)

                def add_share(half, n, b, first_head):
                    dve.wait_ge(share_rdy, SHARE0 + n + 1)
                    dve.wait_ge(z_rdy[half], Z0 + n)
                    zf, sf = (a[:, half * (NT // 2):(half + 1) * (NT // 2), :, :].rearrange("p t e d -> p (t e d)") for a in (z, share))
                    if first_head:
                        dve.wait_ge(zT_ps, ZT0 + (NT + 1) * b)
                        nc.vector.tensor_copy(zf, sf).then_inc(z_rdy[half], 1)
                    else:
                        nc.vector.tensor_tensor(zf, zf, sf, ALU.add).then_inc(z_rdy[half], 1)

                def norm_parts(b):
                    dve.wait_ge(y_rdy, b + 1)
                    st = Steps(dve, norm_steps, ONE + NORM_STEPS * b)
                    yield from layer_norm_parts(nc, st, y, out[:, bass.ds(b * NT, NT), :], stats, mv, rs, tmp)
                    st.settle_apart()
                    assert st.n == NORM_STEPS

                def max_rows(n):
                    for qt in range(NT):
                        dve.wait_ge(max_ps, NT * n + qt + 1)
                        nc.vector.reduce_max(mx[:, qt:qt + 1], score_b[qt % 2], AX.X).then_inc(max_rdy, 1)
                    for half, (lo, hi) in enumerate(HALVES):
                        dve.wait_ge(neg_ps, 2 * n + half + 1)
                        nc.vector.tensor_scalar(neg_max[:, lo:hi], turn_b[0:1, :], -1.0, None, ALU.mult).then_inc(neg_rdy, 1)

                def period(n, b, h, par, share, ahead, start, has_next, projecting, splitting, project_out, norm_last, gates_next, new_x):
                    if new_x:
                        split_x(b + 1)
                    if with_max:
                        max_rows(n)

                    def between(i):
                        if not start and i == 1:
                            reciprocals(n - 1)
                        if not start and i == 2:
                            normalize(n - 1)
                        if 3 <= i < 7 and has_next:
                            low_part(n + 1, 1 - par, i - 3)

                    if gates_next and h == 4:
                        waiting["gates"] = gate_parts(b + 1)
                    if norm_last and h == 2:
                        waiting["norm"] = norm_parts(b - 1)
                    for i in range(NT):
                        if not projecting:
                            between(i)
                        if projecting:
                            for j in range(3):
                                gate_part(n + 2, b + 1 if h >= NH - 2 else b, ahead, i, j)
                                if j == (0 if i == 2 else 1):
                                    between(i)
                            sum_experts(n + 2, par, i)
                        if not start and i in (5, 7) and not project_out:
                            add_share(int(i == 7), n - 1, b, h == 1)
                        if norm_last and (i in (0, 2, 4, 6, 7) if h == 2 else i < 3):
                            next(waiting["norm"])
                        if norm_last and h == 3 and i == 2:
                            next(waiting["norm"], None)
                        if gates_next and h > 3:
                            next(waiting["gates"], None)
                    if gates_next and h == 5:
                        for _ in waiting["gates"]:
                            pass
                    if project_out:
                        for half in range(2):
                            add_share(half, n - 1, b, True)

                waiting = {}
                dve.wait_ge(clear, 2)
                for _ in gate_parts(0):
                    pass
                split_x(0)
                for n in range(2):
                    for t in range(NT):
                        for j in range(3):
                            gate_part(n, 0, n, t, j)
                        sum_experts(n, n, t)
                for r in range(4):
                    low_part(0, 0, r)
                run_periods(dve, period)
                last_n = B * NH - 1
                reciprocals(last_n)
                normalize(last_n)
                for half in range(2):
                    add_share(half, last_n, B - 1, False)
                for _ in norm_parts(B - 1):
                    pass
                if not with_max:
                    count_safe(nc, dve, judged, recips[:, :], ok, good)
                    raise_flag(nc, dve, judged, turn_b[0:1, 0:P], total, P * B * NH * NT, flag)


def rotary_attention(nc, x, out, ps, ident, I, redo, flag, tag):
    G = 4
    NG = H // G
    STEPS = G // 2 * NT
    BS = NG * STEPS
    NP = H // 2
    Z_PIECES = [(kind, half) for half in range(2) for kind in ("turn_out", "project_out")]
    X_PIECES = ([("turn_x", 0), ("turn_x", 1)] + [(kind, half) for kinds in (("q", "q_sw"), ("k", "k_sw")) for half in range(2) for kind in kinds]
                + [("v", 0), ("v", 1)])
    NZ, NX = len(Z_PIECES), len(X_PIECES)
    TURN = 4
    Z_AT, NORM_AT, X_AT = 5, 9, 14
    with_max = redo is not None
    ctx = ExitStack()
    with ctx:
        sb = lambda name, shape, dt=F32: ctx.enter_context(nc.sbuf_tensor(tag + name, shape, dt))
        sems, sem = semaphores(nc, ctx, tag)
        wq, wk, wv, wo, wq_sw, wk_sw = (sb(n, [P, D]) for n in ("wq", "wk", "wv", "wo", "wq_sw", "wk_sw"))
        rows = sb("rows", [1, 6, D])
        b_col = sb("b_col", [P, 4])
        b_all = sb("b_all", [P, 2, D])
        cos, sin = sb("cos", [P, T]), sb("sin", [P, T])
        ones = sb("ones", [1, P])
        xs, xT, xb = sb("xs", [P, NT, D]), sb("xT", [P, T]), sb("xb", [P, NT, D])
        rot, part = sb("rot", [P, HALF]), sb("part", [P, HALF])
        split = sb("split", [P, 4, T], F32R)
        keys = sb("keys", [P, 2, T], F32R)
        qpad = sb("qpad", [P, 2, G, T], F32R)
        v = sb("v", [P, B * NT, D])
        vg = sb("vg", [P, 2, NT, G, 32])
        probs = sb("probs", [P, 2, 2, T])
        acc = sb("acc", [P, 2, HALF])
        ao, aoT = sb("ao", [P, NT, D]), sb("aoT", [P, T])
        y = sb("y", [P, NT, D])
        stats, mv, rs, tmp = sb("stats", [P, NT, 6]), sb("mv", [P, NT, 2]), sb("rs", [P, NT]), sb("tmp", [P, 2, NT])
        recips, ok, good, total = sb("recips", [P, B * H * NT]), sb("ok", [P, B * H * NT]), sb("good", [P, 1]), sb("total", [1, 1])
        judged = sem("judged")
        if with_max:
            mx, neg_max = sb("mx", [P, 2, NT]), sb("neg_max", [1, 2, T])
            max_ps, max_rdy, neg_ps, neg_rdy = map(sem, ("max_ps", "max", "neg_ps", "neg"))

        w_in, swapped, clear, bias_ps, bias_sb = map(sem, ("w_in", "swapped", "clear", "bias_ps", "bias_sb"))
        x_in, filled, used, rope_steps = map(sem, ("x_in", "filled", "used", "rope_steps"))
        xb_rdy, vg_rdy, laid_out, laid_first = map(sem, ("xb_rdy", "vg_rdy", "laid_out", "laid_first"))
        staged = [sem("staged0"), sem("staged1")]
        score_ps, exp_rdy, pv_done, acc_sb, accT_ps, recip_rdy, ao_rdy, norm_steps = map(sem, ("score_ps", "exp", "pv", "acc_sb", "accT_ps", "recip_rdy", "ao_rdy", "norm_steps"))
        score_b = [ps[:, i:i + 2, :].rearrange("p a n -> p (a n)") for i in (0, 2)]
        acc_b = [ps[:, 4, :], ps[:, 5, :]]
        accT_b, piece_b = ps[:, 6, :], ps[:, 7, :]
        W_IN = 16 * 10
        SC, VC = 2 * STEPS, STEPS
        NORM_STEPS = LN_STEPS + 1
        ROPE_STEPS = 2 * 2 * 5
        DMAS = 1 + G
        heads_dram = nc.dram_tensor(tag + "heads", [B, 2, H, 4, HD, T], F32).ap()

        def z_index(b, k):
            return NX + (NZ + NX) * b + k

        def x_index(xb_no, k):
            return k if isinstance(xb_no, int) and xb_no == 0 else z_index(xb_no - 1, NZ + k)

        def bank_of(index):
            early = isinstance(index, int) and index < NX
            return (ps[:, 4 + index % 4, :] if early else piece_b), early

        def pieces(b, first, last):
            at = {}
            if not first:
                at.update({Z_AT + k: (z_index(b, k), kind, half, b - 1) for k, (kind, half) in enumerate(Z_PIECES)})
            if not last:
                at.update({X_AT + k: (x_index(b + 1, k), kind, half, b + 1) for k, (kind, half) in enumerate(X_PIECES)})
            return at

        def batches(eng, body):
            body(0, True, False)
            with eng.Fori(1, B - 1) as b:
                body(b, False, False)
            body(B - 1, False, True)

        ctx.callback(clear_semaphores, nc, sems)
        block = ctx.enter_context(nc.Block())

        @block.sync
        def _(sp):
            with only_if(sp, redo):
                sp.sem_inc(laid_out, ONE)
                sp.dma_start(xs[:, :, :], x[:, 0:NT, :]).then_inc(x_in, 16)
                for dst, src in ((wq, "L1_attn_Wq"), (wk, "L1_attn_Wk"), (wv, "L1_attn_Wv"), (wo, "L1_attn_Wo"), (cos, "cos"), (sin, "sin")):
                    sp.dma_start(dst[:, :], I[src]).then_inc(w_in, 16)
                for j, src in enumerate(("L1_attn_bq", "L1_attn_bk", "L1_attn_bv", "L1_attn_bo")):
                    sp.dma_start(rows[:, j, :], I[src].rearrange("(o n) -> o n", o=1)).then_inc(w_in, 16)

                def lay_out(b, groups, laid):
                    heads, rows = slice(groups[0] * G, groups[1] * G), slice(groups[0] * G * HD, groups[1] * G * HD)
                    for j in range(2):
                        sp.wait_ge(rope_steps, ROPE_STEPS * b + ROPE_STEPS // 2 * (j + 1))
                        for lo in range(2):
                            for c in ((2 * lo, 2 * lo + 1) if j == 0 else (lo, lo + 2)):
                                sp.dma_start(heads_dram[bass.ds(b, 1), j, heads, c, :, :].rearrange("b h d t -> (b h) d t"), split[rows, 2 * j + lo, :].bitcast(F32)).then_inc(laid, 16)

                def stage(b, g):
                    par = g % 2
                    sp.wait_ge(score_ps, ONE + SC * (b * NG + g))
                    sp.dma_start(keys[:, par, :].bitcast(F32), heads_dram[bass.ds(b, 1), 1, g * G:g * G + G, :, :, :].rearrange("b h c d t -> (b h c d) t")).then_inc(staged[par], 16)
                    for hh in range(G):
                        sp.dma_start(qpad[32 * hh:32 * hh + 32, par, hh, :].bitcast(F32), heads_dram[bass.ds(b, 1), 0, g * G + hh:g * G + hh + 1, :, :, :].rearrange("b h c d t -> (b h c d) t")).then_inc(staged[par], 16)

                lay_out(0, (0, 1), laid_first)
                sp.wait_ge(clear, 4)
                sp.wait_ge(laid_first, 16 * 8)
                stage(0, 0)
                lay_out(0, (1, NG), laid_out)

                def batch(b, first, last):
                    sp.wait_ge(laid_out, ONE + 16 * 8 * (b + 1))
                    if not first:
                        stage(b, 0)
                    stage(b, 1)
                    if not last:
                        sp.wait_ge(filled, x_index(b, 1) + 1)
                        sp.dma_start(xs[:, :, :], x[:, bass.ds((b + 1) * NT, NT), :]).then_inc(x_in, 16)
                        lay_out(b + 1, (0, NG), laid_out)
                    stage(b, 2)
                    stage(b, 3)

                batches(sp, batch)

        @block.gpsimd
        def _(pool):
            with only_if(pool, redo):
                pool.sem_inc(vg_rdy, ONE)
                nc.gpsimd.memset(ones[:, :], 1.0).then_inc(clear, 1)
                pool.wait_ge(w_in, W_IN)
                for src, dst in ((wq[:, :], wq_sw[:, :]), (wk[:, :], wk_sw[:, :]), (rows[:, 0, :], rows[:, 4, :]), (rows[:, 1, :], rows[:, 5, :])):
                    s2, d2 = src.rearrange("p (n two) -> p n two", two=2), dst.rearrange("p (n two) -> p n two", two=2)
                    nc.gpsimd.tensor_copy(d2[:, :, 0], s2[:, :, 1]).then_inc(swapped, 1)
                    nc.gpsimd.tensor_copy(d2[:, :, 1], s2[:, :, 0]).then_inc(swapped, 1)
                nc.gpsimd.memset(vg[:, :, :, :, :], 0.0).then_inc(clear, 1)
                nc.gpsimd.memset(qpad[:, :, :, :].bitcast(F32), 0.0).then_inc(clear, 1)
                pool.wait_ge(clear, 3)
                nc.gpsimd.memset(vg[:, :, :, :, HD:HD + 1], 1.0).then_inc(clear, 1)
                pool.wait_ge(bias_sb, 3)
                pool.wait_ge(clear, 4)

                def residual(b):
                    pool.wait_ge(used, z_index(b, NZ))
                    nc.gpsimd.tensor_tensor(xb[:, :, :], x[:, bass.ds(b * NT, NT), :], b_all[:, 1, :].unsqueeze(1).broadcast_to([P, NT, D]), ALU.add).then_inc(xb_rdy, 1)

                def batch(b, first, last):
                    pool.wait_ge(used, z_index(b, 0))
                    for g in range(NG):
                        pool.wait_ge(pv_done, ONE + VC * (b * NG + g))
                        for hh in range(G):
                            at = (g * G + hh) * HD
                            nc.gpsimd.tensor_copy(vg[:, g % 2, :, hh, 0:HD], v[:, bass.ds(b * NT, NT), at:at + HD]).then_inc(vg_rdy, 1)
                        if g == 2:
                            residual(b)

                batches(pool, batch)

        @block.scalar
        def _(act):
            with only_if(act, redo):
                act.sem_inc(exp_rdy, ONE)
                nc.scalar.preload_act_table(ACT.Exp)
                with act.Fori(0, B * NP) as pair:
                    for kt in range(NT):
                        step = pair * NT + kt
                        act.wait_ge(pv_done, ONE + VC - 1 + step)
                        for s in range(2):
                            act.wait_ge(score_ps, ONE + SC + 2 * step + s + 1)
                            nc.scalar.activation(probs[:, kt % 2, s, :], score_b[s], ACT.Exp, scale=float(HD) ** -0.5).then_inc(exp_rdy, 1)

        @block.tensor
        def _(pe):
            with only_if(pe, redo):
                pe.sem_inc(score_ps, ONE + SC)
                pe.sem_inc(pv_done, ONE + VC)
                pe.wait_ge(w_in, W_IN)
                pe.wait_ge(clear, 1)
                pe.wait_ge(swapped, 8)
                for j, src in enumerate((0, 1, 4, 5)):
                    last = nc.tensor.matmul(ps[:, 0, j:j + 1], rows[:, src, :], ones[0:1, 0:1], start=True, stop=True)
                last.then_inc(bias_ps, 1)
                for j in range(2):
                    nc.tensor.matmul(ps[:, 1 + j, 0:D], ones[0:1, 0:P], rows[:, 2 + j, :], start=True, stop=True).then_inc(bias_ps, 1)
                pe.wait_ge(bias_sb, 3)

                def piece(index, kind, half, b):
                    bank, early = bank_of(index)
                    if early:
                        before = max(index - 3, 0 if kind == "turn_x" else 2)
                        if before > 0:
                            pe.wait_ge(used, before)
                    else:
                        pe.wait_ge(used, index)
                    c = half * HALF
                    if kind == "turn_x" and half == 0:
                        pe.wait_ge(x_in, 16 * (b + 1))
                    if kind == "turn_out" and half == 0:
                        pe.wait_ge(ao_rdy, ONE + 2 * NP * (b + 1))
                    if kind in ("q", "q_sw", "k", "k_sw"):
                        w = {"q": wq, "q_sw": wq_sw, "k": wk, "k_sw": wk_sw}[kind]
                        last = nc.tensor.matmul(bank, w[:, :], xT[:, c:c + HALF], start=True, stop=True)
                    for j in range(4):
                        t, cols = 4 * half + j, bank[:, j * P:(j + 1) * P]
                        if kind == "turn_x":
                            last = nc.tensor.transpose(cols, xs[:, t, :], ident[:, :])
                        elif kind == "turn_out":
                            last = nc.tensor.transpose(cols, ao[:, t, :], ident[:, :])
                        elif kind == "v":
                            last = nc.tensor.matmul(cols, xT[:, t * P:(t + 1) * P], wv[:, :], start=True, stop=True)
                        elif kind == "project_out":
                            last = nc.tensor.matmul(cols, aoT[:, t * P:(t + 1) * P], wo[:, :], start=True, stop=True)
                    last.then_inc(filled, 1)

                def query_max(par, hh, s, pair_no):
                    head = 2 * pair_no + s
                    for qt in range(NT):
                        if qt >= 2:
                            pe.wait_ge(max_rdy, NT * head + qt - 1)
                        for c in range(0, T, HALF):
                            last = nc.tensor.matmul(score_b[qt % 2][:, c:c + HALF], qpad[:, par, hh, qt * P:(qt + 1) * P], keys[:, par, c:c + HALF], start=True, stop=True)
                        last.then_inc(max_ps, 1)
                    pe.wait_ge(max_rdy, NT * head + NT)
                    for half in range(2):
                        if half:
                            pe.wait_ge(neg_rdy, 2 * head + 1)
                        for j in range(NT // 2):
                            qt = half * (NT // 2) + j
                            last = nc.tensor.matmul(piece_b[0:1, j * P:(j + 1) * P], mx[:, s, qt:qt + 1], ident[:, :], start=True, stop=True)
                        last.then_inc(neg_ps, 1)
                    pe.wait_ge(neg_rdy, 2 * head + 2)

                def scores(b, i, first, pieces_before):
                    g, pp, kt = i // STEPS, i // NT % (G // 2), i % NT
                    par, step = g % 2, b * BS + i
                    if i % STEPS == 0:
                        pe.wait_ge(staged[par], 16 * DMAS * (b * (NG // 2) + g // 2 + 1))
                        pe.wait_ge(vg_rdy, ONE + G * (b * NG + g + 1))
                    if with_max and kt == 0:
                        pe.wait_ge(exp_rdy, ONE + 2 * step)
                        pe.wait_ge(used, z_index(b, 0) + pieces_before)
                        for s in range(2):
                            query_max(par, 2 * pp + s, s, b * NP + i // NT)
                    for s in range(2):
                        hh = 2 * pp + s
                        if not (first and i == 0):
                            pe.wait_ge(exp_rdy, ONE + 2 * step + s - 1)
                        for c in range(0, T, HALF):
                            last = nc.tensor.matmul(score_b[s][:, c:c + HALF], keys[:, par, kt * P:(kt + 1) * P], qpad[:, par, hh, c:c + HALF], start=True, stop=not with_max)
                            if with_max:
                                last = nc.tensor.matmul(score_b[s][:, c:c + HALF], ones[0:1, :], neg_max[:, s, c:c + HALF], start=False, stop=True)
                        last.then_inc(score_ps, 1)

                def products(b, i):
                    par, pp, kt, pair = i // STEPS % 2, i // NT % (G // 2), i % NT, i // NT
                    pe.wait_ge(exp_rdy, ONE + 2 * (b * BS + i) + 2)
                    if kt == 0:
                        pe.wait_ge(acc_sb, ONE + b * NP + max(pair - 1, 0 if isinstance(b, int) and b == 0 else -1))
                    for s in range(2):
                        for half in range(2):
                            at = 64 * s + 32 * half
                            last = nc.tensor.matmul(acc_b[pair % 2][at:at + 32, :], vg[:, par, kt, 2 * pp + s, :], probs[:, kt % 2, s, half * HALF:(half + 1) * HALF],
                                                    start=(kt == 0), stop=(kt == NT - 1))
                    last.then_inc(pv_done, 1)

                def turn(b, pair):
                    n = b * NP + pair
                    pe.wait_ge(acc_sb, ONE + n + 1)
                    pe.wait_ge(ao_rdy, ONE + 2 * n)
                    for j in range(4):
                        last = nc.tensor.transpose(accT_b[:, j * P:(j + 1) * P], acc[:, pair % 2, j * P:(j + 1) * P], ident[:, :])
                    last.then_inc(accT_ps, 1)

                for k, (kind, half) in enumerate(X_PIECES):
                    piece(k, kind, half, 0)
                pe.wait_ge(used, NX)
                pe.sem_inc(filled, NZ)

                def batch(b, first, last):
                    at = pieces(b, first, last)
                    for i in range(BS):
                        scores(b, i, first, (NZ if first else 0) + sum(j < i for j in at))
                        if i:
                            products(b, i - 1)
                        elif not first:
                            products(b - 1, BS - 1)
                        if i % NT == TURN and not (first and i == TURN):
                            turn(*((b, i // NT - 1) if i > TURN else (b - 1, NP - 1)))
                        if i in at:
                            piece(*at[i])

                batches(pe, batch)
                products(B - 1, BS - 1)
                turn(B - 1, NP - 1)
                for k, (kind, half) in enumerate(Z_PIECES):
                    piece(z_index(B, k) - NX, kind, half, B - 1)
                if not with_max:
                    turn_counts(nc, pe, judged, good, ident, accT_b[0:1, 0:P])

        @block.vector
        def _(dve):
            with only_if(dve, redo):
                dve.sem_inc(acc_sb, ONE)
                dve.sem_inc(ao_rdy, ONE)
                dve.sem_inc(norm_steps, ONE)
                dve.wait_ge(bias_ps, 3)
                nc.vector.tensor_copy(b_col[:, :], ps[:, 0, 0:4]).then_inc(bias_sb, 1)
                for j in range(2):
                    nc.vector.tensor_copy(b_all[:, j, :], ps[:, 1 + j, 0:D]).then_inc(bias_sb, 1)
                dve.wait_ge(bias_sb, 3)
                dve.wait_ge(w_in, W_IN)

                def piece(index, kind, half, b):
                    bank, _ = bank_of(index)
                    dve.wait_ge(filled, index + 1)
                    cols = slice(half * HALF, (half + 1) * HALF)
                    tiles = bank.rearrange("p (t c) -> p t c", t=4)
                    if kind == "turn_x":
                        nc.vector.tensor_copy(xT[:, cols], bank).then_inc(used, 1)
                    elif kind == "turn_out":
                        nc.vector.tensor_copy(aoT[:, cols], bank).then_inc(used, 1)
                    elif kind == "v":
                        nc.vector.tensor_tensor(v[:, bass.ds(b * NT + 4 * half, 4), :], tiles, b_all[:, 0, :].unsqueeze(1).broadcast_to([P, 4, D]), ALU.add).then_inc(used, 1)
                    elif kind == "project_out":
                        if half == 0:
                            dve.wait_ge(xb_rdy, b + 1)
                        nc.vector.tensor_tensor(y[:, 4 * half:4 * half + 4, :], tiles, xb[:, 4 * half:4 * half + 4, :], ALU.add).then_inc(used, 1)
                    elif kind in ("q", "k"):
                        j = "qk".index(kind)
                        if half == 0 and j == 0:
                            dve.wait_ge(laid_out, ONE + 16 * 8 * b)
                        nc.vector.scalar_tensor_tensor(rot[:, :], bank, b_col[:, j:j + 1], cos[:, cols], ALU.add, ALU.mult).then_inc(used, 1)
                    else:
                        j = ("q_sw", "k_sw").index(kind)
                        st = Steps(dve, rope_steps, ROPE_STEPS * b + 10 * j + 5 * half)
                        nc.vector.scalar_tensor_tensor(part[:, :], bank, b_col[:, 2 + j:3 + j], sin[:, cols], ALU.add, ALU.mult).then_inc(used, 1)
                        dve.wait_ge(used, index + 1)
                        st.link(nc.vector.tensor_tensor(rot[:, :], rot[:, :], part[:, :], ALU.add))
                        st.link(nc.vector.tensor_copy(split[:, 2 * j, cols], rot[:, :]))
                        st.link(nc.vector.tensor_tensor(split[:, 2 * j + 1, cols], rot[:, :], split[:, 2 * j, cols].bitcast(F32), ALU.subtract))
                        dve.sem_inc(rope_steps, 2)

                def norm(b):
                    dve.wait_ge(used, z_index(b + 1, NZ) if not (isinstance(b, int) and b == B - 1) else z_index(B, NZ) - NX)
                    st = Steps(dve, norm_steps, ONE + NORM_STEPS * b)
                    layer_norm(nc, st, y, out[:, bass.ds(b * NT, NT), :], stats, mv, rs, tmp)
                    st.settle_apart()
                    assert st.n == NORM_STEPS, st.n

                def row_max(s, head):
                    for qt in range(NT):
                        dve.wait_ge(max_ps, NT * head + qt + 1)
                        nc.vector.reduce_max(mx[:, s, qt:qt + 1], score_b[qt % 2], AX.X).then_inc(max_rdy, 1)
                    for half in range(2):
                        dve.wait_ge(neg_ps, 2 * head + half + 1)
                        nc.vector.tensor_scalar(neg_max[:, s, half * HALF:(half + 1) * HALF], piece_b[0:1, :], -1.0, None, ALU.mult).then_inc(neg_rdy, 1)

                def copy_acc(b, pair):
                    dve.wait_ge(pv_done, ONE + VC + NT * (b * NP + pair + 1))
                    nc.vector.tensor_copy(acc[:, pair % 2, :], acc_b[pair % 2]).then_inc(acc_sb, 1)

                def normalize(b, pair):
                    n = b * NP + pair
                    dve.wait_ge(accT_ps, n + 1)
                    t5 = accT_b.rearrange("p (j s f c) -> p s f j c", j=4, s=2, f=2)
                    recip = recips[:, bass.ds(n * 2 * NT, 2 * NT)].rearrange("p (s f j) -> p s f j", s=2, f=2)
                    nc.vector.reciprocal(recip, t5[:, :, :, :, HD]).then_inc(recip_rdy, 1)
                    dve.wait_ge(recip_rdy, n + 1)
                    for s in range(2):
                        at = pair * 2 * HD + s * HD
                        o = ao[:, :, at:at + HD].rearrange("p (f j) c -> p f j c", f=2)
                        nc.vector.tensor_tensor(o, t5[:, s, :, :, 0:HD], recip[:, s, :, :].unsqueeze(3).broadcast_to([P, 2, 4, HD]), ALU.mult).then_inc(ao_rdy, 1)

                for k, (kind, half) in enumerate(X_PIECES):
                    piece(k, kind, half, 0)
                dve.wait_ge(used, NX)
                dve.sem_inc(used, NZ)

                def batch(b, first, last):
                    at = pieces(b, first, last)
                    for i in range(BS):
                        if with_max and i % NT == 0:
                            for s in range(2):
                                row_max(s, 2 * (b * NP + i // NT) + s)
                        before = (b, i // NT - 1) if i >= NT else (b - 1, NP - 1)
                        if i % NT == 1 and not (first and i < NT):
                            copy_acc(*before)
                        if i % NT == TURN and not (first and i < NT):
                            normalize(*before)
                        if i in at:
                            piece(*at[i])
                        if i == NORM_AT and not first:
                            norm(b - 1)

                batches(dve, batch)
                copy_acc(B - 1, NP - 1)
                normalize(B - 1, NP - 1)
                for k, (kind, half) in enumerate(Z_PIECES):
                    piece(z_index(B, k) - NX, kind, half, B - 1)
                norm(B - 1)
                if not with_max:
                    count_safe(nc, dve, judged, recips[:, :], ok[:, :], good)
                    raise_flag(nc, dve, judged, accT_b[0:1, 0:P], total, P * B * H * NT, flag)



def depth_ffn(nc, x, out_dram, ps, ident, I):
    FF = 512
    NB = FF // P
    K = T // 2
    ctx = ExitStack()
    with ctx:
        sb = lambda name, shape, dt=F32: ctx.enter_context(nc.sbuf_tensor("d_" + name, shape, dt))
        sems, sem = semaphores(nc, ctx, "d_")
        w1, w2 = sb("w1", [P, FF]), sb("w2", [P, NB, D])
        b1, b2 = sb("b1", [P, NB]), sb("b2", [P, 1])
        wr, wr_rep, br = sb("wr", [P, 1]), sb("wr_rep", [P, P]), sb("br", [P, 1])
        xs, xT = sb("xs", [P, NT, D]), sb("xT", [P, T])
        w_row, w_col, ge = sb("w_row", [P, T]), sb("w_col", [P, NT]), sb("ge", [P, 2, T])
        count, sel, keep = sb("count", [P, NT]), sb("sel", [P, NT]), sb("keep", [P, NT])
        hid, blk = sb("hid", [P, NB, T]), sb("blk", [P, T])
        kept, y, yo = sb("kept", [P, NT, D]), sb("y", [P, NT, D]), sb("yo", [P, NT, D])
        stats, mv, rs, tmp = sb("stats", [P, NT, 6]), sb("mv", [P, NT, 2]), sb("rs", [P, NT]), sb("tmp", [P, 2, NT])

        w_in, wr_rdy, x_in, x_used, xT_ps, xT_sb = map(sem, ("w_in", "wr", "x_in", "x_used", "xT_ps", "xT_sb"))
        row_ps, row_sb, col_ps, col_sb = map(sem, ("row_ps", "row_sb", "col_ps", "col_sb"))
        hid_ps, hid_sb, blk_ps, blk_sb, blkT_ps = map(sem, ("hid_ps", "hid_sb", "blk_ps", "blk_sb", "blkT_ps"))
        y_rdy, out_rdy, out_done, steps = map(sem, ("y", "out", "out_done", "steps"))
        bank2 = lambda i: ps[:, i:i + 2, :].rearrange("p a n -> p (a n)")
        tr_ps, row_b, hid_b = bank2(0), bank2(2), [bank2(4), bank2(6)]
        W_IN = 16 * 6
        V_STEPS = NT + 2 + (NT - 1) + (NT - 1) + LN_STEPS

        ctx.callback(clear_semaphores, nc, sems)
        block = ctx.enter_context(nc.Block())

        @block.sync
        def _(sp):
            sp.sem_inc(out_done, ONE)
            sp.dma_start(xs[:, :, :], x[:, 0:NT, :]).then_inc(x_in, 16)
            sp.dma_start(wr[:, :], I["L1_ffn_w_r"]).then_inc(w_in, 16)
            sp.dma_start(br[:, :], I["L1_ffn_b_r"].rearrange("(o n) -> o n", o=1).broadcast_to([P, 1])).then_inc(w_in, 16)
            sp.dma_start(w1[:, :], I["L1_ffn_W1"]).then_inc(w_in, 16)
            sp.dma_start(w2[:, :, :], I["L1_ffn_W2"].rearrange("(n p) c -> p n c", p=P)).then_inc(w_in, 16)
            with nc.allow_non_contiguous_dma("two bias vectors onto partitions"):
                sp.dma_start(b1[:, :], I["L1_ffn_b1"].rearrange("(n p) -> p n", p=P)).then_inc(w_in, 16)
                sp.dma_start(b2[:, :], I["L1_ffn_b2"].rearrange("(p o) -> p o", o=1)).then_inc(w_in, 16)

            def store(b):
                sp.wait_ge(out_rdy, b + 1)
                sp.dma_start(out_dram[b].rearrange("(t p) c -> p t c", p=P), yo[:, :, :]).then_inc(out_done, 16)

            with sp.Fori(0, B - 1) as b:
                sp.wait_ge(x_used, ONE + b + 1)
                sp.wait_ge(xT_ps, ONE + b + 1)
                sp.dma_start(xs[:, :, :], x[:, bass.ds((b + 1) * NT, NT), :]).then_inc(x_in, 16)
                store(b)
            store(B - 1)
            sp.wait_ge(out_done, ONE + 16 * B)

        @block.gpsimd
        def _(pool):
            pool.wait_ge(w_in, W_IN)
            nc.gpsimd.tensor_copy(wr_rep[:, :], wr[:, 0:1].broadcast_to([P, P])).then_inc(wr_rdy, 1)

        @block.scalar
        def _(act):
            act.sem_inc(blk_sb, ONE)
            nc.scalar.preload_act_table(ACT.Gelu)
            act.wait_ge(w_in, W_IN)
            with act.Fori(0, B) as b:
                act.wait_ge(xT_ps, ONE + b + 1)
                nc.scalar.copy(xT[:, :], tr_ps).then_inc(xT_sb, 1)
                act.wait_ge(x_used, ONE + b)
                act.wait_ge(row_ps, b + 1)
                nc.scalar.activation(w_row[:, :], row_b, ACT.Identity, bias=br[:, 0:1]).then_inc(row_sb, 1)
                act.wait_ge(blk_ps, ONE + b)
                for n in range(NB):
                    act.wait_ge(hid_ps, NB * b + n + 1)
                    nc.scalar.activation(hid[:, n, :], hid_b[n % 2], ACT.Gelu, bias=b1[:, n:n + 1]).then_inc(hid_sb, 1)
                act.wait_ge(blk_ps, ONE + b + 1)
                nc.scalar.activation(blk[:, :], tr_ps, ACT.Identity, bias=b2[:, 0:1]).then_inc(blk_sb, 1)

        @block.tensor
        def _(pe):
            pe.sem_inc(blk_ps, ONE)
            pe.sem_inc(xT_ps, ONE)
            pe.wait_ge(w_in, W_IN)
            pe.wait_ge(wr_rdy, 1)
            with pe.Fori(0, B) as b:
                pe.wait_ge(x_in, 16 * b + 16)
                pe.wait_ge(blk_sb, ONE + b)
                for t in range(NT):
                    last = nc.tensor.transpose(tr_ps[:, t * P:(t + 1) * P], xs[:, t, :], ident[:, :])
                last.then_inc(xT_ps, 1)
                pe.wait_ge(xT_sb, b + 1)
                pe.wait_ge(y_rdy, ONE + b)
                for s in range(0, T, HALF):
                    last = nc.tensor.matmul(row_b[:, s:s + HALF], wr_rep[:, :], xT[:, s:s + HALF], start=True, stop=True)
                last.then_inc(row_ps, 1)
                for n in range(NB):
                    if n >= 2:
                        pe.wait_ge(hid_sb, NB * b + n - 1)
                    for s in range(0, T, HALF):
                        last = nc.tensor.matmul(hid_b[n % 2][:, s:s + HALF], w1[:, n * P:(n + 1) * P], xT[:, s:s + HALF], start=True, stop=True)
                    last.then_inc(hid_ps, 1)
                    if n == 0:
                        pe.wait_ge(row_sb, b + 1)
                        for t in range(NT):
                            last = nc.tensor.transpose(row_b[:, t * P:(t + 1) * P], w_row[:, t * P:(t + 1) * P], ident[:, :])
                        last.then_inc(col_ps, 1)
                for n in range(NB):
                    pe.wait_ge(hid_sb, NB * b + n + 1)
                    for s in range(0, T, HALF):
                        last = nc.tensor.matmul(tr_ps[:, s:s + HALF], w2[:, n, :], hid[:, n, s:s + HALF], start=(n == 0), stop=(n == NB - 1))
                last.then_inc(blk_ps, 1)
                pe.wait_ge(blk_sb, ONE + b + 1)
                pe.wait_ge(col_sb, b + 1)
                for t in range(NT):
                    last = nc.tensor.transpose(row_b[:, t * P:(t + 1) * P], blk[:, t * P:(t + 1) * P], ident[:, :])
                last.then_inc(blkT_ps, 1)

        @block.vector
        def _(dve):
            dve.sem_inc(y_rdy, ONE)
            dve.sem_inc(x_used, ONE)
            dve.wait_ge(w_in, W_IN)
            with dve.Fori(0, B) as b:
                st = Steps(dve, steps, b * V_STEPS)
                dve.wait_ge(col_ps, b + 1)
                nc.vector.tensor_copy(w_col[:, :], row_b.rearrange("p (t r) -> p t r", r=P)[:, :, 0]).then_inc(col_sb, 1)
                dve.wait_ge(col_sb, b + 1)
                for t in range(NT):
                    if t >= 2:
                        dve.wait_ge(steps, b * V_STEPS + t - 1)
                    st.done(nc.vector.tensor_scalar(ge[:, t % 2, :], w_row[:, :], w_col[:, t:t + 1], None, ALU.is_ge, ALU.add,
                                                    accum_out=count[:, t:t + 1]))
                st.settle()
                st.link(nc.vector.tensor_scalar(sel[:, :], count[:, :], float(K), None, ALU.is_lt))
                st.link(nc.vector.tensor_scalar(keep[:, :], sel[:, :], -1.0, 2.0, ALU.mult, ALU.add))
                dve.wait_ge(x_in, 16 * b + 16)
                for t in range(NT):
                    last = nc.vector.tensor_scalar(kept[:, t, :], xs[:, t, :], keep[:, t:t + 1], None, ALU.mult)
                    if t < NT - 1:
                        st.done(last)
                last.then_inc(x_used, 1)
                dve.wait_ge(x_used, ONE + b + 1)
                st.settle()
                dve.wait_ge(blkT_ps, b + 1)
                for t in range(NT):
                    last = nc.vector.scalar_tensor_tensor(y[:, t, :], row_b[:, t * P:(t + 1) * P], sel[:, t:t + 1], kept[:, t, :], ALU.mult, ALU.add)
                    if t < NT - 1:
                        st.done(last)
                last.then_inc(y_rdy, 1)
                dve.wait_ge(y_rdy, ONE + b + 1)
                st.settle()
                dve.wait_ge(out_done, ONE + 16 * b)
                layer_norm(nc, st, y, yo[:, :, :], stats, mv, rs, tmp)
                st.settle()
                nc.vector.tensor_copy(tmp[:, 0, :], mv[:, :, 1]).then_inc(out_rdy, 1)
                assert st.n == V_STEPS, st.n


def program(nc, I, out_dram):
    ctx = ExitStack()
    with ctx:
        ps = ctx.enter_context(nc.psum_tensor("banks", [P, 8, HALF], F32))
        ident = ctx.enter_context(nc.sbuf_tensor("ident", [P, P], F32))
        flag = ctx.enter_context(nc.sbuf_tensor("flag", [1, 1], I32))
        r1 = ctx.enter_context(nc.sbuf_tensor("r1", [P, B * NT, D], F32))
        r2 = ctx.enter_context(nc.sbuf_tensor("r2", [P, B * NT, D], F32))
        linear_attention(nc, I["L0_attn_x"], r1, ps, ident, I)
        for attention, x, y, tag in ((switch_attention, r1, r2, "b"), (rotary_attention, r2, r1, "c")):
            attention(nc, x, y, ps, ident, I, None, flag, tag + "_")
            attention(nc, x, y, ps, ident, I, flag, flag, tag + "_redo_")
        depth_ffn(nc, r1, out_dram, ps, ident, I)


def constants():
    import numpy as np

    ident = np.eye(P, dtype=np.float32)
    row, col = np.arange(P)[:, None], np.arange(P)[None, :]
    same_head = row // HD == col // HD
    sel = np.stack([same_head & (col % HD == m) for m in range(HD)] + [same_head], axis=1).astype(np.float32)
    inv = (1.0 / np.float32(10000.0) ** (np.arange(0, HD, 2, dtype=np.float32) / HD)).astype(np.float32)
    freqs = np.arange(T, dtype=np.float32)[:, None] * inv[None, :]
    ang = np.concatenate((freqs, freqs), axis=-1)[:, ::2].astype(np.float64)
    pair = np.arange(D) % HD // 2
    cos = np.cos(ang)[:, pair].T.astype(np.float32)
    sin = (np.sin(ang)[:, pair] * np.where(np.arange(D) % 2 == 0, -1, 1)).T.astype(np.float32)
    return {"ident": ident, "sel": sel, "cos": np.ascontiguousarray(cos), "sin": np.ascontiguousarray(sin)}


_NAMES = ("L0_attn_x", "L0_attn_Wq", "L0_attn_bq", "L0_attn_Wk", "L0_attn_bk", "L0_attn_Wv", "L0_attn_bv",
          "L0_attn_Wo", "L0_attn_bo", "L0_ffn_Wq", "L0_ffn_Wkv", "L0_ffn_Ws", "L0_ffn_Wd", "L0_ffn_Wo",
          "L1_attn_Wq", "L1_attn_bq", "L1_attn_Wk", "L1_attn_bk", "L1_attn_Wv", "L1_attn_bv",
          "L1_attn_Wo", "L1_attn_bo", "L1_ffn_w_r", "L1_ffn_b_r", "L1_ffn_W1", "L1_ffn_b1",
          "L1_ffn_W2", "L1_ffn_b2")


def kernel(**inputs):
    import numpy as _np
    import concourse.bacc as _bacc
    from concourse import mybir as _mybir
    from concourse.bass_utils import run_bass_kernel_spmd as _run

    nc = _bacc.Bacc("TRN2", target_bir_lowering=False, num_devices=1)
    arrays, aps = {}, {}
    given = {name: inputs[name] for name in _NAMES}
    given.update(constants())
    for name, value in given.items():
        a = _np.ascontiguousarray(value)
        arrays[f"in_{name}"] = a
        aps[name] = nc.dram_tensor(f"in_{name}", a.shape, _mybir.dt.from_np(a.dtype), kind="ExternalInput").ap()
    out = nc.dram_tensor("out", (B, T, D), F32, kind="ExternalOutput").ap()
    program(nc, aps, out)
    r = _run(nc, [arrays], core_ids=[0])
    return r.results[0]["out"]
```
